# Optimizing a Trainium2 kernel written in Bass

```python
import numpy as np
import jax
import jax.numpy as jnp

def _softmax(x, axis=-1):
    return jax.nn.softmax(x, axis=axis)

def _gelu(x):
    return jax.nn.gelu(x, approximate=True)

def _silu(x):
    return jax.nn.silu(x)

def _sigmoid(x):
    return jax.nn.sigmoid(x)

def _layernorm(x, axis=-1, eps=1e-05):
    m = jnp.mean(x, axis=axis, keepdims=True)
    v = jnp.var(x, axis=axis, keepdims=True)
    return (x - m) / jnp.sqrt(v + eps)

def _scatter_add(tgt, idx, src, axis=0):
    return tgt.at[idx].add(src)

def _segment_sum(src, seg, n):
    return jax.ops.segment_sum(src, seg, n)
kernel_name = 'mk_decoder_postln_d2_seqx_r4_187365'

def setup_inputs(seed: int=0):
    np.random.seed(seed)
    _w = jnp.asarray

    def _rec_inputs():
        import jax
        import jax.numpy as jnp
        _rk = jax.random.key(seed)
        x = -0.0002928 + 1 * jax.random.normal(jax.random.fold_in(_rk, 1), (2, 1024, 256), jnp.float32)
        _lenS = 1024 - jax.random.randint(jax.random.fold_in(_rk, 7), (2,), 0, max(1, 1024 // 4) + 1, jnp.int32)
        _lenS2 = 77 - jax.random.randint(jax.random.fold_in(_rk, 8), (2,), 0, max(1, 77 // 4) + 1, jnp.int32)
        _ctx_1024P = jax.random.normal(jax.random.fold_in(_rk, 11), (2, 16, 256), jnp.float32)
        _ctx_1024c = jax.random.dirichlet(jax.random.fold_in(_rk, 511), 0.3 * jnp.ones((16,), jnp.float32), (2, 77))
        _ctx_1024t = jnp.einsum('bsk,bkd->bsd', _ctx_1024c, _ctx_1024P)
        _ctx_1024t = _ctx_1024t * jax.lax.rsqrt(jnp.mean(jnp.square(_ctx_1024t)) + 1e-12) * 0.953939
        ctx_1024 = -1.39393e-06 + 0.999914 * (_ctx_1024t + 0.3 * jax.random.normal(jax.random.fold_in(_rk, 611), (2, 77, 256), jnp.float32))
        _validS = jnp.arange(1024)[None, :] < _lenS[:, None]
        _validS2 = jnp.arange(77)[None, :] < _lenS2[:, None]
        _causal = jnp.tril(jnp.ones((1024, 1024), dtype=bool))
        mask_1x1xSxS2_fk0 = jnp.where(jnp.broadcast_to(_validS2[0:1, None, None, :], (1, 1, 1024, 77)), 0.0, 1.0).astype(jnp.float32)
        return (x, ctx_1024, mask_1x1xSxS2_fk0)
    x, ctx_1024, mask_1x1xSxS2_fk0 = _rec_inputs()

    def _L0_attn_setup():
        import jax, jax.numpy as jnp
        import numpy as np
        BATCH, SEQ, HIDDEN = (8, 512, 256)
        WSIZE = 64
        NEG_INF = -1000000000.0
        key = jax.random.key(seed)
        k1, k2 = jax.random.split(key)
        repr_ = jax.random.normal(k1, (BATCH, SEQ, HIDDEN), dtype=jnp.float32)
        W = jax.random.normal(k2, (HIDDEN, HIDDEN), dtype=jnp.float32) * 0.02
        return {'repr': repr_, 'W': W}
    _L0_attn_all = _L0_attn_setup()
    _L0_attn_in = {k: v for k, v in _L0_attn_all.items() if k in ('W',)}
    del _L0_attn_all

    def _L0_xattn_setup():
        import jax, jax.numpy as jnp
        import numpy as np
        B, T, E, H = (2, 512, 256, 16)
        key = jax.random.key(seed)
        ks = jax.random.split(key, 8)
        std = 1.0 / np.sqrt(E)
        x = jax.random.normal(ks[0], (B, T, E), dtype=jnp.float32)
        y = jax.random.normal(ks[1], (B, T, E), dtype=jnp.float32)
        mask = jnp.tril(jnp.ones((T, T), dtype=jnp.float32))[None, None]
        Wq = jax.random.normal(ks[2], (E, E), dtype=jnp.float32) * std
        Wk = jax.random.normal(ks[3], (E, E), dtype=jnp.float32) * std
        Wv = jax.random.normal(ks[4], (E, E), dtype=jnp.float32) * std
        Wo = jax.random.normal(ks[5], (E, E), dtype=jnp.float32) * std
        bq = jnp.zeros((E,), jnp.float32)
        bk = jnp.zeros((E,), jnp.float32)
        bv = jnp.zeros((E,), jnp.float32)
        bo = jnp.zeros((E,), jnp.float32)
        return {'x': x, 'y': y, 'mask': mask, 'Wq': Wq, 'bq': bq, 'Wk': Wk, 'bk': bk, 'Wv': Wv, 'bv': bv, 'Wo': Wo, 'bo': bo, 'num_heads': H}
    _L0_xattn_all = _L0_xattn_setup()
    _L0_xattn_in = {k: v for k, v in _L0_xattn_all.items() if k in ('Wq', 'bq', 'Wk', 'bk', 'Wv', 'bv', 'Wo', 'bo')}
    del _L0_xattn_all

    def _L0_ffn_setup():
        import jax, jax.numpy as jnp
        import numpy as np
        B, S, D, E, H, K = (4, 512, 256, 8, 1024, 2)
        EPS = 1e-06

        def _ln(x, scale, bias):
            m = jnp.mean(x, axis=-1, keepdims=True)
            v = jnp.mean(jnp.square(x - m), axis=-1, keepdims=True)
            return (x - m) * jax.lax.rsqrt(v + EPS) * scale + bias
        key = jax.random.key(seed)
        ks = jax.random.split(key, 4)
        s1 = 1.0 / np.sqrt(D)
        s2 = 1.0 / np.sqrt(H)
        return {'x': jax.random.normal(ks[0], (B, S, D), jnp.float32), 'router_ln_scale': jnp.ones((D,), jnp.float32), 'router_ln_bias': jnp.zeros((D,), jnp.float32), 'router_w': jax.random.normal(ks[1], (E, D), jnp.float32) * s1, 'router_b': jnp.zeros((E,), jnp.float32), 'expert_ln_scale': jnp.ones((E, D), jnp.float32), 'expert_ln_bias': jnp.zeros((E, D), jnp.float32), 'w1': jax.random.normal(ks[2], (E, H, D), jnp.float32) * s1, 'b1': jnp.zeros((E, H), jnp.float32), 'w2': jax.random.normal(ks[3], (E, D, H), jnp.float32) * s2, 'b2': jnp.zeros((E, D), jnp.float32)}
    _L0_ffn_all = _L0_ffn_setup()
    _L0_ffn_in = {k: v for k, v in _L0_ffn_all.items() if k in ('router_ln_scale', 'router_ln_bias', 'router_w', 'router_b', 'expert_ln_scale', 'expert_ln_bias', 'w1', 'b1', 'w2', 'b2')}
    del _L0_ffn_all

    def _L1_attn_setup():
        import jax, jax.numpy as jnp
        import numpy as np
        EMB = 256
        HEADS = 16
        EPS = 1e-05

        def layer_norm(x):
            mu = jnp.mean(x, axis=-1, keepdims=True)
            var = jnp.var(x, axis=-1, keepdims=True)
            return (x - mu) / jnp.sqrt(var + EPS)

        def pattention(x, K, V):
            scale = EMB ** (-0.5)
            a = jax.nn.softmax(scale * jnp.einsum('btc,nc->btn', x, K), axis=-1)
            return jnp.einsum('btn,nc->btc', a, V)

        def causal_sdpa(q, k, v):
            T = q.shape[2]
            d = q.shape[-1]
            scores = jnp.einsum('bhqd,bhkd->bhqk', q, k) / jnp.sqrt(jnp.asarray(d, q.dtype))
            mask = jnp.tril(jnp.ones((T, T), dtype=bool))
            scores = jnp.where(mask, scores, jnp.asarray(-jnp.inf, q.dtype))
            attn = jax.nn.softmax(scores, axis=-1)
            return jnp.einsum('bhqk,bhkd->bhqd', attn, v)
        key = jax.random.key(seed)
        ks = jax.random.split(key, 11)
        B, T, C = (2, 512, EMB)
        N = 512 // 2
        inp = {'x': jax.random.normal(ks[0], (B, T, C), dtype=jnp.float32)}
        names = ['qK', 'qV', 'kK', 'kV', 'vK', 'vV', 'pK', 'pV']
        for i, nm in enumerate(names):
            inp[nm] = jax.random.normal(ks[1 + i], (N, C), dtype=jnp.float32)
        inp['fK'] = jax.random.normal(ks[9], (4 * N, C), dtype=jnp.float32)
        inp['fV'] = jax.random.normal(ks[10], (4 * N, C), dtype=jnp.float32)
        return inp
    _L1_attn_all = _L1_attn_setup()
    _L1_attn_in = {k: v for k, v in _L1_attn_all.items() if k in ('qK', 'qV', 'kK', 'kV', 'vK', 'vV', 'pK', 'pV', 'fK', 'fV')}
    del _L1_attn_all

    def _L1_xattn_setup():
        import jax, jax.numpy as jnp
        import numpy as np
        B, L, D_MODEL, H = (4, 512, 256, 16)
        E = D_MODEL // H
        EPS = 1e-05

        def layernorm(x, w, b):
            mu = jnp.mean(x, axis=-1, keepdims=True)
            var = jnp.mean((x - mu) ** 2, axis=-1, keepdims=True)
            return (x - mu) * jax.lax.rsqrt(var + EPS) * w + b
        key = jax.random.key(seed)
        ks = jax.random.split(key, 12)
        s_in = 1.0 / np.sqrt(D_MODEL)
        inp = {'q': jax.random.normal(ks[0], (B, L, D_MODEL), jnp.float32), 'k': jax.random.normal(ks[1], (B, L, D_MODEL), jnp.float32), 'v': jax.random.normal(ks[2], (B, L, D_MODEL), jnp.float32), 'norm_w': jnp.ones((D_MODEL,), jnp.float32), 'norm_b': jnp.zeros((D_MODEL,), jnp.float32), 'norm1_w': jnp.ones((D_MODEL,), jnp.float32), 'norm1_b': jnp.zeros((D_MODEL,), jnp.float32), 'Wq': jax.random.uniform(ks[3], (D_MODEL, H * E), jnp.float32, -s_in, s_in), 'bq': jnp.zeros((H * E,), jnp.float32), 'Wk': jax.random.uniform(ks[4], (D_MODEL, H * E), jnp.float32, -s_in, s_in), 'bk': jnp.zeros((H * E,), jnp.float32), 'Wv': jax.random.uniform(ks[5], (D_MODEL, H * E), jnp.float32, -s_in, s_in), 'bv': jnp.zeros((H * E,), jnp.float32), 'Wo': jax.random.uniform(ks[6], (H * E, D_MODEL), jnp.float32, -s_in, s_in), 'bo': jnp.zeros((D_MODEL,), jnp.float32)}
        return inp
    _L1_xattn_all = _L1_xattn_setup()
    _L1_xattn_in = {k: v for k, v in _L1_xattn_all.items() if k in ('norm_w', 'norm_b', 'norm1_w', 'norm1_b', 'Wq', 'bq', 'Wk', 'bk', 'Wv', 'bv', 'Wo', 'bo')}
    del _L1_xattn_all

    def _L1_ffn_setup():
        import jax, jax.numpy as jnp
        import numpy as np
        B, S, H = (2, 512, 256)
        E_ROUTED = 8
        TOP_K = 2
        I = 512
        key = jax.random.key(seed)
        ks = jax.random.split(key, 9)
        s = 0.02
        return {'x': jax.random.normal(ks[0], (B, S, H), dtype=jnp.float32), 'shared_gate': jax.random.normal(ks[1], (I, H), dtype=jnp.float32) * s, 'shared_up': jax.random.normal(ks[2], (I, H), dtype=jnp.float32) * s, 'shared_down': jax.random.normal(ks[3], (H, I), dtype=jnp.float32) * s, 'gate_w': jax.random.normal(ks[4], (E_ROUTED, H, I), dtype=jnp.float32) * s, 'up_w': jax.random.normal(ks[5], (E_ROUTED, H, I), dtype=jnp.float32) * s, 'down_w': jax.random.normal(ks[6], (E_ROUTED, I, H), dtype=jnp.float32) * s, 'router_w': jax.random.normal(ks[7], (E_ROUTED, H), dtype=jnp.float32) * s, 'routing_bias': jnp.zeros((E_ROUTED,), dtype=jnp.float32)}
    _L1_ffn_all = _L1_ffn_setup()
    _L1_ffn_in = {k: v for k, v in _L1_ffn_all.items() if k in ('shared_gate', 'shared_up', 'shared_down', 'gate_w', 'up_w', 'down_w', 'router_w', 'routing_bias')}
    del _L1_ffn_all
    return {'x': x, 'ctx_1024': ctx_1024, 'mask_1x1xSxS2_fk0': mask_1x1xSxS2_fk0, 'L0_attn_W': _L0_attn_in['W'], 'L0_xattn_Wq': _L0_xattn_in['Wq'], 'L0_xattn_bq': _L0_xattn_in['bq'], 'L0_xattn_Wk': _L0_xattn_in['Wk'], 'L0_xattn_bk': _L0_xattn_in['bk'], 'L0_xattn_Wv': _L0_xattn_in['Wv'], 'L0_xattn_bv': _L0_xattn_in['bv'], 'L0_xattn_Wo': _L0_xattn_in['Wo'], 'L0_xattn_bo': _L0_xattn_in['bo'], 'L0_ffn_router_ln_scale': _L0_ffn_in['router_ln_scale'], 'L0_ffn_router_ln_bias': _L0_ffn_in['router_ln_bias'], 'L0_ffn_router_w': _L0_ffn_in['router_w'], 'L0_ffn_router_b': _L0_ffn_in['router_b'], 'L0_ffn_expert_ln_scale': _L0_ffn_in['expert_ln_scale'], 'L0_ffn_expert_ln_bias': _L0_ffn_in['expert_ln_bias'], 'L0_ffn_w1': _L0_ffn_in['w1'], 'L0_ffn_b1': _L0_ffn_in['b1'], 'L0_ffn_w2': _L0_ffn_in['w2'], 'L0_ffn_b2': _L0_ffn_in['b2'], 'L1_attn_qK': _L1_attn_in['qK'], 'L1_attn_qV': _L1_attn_in['qV'], 'L1_attn_kK': _L1_attn_in['kK'], 'L1_attn_kV': _L1_attn_in['kV'], 'L1_attn_vK': _L1_attn_in['vK'], 'L1_attn_vV': _L1_attn_in['vV'], 'L1_attn_pK': _L1_attn_in['pK'], 'L1_attn_pV': _L1_attn_in['pV'], 'L1_attn_fK': _L1_attn_in['fK'], 'L1_attn_fV': _L1_attn_in['fV'], 'L1_xattn_norm_w': _L1_xattn_in['norm_w'], 'L1_xattn_norm_b': _L1_xattn_in['norm_b'], 'L1_xattn_norm1_w': _L1_xattn_in['norm1_w'], 'L1_xattn_norm1_b': _L1_xattn_in['norm1_b'], 'L1_xattn_Wq': _L1_xattn_in['Wq'], 'L1_xattn_bq': _L1_xattn_in['bq'], 'L1_xattn_Wk': _L1_xattn_in['Wk'], 'L1_xattn_bk': _L1_xattn_in['bk'], 'L1_xattn_Wv': _L1_xattn_in['Wv'], 'L1_xattn_bv': _L1_xattn_in['bv'], 'L1_xattn_Wo': _L1_xattn_in['Wo'], 'L1_xattn_bo': _L1_xattn_in['bo'], 'L1_ffn_shared_gate': _L1_ffn_in['shared_gate'], 'L1_ffn_shared_up': _L1_ffn_in['shared_up'], 'L1_ffn_shared_down': _L1_ffn_in['shared_down'], 'L1_ffn_gate_w': _L1_ffn_in['gate_w'], 'L1_ffn_up_w': _L1_ffn_in['up_w'], 'L1_ffn_down_w': _L1_ffn_in['down_w'], 'L1_ffn_router_w': _L1_ffn_in['router_w'], 'L1_ffn_routing_bias': _L1_ffn_in['routing_bias']}

def reference(x, ctx_1024, mask_1x1xSxS2_fk0, L0_attn_W, L0_xattn_Wq, L0_xattn_bq, L0_xattn_Wk, L0_xattn_bk, L0_xattn_Wv, L0_xattn_bv, L0_xattn_Wo, L0_xattn_bo, L0_ffn_router_ln_scale, L0_ffn_router_ln_bias, L0_ffn_router_w, L0_ffn_router_b, L0_ffn_expert_ln_scale, L0_ffn_expert_ln_bias, L0_ffn_w1, L0_ffn_b1, L0_ffn_w2, L0_ffn_b2, L1_attn_qK, L1_attn_qV, L1_attn_kK, L1_attn_kV, L1_attn_vK, L1_attn_vV, L1_attn_pK, L1_attn_pV, L1_attn_fK, L1_attn_fV, L1_xattn_norm_w, L1_xattn_norm_b, L1_xattn_norm1_w, L1_xattn_norm1_b, L1_xattn_Wq, L1_xattn_bq, L1_xattn_Wk, L1_xattn_bk, L1_xattn_Wv, L1_xattn_bv, L1_xattn_Wo, L1_xattn_bo, L1_ffn_shared_gate, L1_ffn_shared_up, L1_ffn_shared_down, L1_ffn_gate_w, L1_ffn_up_w, L1_ffn_down_w, L1_ffn_router_w, L1_ffn_routing_bias):
    import jax
    import jax.numpy as jnp

    def _L0_attn_ref(repr, W):
        import jax, jax.numpy as jnp
        import numpy as np
        BATCH, SEQ, HIDDEN = (8, 512, 256)
        WSIZE = 64
        NEG_INF = -1000000000.0
        b, s, d = repr.shape
        idx = jnp.arange(s)
        mask = jnp.abs(idx[:, None] - idx[None, :]) > WSIZE
        scores = jnp.einsum('bqd,de,bke->bqk', repr, W, repr)
        scores = jnp.where(mask[None, :, :], NEG_INF, scores)
        probs = jax.nn.softmax(scores, axis=-1)
        ra = jnp.einsum('bqk,bkd->bqd', probs, repr)
        return repr + jax.nn.relu(ra)

    def _L0_xattn_ref(x, y, mask, Wq, bq, Wk, bk, Wv, bv, Wo, bo, num_heads):
        import jax, jax.numpy as jnp
        import numpy as np
        B, T, E, H = (2, 512, 256, 16)
        Bx, Tq, Emb = x.shape
        Tkv = y.shape[1]
        d = Emb // num_heads
        q = (x @ Wq + bq).reshape(Bx, Tq, num_heads, d)
        k = (y @ Wk + bk).reshape(Bx, Tkv, num_heads, d)
        v = (y @ Wv + bv).reshape(Bx, Tkv, num_heads, d)
        scale = 1.0 / np.sqrt(d).astype(np.float32)
        att = scale * jnp.einsum('bthd,bThd->bhtT', q, k)
        att = att * mask - 10000000000.0 * (1.0 - mask)
        att = jax.nn.softmax(att, axis=-1)
        out = jnp.einsum('bhtT,bThd->bthd', att, v).reshape(Bx, Tq, Emb)
        return out @ Wo + bo

    def _L0_ffn_ref(x, router_ln_scale, router_ln_bias, router_w, router_b, expert_ln_scale, expert_ln_bias, w1, b1, w2, b2):
        import jax, jax.numpy as jnp
        import numpy as np
        B, S, D, E, H, K = (4, 512, 256, 8, 1024, 2)
        EPS = 1e-06

        def _ln(x, scale, bias):
            m = jnp.mean(x, axis=-1, keepdims=True)
            v = jnp.mean(jnp.square(x - m), axis=-1, keepdims=True)
            return (x - m) * jax.lax.rsqrt(v + EPS) * scale + bias
        orig_shape = x.shape
        xf = x.reshape(-1, D)
        T = xf.shape[0]
        logits = _ln(xf, router_ln_scale, router_ln_bias) @ router_w.T + router_b
        probs = jax.nn.softmax(logits, axis=-1)
        topw, topi = jax.lax.top_k(probs, K)
        topw = topw / jnp.sum(topw, axis=-1, keepdims=True)
        gates = jnp.zeros((T, E), xf.dtype).at[jnp.arange(T)[:, None], topi].set(topw)

        def expert(ls, lb, W1, B1, W2, B2):
            h = jax.nn.gelu(_ln(xf, ls, lb) @ W1.T + B1, approximate=False)
            return h @ W2.T + B2
        ys = jax.vmap(expert)(expert_ln_scale, expert_ln_bias, w1, b1, w2, b2)
        out = jnp.einsum('te,etd->td', gates, ys)
        return out.reshape(orig_shape)

    def _L1_attn_ref(x, qK, qV, kK, kV, vK, vV, pK, pV, fK, fV):
        import jax, jax.numpy as jnp
        import numpy as np
        EMB = 256
        HEADS = 16
        EPS = 1e-05

        def layer_norm(x):
            mu = jnp.mean(x, axis=-1, keepdims=True)
            var = jnp.var(x, axis=-1, keepdims=True)
            return (x - mu) / jnp.sqrt(var + EPS)

        def pattention(x, K, V):
            scale = EMB ** (-0.5)
            a = jax.nn.softmax(scale * jnp.einsum('btc,nc->btn', x, K), axis=-1)
            return jnp.einsum('btn,nc->btc', a, V)

        def causal_sdpa(q, k, v):
            T = q.shape[2]
            d = q.shape[-1]
            scores = jnp.einsum('bhqd,bhkd->bhqk', q, k) / jnp.sqrt(jnp.asarray(d, q.dtype))
            mask = jnp.tril(jnp.ones((T, T), dtype=bool))
            scores = jnp.where(mask, scores, jnp.asarray(-jnp.inf, q.dtype))
            attn = jax.nn.softmax(scores, axis=-1)
            return jnp.einsum('bhqk,bhkd->bhqd', attn, v)
        B, T, C = x.shape
        H = HEADS
        D = C // H
        x_in = x
        h = layer_norm(x)
        k = pattention(h, kK, kV)
        q = pattention(h, qK, qV)
        v = pattention(h, vK, vV)
        to_heads = lambda t: t.reshape(B, T, H, D).transpose(0, 2, 1, 3)
        o = causal_sdpa(to_heads(q), to_heads(k), to_heads(v))
        o = o.transpose(0, 2, 1, 3).reshape(B, T, C)
        o = pattention(o, pK, pV)
        x = o + x_in
        x_inter = x
        x = pattention(layer_norm(x), fK, fV)
        return x + x_inter

    def _L1_xattn_ref(q, k, v, norm_w, norm_b, norm1_w, norm1_b, Wq, bq, Wk, bk, Wv, bv, Wo, bo):
        import jax, jax.numpy as jnp
        import numpy as np
        B, L, D_MODEL, H = (4, 512, 256, 16)
        E = D_MODEL // H
        EPS = 1e-05

        def layernorm(x, w, b):
            mu = jnp.mean(x, axis=-1, keepdims=True)
            var = jnp.mean((x - mu) ** 2, axis=-1, keepdims=True)
            return (x - mu) * jax.lax.rsqrt(var + EPS) * w + b
        b, l, _ = q.shape
        s = k.shape[1]
        qn = layernorm(q, norm_w, norm_b)
        kn = layernorm(k, norm_w, norm_b)
        vn = layernorm(v, norm_w, norm_b)
        Q = (qn @ Wq + bq).reshape(b, l, H, E)
        K = (kn @ Wk + bk).reshape(b, s, H, E)
        V = (vn @ Wv + bv).reshape(b, s, H, E)
        scale = 1.0 / jnp.sqrt(jnp.asarray(E, Q.dtype))
        scores = jnp.einsum('blhe,bshe->bhls', Q, K)
        A = jax.nn.softmax(scale * scores, axis=-1)
        O = jnp.einsum('bhls,bshd->blhd', A, V)
        O = O + Q
        out = jnp.transpose(O, (0, 2, 1, 3)).reshape(b, l, H * E)
        return layernorm(out, norm1_w, norm1_b) @ Wo + bo + out

    def _L1_ffn_ref(x, shared_gate, shared_up, shared_down, gate_w, up_w, down_w, router_w, routing_bias):
        import jax, jax.numpy as jnp
        import numpy as np
        B, S, H = (2, 512, 256)
        E_ROUTED = 8
        TOP_K = 2
        I = 512
        b, s, h = x.shape
        shared = jnp.einsum('bsi,hi->bsh', jax.nn.silu(jnp.einsum('bsh,ih->bsi', x, shared_gate)) * jnp.einsum('bsh,ih->bsi', x, shared_up), shared_down)
        logits = jnp.einsum('bsh,eh->bse', x, router_w) + routing_bias
        probs = jax.nn.sigmoid(logits)
        scores, indices = jax.lax.top_k(probs, TOP_K)
        scores = scores / jnp.sum(scores, axis=-1, keepdims=True)
        t = b * s
        xf = x.reshape(t, h)
        idx = indices.reshape(t, TOP_K)
        sc = scores.reshape(t, TOP_K)
        w = jnp.zeros((t, E_ROUTED), dtype=x.dtype)
        w = w.at[jnp.arange(t)[:, None], idx].add(sc)
        g = jax.nn.silu(jnp.einsum('th,ehi->tei', xf, gate_w))
        u = jnp.einsum('th,ehi->tei', xf, up_w)
        combined = jnp.einsum('tei,eih,te->th', g * u, down_w, w)
        return shared + combined.reshape(b, s, h)
    x = _layernorm(x + _L0_attn_ref(x, L0_attn_W), axis=-1)
    x = _layernorm(x + _L0_xattn_ref(x, ctx_1024, mask_1x1xSxS2_fk0, L0_xattn_Wq, L0_xattn_bq, L0_xattn_Wk, L0_xattn_bk, L0_xattn_Wv, L0_xattn_bv, L0_xattn_Wo, L0_xattn_bo, 16), axis=-1)
    x = _layernorm(x + _L0_ffn_ref(x, L0_ffn_router_ln_scale, L0_ffn_router_ln_bias, L0_ffn_router_w, L0_ffn_router_b, L0_ffn_expert_ln_scale, L0_ffn_expert_ln_bias, L0_ffn_w1, L0_ffn_b1, L0_ffn_w2, L0_ffn_b2), axis=-1)
    x = _layernorm(x + _L1_attn_ref(x, L1_attn_qK, L1_attn_qV, L1_attn_kK, L1_attn_kV, L1_attn_vK, L1_attn_vV, L1_attn_pK, L1_attn_pV, L1_attn_fK, L1_attn_fV), axis=-1)
    x = _layernorm(x + _L1_xattn_ref(x, ctx_1024, ctx_1024, L1_xattn_norm_w, L1_xattn_norm_b, L1_xattn_norm1_w, L1_xattn_norm1_b, L1_xattn_Wq, L1_xattn_bq, L1_xattn_Wk, L1_xattn_bk, L1_xattn_Wv, L1_xattn_bv, L1_xattn_Wo, L1_xattn_bo), axis=-1)
    x = _layernorm(x + _L1_ffn_ref(x, L1_ffn_shared_gate, L1_ffn_shared_up, L1_ffn_shared_down, L1_ffn_gate_w, L1_ffn_up_w, L1_ffn_down_w, L1_ffn_router_w, L1_ffn_routing_bias), axis=-1)
    return x

_drawn_inputs = setup_inputs


def setup_inputs(seed=0):
    import zlib

    import numpy as np

    out = dict(_drawn_inputs(seed))
    spreads = {'L0_xattn_bq': (0.0, 0.1),
     'L0_xattn_bk': (0.0, 2.0),
     'L0_xattn_bv': (0.0, 0.1),
     'L0_xattn_bo': (0.0, 0.1),
     'L0_ffn_router_ln_scale': (1.0, 0.2),
     'L0_ffn_router_ln_bias': (0.0, 0.1),
     'L0_ffn_router_b': (0.0, 0.1),
     'L0_ffn_expert_ln_scale': (1.0, 0.2),
     'L0_ffn_expert_ln_bias': (0.0, 0.1),
     'L0_ffn_b1': (0.0, 0.1),
     'L0_ffn_b2': (0.0, 0.1),
     'L1_xattn_norm_w': (1.0, 0.2),
     'L1_xattn_norm_b': (0.0, 0.1),
     'L1_xattn_norm1_w': (1.0, 0.2),
     'L1_xattn_norm1_b': (0.0, 0.1),
     'L1_xattn_bq': (0.0, 0.1),
     'L1_xattn_bk': (0.0, 2.0),
     'L1_xattn_bv': (0.0, 0.1),
     'L1_xattn_bo': (0.0, 0.1),
     'L1_ffn_routing_bias': (0.0, 0.8)}
    factors = {'L1_attn_qK': 8.0,
     'L1_attn_qV': 8.0,
     'L1_attn_kK': 8.0,
     'L1_attn_kV': 8.0,
     'L1_attn_vK': 8.0,
     'L1_attn_vV': 8.0,
     'L1_attn_pK': 8.0,
     'L1_attn_fK': 3.019,
     'L1_ffn_gate_w': 3.399,
     'L1_ffn_up_w': 3.354,
     'L1_ffn_down_w': 3.359,
     'L1_ffn_router_w': 3.888,
     'L1_ffn_shared_gate': 2.97,
     'L1_ffn_shared_up': 2.875,
     'L1_ffn_shared_down': 2.886}
    for name, (base, spread) in spreads.items():
        noise = np.random.default_rng([zlib.crc32(name.encode()), seed]).standard_normal(out[name].shape)
        drawn = base * np.exp(spread * noise) if base else spread * noise
        out[name] = jnp.asarray(drawn.astype(out[name].dtype))
    for name, factor in factors.items():
        out[name] = (out[name] * factor).astype(out[name].dtype)
    return out
```

```python
import concourse.bass as bass
import numpy as np
from concourse import mybir
from contextlib import ExitStack

F32 = mybir.dt.float32
BF16 = mybir.dt.bfloat16
I32 = mybir.dt.int32
U32 = mybir.dt.uint32
ACT = mybir.ActivationFunctionType
ALU = mybir.AluOpType
AX = mybir.AxisListType

P = 128
B, S, D = 2, 1024, 256
T = B * S // P
TB = S // P
DC = D // P
G = 4
GT = G * P
NG = T // G
GB = TB // G
H, DH = 16, 16
HB = P // DH
S2 = 77
WIN = 64
NEG = -1.0e9


class Signal:

    def __init__(self, cx, nc, name, per=1, sem=None):
        self.sem = sem if sem is not None else cx.enter_context(nc.semaphore(name))
        if sem is None:
            cx.callback(nc.sync.sem_clear, self.sem)
        self.per = per

    def at(self, i, n):
        return i * self.per + n


def tiles(nc, cx):
    def sb(name, shape, dt=F32):
        return cx.enter_context(nc.sbuf_tensor(name, shape, dt))
    return sb


def ln_stats(dve, stats, mv, sem_var, src, n, eps):
    for j in range(n):
        dve.bn_stats(stats[:, j, :], src[:, j, :])
    dve.drain()
    for j in range(n):
        dve.bn_aggr(mv[:, j, :], stats[:, j, :])
    dve.drain()
    dve.tensor_scalar(mv[:, 0:n, 1], mv[:, 0:n, 1], eps, None, ALU.add).then_inc(sem_var, 1)


def window_attention(nc, X, ident, ps, a, spare, x_loaded, prefetch):
    KW = 2 * P
    PADDED = S + 2 * WIN
    with ExitStack() as cx:
        sb = tiles(nc, cx)
        xT = sb("a_xT", [P, DC, B * PADDED])
        xs = spare[:, 0:B * (TB + 1) * D].rearrange("p (b t d) -> p b t d", b=B, t=TB + 1)
        w = sb("a_w", [P, DC, D])
        band = sb("a_band", [P, KW])
        pad = sb("a_pad", [1, B * PADDED])
        ones = sb("a_ones", [1, P])
        xwT = sb("a_xwT", [P, DC, GT])
        probs = sb("a_probs", [P, 2, KW])
        probsT = sb("a_probsT", [P, 2, 2, P])
        nmax = sb("a_nmax", [P, G])
        total = sb("a_total", [P, G])
        inv = sb("a_inv", [P, G])
        ra = sb("a_ra", [P, G, D])
        y = sb("a_y", [P, G, D])
        stats = sb("a_stats", [P, G, 6])
        mv = sb("a_mv", [P, G, 2])
        rstd = sb("a_rstd", [P, G])
        half = sb("a_half", [P, G])

        def sig(name, per=1):
            return Signal(cx, nc, "a_" + name, per)
        loaded, masks, zeroed = sig("loaded"), sig("masks"), sig("zeroed")
        xw_done, xw_out = sig("xw_done"), sig("xw_out")
        scored, maxed, exped = sig("scored", G), sig("maxed", G), sig("exped", G)
        turned, turned_out = sig("turned", G), sig("turned_out", G)
        mixed, relued, inved = sig("mixed", G), sig("relued", G), sig("inved", G)
        var, rs = sig("var"), sig("rs")
        block = cx.enter_context(nc.Block())

        @block.sync
        def _(sp):
            sp.wait_ge(zeroed.sem, 2)
            for b in range(B):
                sp.dma_start(xT[:, :, b * PADDED + WIN:b * PADDED + WIN + S],
                             a["xT"][:, b * S:(b + 1) * S].rearrange("(k p) t -> p k t", p=P)).then_inc(loaded.sem, 16)
            sp.dma_start(w[:, :, :], a["L0_attn_W"].rearrange("(k p) n -> p k n", p=P)).then_inc(loaded.sem, 16)
            for b in range(B):
                sp.dma_start(xs[WIN:P, b, 0:TB, :], a["x"][b, :, :].rearrange("(t p) d -> p t d", p=P)[0:WIN]).then_inc(loaded.sem, 16)
                sp.dma_start(xs[0:WIN, b, 1:TB + 1, :], a["x"][b, :, :].rearrange("(t p) d -> p t d", p=P)[WIN:P]).then_inc(loaded.sem, 16)
            prefetch(sp)

        @block.gpsimd
        def _(pool):
            pool.memset(xT[:, :, :], 0.0).then_inc(zeroed.sem, 1)
            pool.drain()
            for b in range(B):
                pool.memset(xs[0:WIN, b, 0, :], 0.0)
                pool.drain()
                pool.memset(xs[WIN:P, b, TB, :], 0.0)
                pool.drain()
            pool.memset(half[:, :], -0.5).then_inc(zeroed.sem, 1)
            pool.drain()
            pool.memset(pad[:, :], NEG)
            pool.drain()
            pool.memset(band[:, :], 0.0)
            pool.drain()
            pool.memset(ones[:, :], 1.0)
            for b in range(B):
                pool.drain()
                pool.memset(pad[:, b * PADDED + WIN:b * PADDED + WIN + S], 0.0)
            pool.drain()
            pool.affine_select(out=band[:, :], in_=band[:, :], compare_op=ALU.is_ge, fill=NEG,
                               base=0, pattern=[[1, KW]], channel_multiplier=-1)
            pool.drain()
            pool.affine_select(out=band[:, :], in_=band[:, :], compare_op=ALU.is_ge, fill=NEG,
                               base=2 * WIN, pattern=[[-1, KW]], channel_multiplier=1).then_inc(masks.sem, 1)
            with pool.Fori(0, NG) as i:
                pool.wait_ge(var.sem, var.at(i, 1))
                pool.tensor_tensor(rstd[:, :], mv[:, :, 1], half[:, :], ALU.pow).then_inc(rs.sem, 1)

        @block.tensor
        def _(pe):
            pe.wait_ge(loaded.sem, 16 * (3 + 2 * B))
            pe.wait_ge(masks.sem, 1)

            def project(i, at):
                for n in range(DC):
                    for k in range(DC):
                        last = nc.tensor.matmul(ps[:, n, :], w[:, k, n * P:(n + 1) * P], xT[:, k, bass.ds(at + WIN, GT)],
                                                start=(k == 0), stop=(k == DC - 1))
                last.then_inc(xw_done.sem, 1)

            def score(i, at, j):
                if j >= 2:
                    pe.wait_ge(exped.sem, exped.at(i, j - 1))
                out = ps[:, 2 + j % 2, 0:KW]
                for k in range(DC):
                    nc.tensor.matmul(out, xwT[:, k, j * P:(j + 1) * P], xT[:, k, bass.ds(at + j * P, KW)],
                                     start=(k == 0), stop=False)
                nc.tensor.matmul(out, ident[:, :], band[:, :], start=False, stop=False)
                nc.tensor.matmul(out, ones[:, :], pad[:, bass.ds(at + j * P, KW)],
                                 start=False, stop=True).then_inc(scored.sem, 1)

            def turn(i, j):
                pe.wait_ge(exped.sem, exped.at(i, j + 1))
                if j >= 2:
                    pe.wait_ge(turned_out.sem, turned_out.at(i, j - 1))
                for c in range(2):
                    last = nc.tensor.transpose(ps[:, 4 + j % 2, c * P:(c + 1) * P], probs[:, j % 2, c * P:(c + 1) * P], ident[:, :])
                last.then_inc(turned.sem, 1)

            def mix(i, b, h, j):
                pe.wait_ge(turned_out.sem, turned_out.at(i, j + 1))
                if j >= 2:
                    pe.wait_ge(relued.sem, relued.at(i, j - 1))
                for c in range(2):
                    row = (b * (TB + 1) + h * G + (j + c)) * D
                    last = nc.tensor.matmul(ps[:, 6 + j % 2, 0:D], probsT[:, j % 2, c, :],
                                            spare[:, bass.ds(row, D)],
                                            start=(c == 0), stop=(c == 1))
                last.then_inc(mixed.sem, 1)

            with pe.Fori(0, B) as b:
                with pe.Fori(0, GB) as h:
                    i = b * GB + h
                    at = b * PADDED + h * GT
                    pe.wait_ge(relued.sem, relued.at(i, 0))
                    project(i, at)
                    pe.wait_ge(xw_out.sem, xw_out.at(i, 1))
                    for step in range(G + 2):
                        if step < G:
                            score(i, at, step)
                        if 0 <= step - 1 < G:
                            turn(i, step - 1)
                        if 0 <= step - 2 < G:
                            mix(i, b, h, step - 2)

        @block.scalar
        def _(act):
            with act.Fori(0, NG) as i:
                act.wait_ge(xw_done.sem, xw_done.at(i, 1))
                nc.scalar.activation(xwT[:, :, :], ps[:, 0:DC, :], ACT.Copy).then_inc(xw_out.sem, 1)
                for step in range(G + 2):
                    j = step
                    if j < G:
                        act.wait_ge(maxed.sem, maxed.at(i, j + 1))
                        if j >= 2:
                            act.wait_ge(turned.sem, turned.at(i, j - 1))
                        nc.scalar.activation(probs[:, j % 2, :], ps[:, 2 + j % 2, 0:KW], ACT.Exp, bias=nmax[:, j:j + 1],
                                             accum_out=total[:, j:j + 1]).then_inc(exped.sem, 1)
                    j = step - 2
                    if 0 <= j < G:
                        act.wait_ge(mixed.sem, mixed.at(i, j + 1))
                        act.wait_ge(inved.sem, inved.at(i, j + 1))
                        if j == 0:
                            act.wait_ge(rs.sem, rs.at(i, 0))
                        nc.scalar.activation(ra[:, j, :], ps[:, 6 + j % 2, 0:D], ACT.Relu,
                                             scale=inv[:, j:j + 1]).then_inc(relued.sem, 1)

        @block.vector
        def _(dve):
            dve.wait_ge(x_loaded, 16)
            with dve.Fori(0, NG) as i:
                for step in range(G + 1):
                    j = step
                    if j < G:
                        dve.wait_ge(scored.sem, scored.at(i, j + 1))
                        nc.vector.tensor_reduce(nmax[:, j:j + 1], ps[:, 2 + j % 2, 0:KW], AX.X, ALU.max,
                                                negate=True).then_inc(maxed.sem, 1)
                    j = step - 1
                    if 0 <= j < G:
                        dve.wait_ge(turned.sem, turned.at(i, j + 1))
                        if j >= 2:
                            dve.wait_ge(mixed.sem, mixed.at(i, j - 1))
                        nc.vector.tensor_copy(probsT[:, j % 2, :, :].rearrange("p c q -> p (c q)"),
                                              ps[:, 4 + j % 2, 0:KW]).then_inc(turned_out.sem, 1)
                        nc.vector.reciprocal(inv[:, j:j + 1], total[:, j:j + 1]).then_inc(inved.sem, 1)
                dve.wait_ge(relued.sem, relued.at(i, G))
                nc.vector.scalar_tensor_tensor(out=y[:, :, :].rearrange("p g d -> p (g d)"),
                                               in0=X[:, :, :].rearrange("p t d -> p (t d)")[:, bass.ds(i * (G * D), G * D)], scalar=2.0,
                                               in1=ra[:, :, :].rearrange("p g d -> p (g d)"), op0=ALU.mult, op1=ALU.add)
                dve.drain()
                ln_stats(nc.vector, stats, mv, var.sem, y, G, 1e-5)
                dve.wait_ge(rs.sem, rs.at(i, 1))
                for j in range(G):
                    nc.vector.tensor_scalar(X[:, bass.ds(i * G + j, 1), :].rearrange("p a d -> p (a d)"), y[:, j, :],
                                            mv[:, j, 0:1], rstd[:, j:j + 1], ALU.subtract, ALU.mult)
                dve.drain()


def cross_attention(nc, X, ident, ps, a, spare, layer):
    first = layer == 0
    HS = H * S2
    BH = 4
    NB = H // BH
    with ExitStack() as cx:
        tag = f"x{layer}_"
        sb = tiles(nc, cx)
        names = ["Wq", "Wk", "Wv", "Wo"]
        wt = {n: sb(tag + n, [P, DC, D]) for n in names}
        bqk = sb(tag + "bqk", [P, 2, DC])
        rows = sb(tag + "rows", [1, 2, D])
        norms = sb(tag + "norms", [P, 4, DC])
        ones = sb(tag + "ones", [1, P])
        own = sb(tag + "own", [P, HB])
        half = sb(tag + "half", [P, G])
        if first:
            mask = sb(tag + "mask", [P, TB, S2])
            less = sb(tag + "less", [P, TB, S2])
        ctx = sb(tag + "ctx", [S2, D])
        ctxT = sb(tag + "ctxT", [P, DC, S2])
        kT = sb(tag + "kT", [P, DC, S2])
        keys = sb(tag + "keys", [P, DC, HB, S2])
        vals = sb(tag + "vals", [S2, H, P])
        xn = sb(tag + "xn", [P, G, D])
        xg = xn if first else sb(tag + "xg", [P, G, D])
        xT = sb(tag + "xT", [P, DC, GT])
        qT = sb(tag + "qT", [P, DC, GT])
        att = sb(tag + "att", [P, 2, H, S2])
        top = sb(tag + "top", [P, 2, H])
        total = sb(tag + "total", [P, 2, H])
        pT = spare[0:S2, 0:H * GT].rearrange("s (h q) -> s h q", h=H)
        oT = xT
        o = None if first else sb(tag + "o", [P, TB, D])
        y = sb(tag + "y", [P, G, D]) if first else xg
        stats = sb(tag + "stats", [P, G, 6])
        mv = sb(tag + "mv", [P, G, 2])
        rstd = sb(tag + "rstd", [P, G])
        cstats, cmv, crstd = stats[0:S2, 0:1, :], mv[0:S2, 0:1, :], rstd[0:S2, 0:1]

        def sig(name, per=1):
            return Signal(cx, nc, tag + name, per)
        loaded, masks = sig("loaded"), sig("masks")
        ctx_in, kv_mm, kv_out = sig("ctx_in", 16), sig("kv_mm", 3 if first else 3), sig("kv_out", 3)
        NLN = 1 if first else 2
        var, rs = sig("var", NLN), sig("rs", NLN)
        qvar, qrs = sig("qvar"), sig("qrs")
        cvar, crs, cready = sig("cvar"), sig("crs"), sig("cready")
        x_ready, x_turned, x_out = sig("x_ready"), sig("x_turned"), sig("x_out")
        q_done, q_out = sig("q_done"), sig("q_out")
        scored, scored_out, topped, exped, summed, normed = (sig(n, G) for n in ("scored", "scored_out", "topped", "exped", "summed", "normed"))
        lowered = sig("lowered", G)
        masked = sig("masked", G)
        turned, turned_out = sig("turned", G), sig("turned_out", 2 * G)
        mixed, mixed_out = sig("mixed"), sig("mixed_out")
        o_turned, o_out, n_ready, n_turned, n_out = (sig(n) for n in ("o_turned", "o_out", "n_ready", "n_turned", "n_out"))
        wo_done = sig("wo_done")
        y_read = sig("y_read")
        block = cx.enter_context(nc.Block())

        def halves(eng, b, attend, finish):
            if first:
                with eng.Fori(0, GB) as h:
                    attend(b * GB + h, h)
                    finish(b * GB + h, h)
            else:
                for h in range(GB):
                    attend(b * GB + h, h)
                for h in range(GB):
                    finish(b * GB + h, h)
        L = "L0_xattn_" if first else "L1_xattn_"
        NLOAD = 4 + 2 + 2 + (1 if first else 4)

        @block.sync
        def _(sp):
            for n in names:
                sp.dma_start(wt[n][:, :, :], a[L + n].rearrange("(k p) n -> p k n", p=P)).then_inc(loaded.sem, 16)
            for n, name in enumerate(("bq", "bk")):
                sp.dma_start(bqk[:, n, :], a[L + name]).then_inc(loaded.sem, 16)
            for n, name in enumerate(("bv", "bo")):
                sp.dma_start(rows[:, n, :], a[L + name].rearrange("(a n) -> a n", a=1)).then_inc(loaded.sem, 16)
            if first:
                sp.dma_start(mask[:, :, :], a["mask_1x1xSxS2_fk0"].rearrange("a c (t p) s -> p (a c t) s", p=P)).then_inc(loaded.sem, 16)
            else:
                for n, name in enumerate(("norm_w", "norm_b", "norm1_w", "norm1_b")):
                    sp.dma_start(norms[:, n, :], a[L + name]).then_inc(loaded.sem, 16)
            with sp.Fori(0, B) as b:
                sp.wait_ge(kv_mm.sem, kv_mm.at(b, 0))
                sp.dma_start(ctx[:, :], a["ctx_1024"].rearrange("b s d -> (b s) d")[bass.ds(b * S2, S2), :]).then_inc(ctx_in.sem, 16)

        @block.gpsimd
        def _(pool):
            pool.memset(half[:, :], -0.5)
            pool.drain()
            pool.memset(ones[:, :], 1.0)
            pool.drain()
            pool.memset(own[:, :], 1.0)
            pool.drain()
            pool.affine_select(out=own[:, :], in_=own[:, :], compare_op=ALU.is_ge, fill=0.0,
                               base=0, pattern=[[-DH, HB]], channel_multiplier=1)
            pool.drain()
            pool.affine_select(out=own[:, :], in_=own[:, :], compare_op=ALU.is_ge, fill=0.0,
                               base=DH - 1, pattern=[[DH, HB]], channel_multiplier=-1)
            pool.drain()
            if not first:
                pool.memset(mv[:, :, :], 1.0)
                pool.drain()
            pool.memset(vals[:, :, :], 0.0).then_inc(masks.sem, 1)
            with pool.Fori(0, B) as b:
                if not first:
                    pool.wait_ge(cvar.sem, cvar.at(b, 1))
                    pool.tensor_tensor(crstd[:, :], cmv[:, :, 1], half[0:S2, 0:1], ALU.pow).then_inc(crs.sem, 1)
                def power(var, rs, i, n):
                    pool.wait_ge(var.sem, var.at(i, n + 1))
                    pool.tensor_tensor(rstd[:, :], mv[:, :, 1], half[:, :], ALU.pow).then_inc(rs.sem, 1)

                def attend(i, h):
                    if not first:
                        power(qvar, qrs, i, 0)
                    for step in range(G + 1):
                        j = step
                        if j < G:
                            m = j % 2
                            if first:
                                pool.wait_ge(scored_out.sem, scored_out.at(i, j + 1))
                                pool.tensor_tensor(att[:, m], att[:, m], less[:, bass.ds(h * G + j, 1), :].broadcast_to((P, H, S2)), ALU.add).then_inc(masked.sem, 1)
                            pool.wait_ge(topped.sem, topped.at(i, j + 1))
                            pool.tensor_tensor(att[:, m], att[:, m], top[:, m, :].unsqueeze(2).broadcast_to((P, H, S2)), ALU.subtract).then_inc(lowered.sem, 1)
                        j = step - 1
                        if 0 <= j < G:
                            m = j % 2
                            pool.wait_ge(summed.sem, summed.at(i, j + 1))
                            pool.tensor_tensor(att[:, m], att[:, m], total[:, m, :].unsqueeze(2).broadcast_to((P, H, S2)), ALU.mult).then_inc(normed.sem, 1)

                def finish(i, h):
                    for n in range(NLN):
                        power(var, rs, i, n)
                halves(pool, b, attend, finish)

        @block.tensor
        def _(pe):
            pe.wait_ge(loaded.sem, 16 * NLOAD)
            pe.wait_ge(masks.sem, 1)
            with pe.Fori(0, B) as b:
                pe.wait_ge(ctx_in.sem, ctx_in.at(b, 16))
                if not first:
                    pe.wait_ge(crs.sem, crs.at(b, 1))
                    pe.wait_ge(cready.sem, cready.at(b, 1))
                pe.wait_ge(y_read.sem, y_read.at(b * GB, 0))
                for k in range(DC):
                    last = nc.tensor.transpose(ps[:, k, 0:S2], ctx[:, k * P:(k + 1) * P], ident[0:S2, 0:S2])
                last.then_inc(kv_mm.sem, 1)
                pe.wait_ge(kv_out.sem, kv_out.at(b, 1))
                for n in range(DC):
                    for k in range(DC):
                        last = nc.tensor.matmul(ps[:, 2 + n, 0:S2], wt["Wk"][:, k, n * P:(n + 1) * P], ctxT[:, k, :],
                                                start=(k == 0), stop=(k == DC - 1))
                last.then_inc(kv_mm.sem, 1)
                for k in range(DC):
                    nc.tensor.matmul(ps[0:S2, 4, 0:D], ctxT[:, k, :], wt["Wv"][:, k, :], start=(k == 0), stop=False)
                nc.tensor.matmul(ps[0:S2, 4, 0:D], ones[:, 0:S2], rows[:, 0, :], start=False, stop=True).then_inc(kv_mm.sem, 1)

                def attend(i, h):
                    pe.wait_ge(kv_out.sem, kv_out.at(b, 3))
                    pe.wait_ge(x_ready.sem, x_ready.at(i, 1))
                    for j in range(G):
                        for k in range(DC):
                            last = nc.tensor.transpose(ps[:, k, j * P:(j + 1) * P], xn[:, j, k * P:(k + 1) * P], ident[:, :])
                    last.then_inc(x_turned.sem, 1)
                    pe.wait_ge(x_out.sem, x_out.at(i, 1))
                    for n in range(DC):
                        for k in range(DC):
                            last = nc.tensor.matmul(ps[:, 2 + n, :], wt["Wq"][:, k, n * P:(n + 1) * P], xT[:, k, :],
                                                    start=(k == 0), stop=(k == DC - 1))
                    last.then_inc(q_done.sem, 1)
                    pe.wait_ge(q_out.sem, q_out.at(i, 1))
                    for step in range(G + 1):
                        j = step
                        if j < G:
                            if j >= 1:
                                pe.wait_ge(scored_out.sem, scored_out.at(i, j))
                            for n in range(NB):
                                c, r = n * BH // HB, n * BH % HB
                                last = nc.tensor.matmul(ps[:, NB + n, 0:BH * S2], qT[:, c, j * P:(j + 1) * P],
                                                        keys[:, c, r:r + BH, :].rearrange("p h s -> p (h s)"), start=True, stop=True)
                            last.then_inc(scored.sem, 1)
                        j = step - 1
                        if 0 <= j < G:
                            pe.wait_ge(normed.sem, normed.at(i, j + 1))
                            if j >= 1:
                                pe.wait_ge(turned_out.sem, turned_out.at(i, 2 * j))
                            for n in range(H):
                                last = nc.tensor.transpose(ps[0:S2, n // 4, (n % 4) * P:(n % 4 + 1) * P], att[:, j % 2, n, :], ident[:, :])
                            last.then_inc(turned.sem, 1)
                    pe.wait_ge(turned_out.sem, turned_out.at(i, 2 * G))
                    for c in range(DC):
                        for n in range(HB):
                            last = nc.tensor.matmul(ps[:, c, :], vals[:, c * HB + n, :], pT[:, c * HB + n, :],
                                                    start=(n == 0), stop=(n == HB - 1))
                    last.then_inc(mixed.sem, 1)
                    pe.wait_ge(mixed_out.sem, mixed_out.at(i, 1))
                    if not first:
                        for j in range(G):
                            for k in range(DC):
                                last = nc.tensor.transpose(ps[:, 2 + j // 2, (j % 2) * D + k * P:(j % 2) * D + (k + 1) * P], oT[:, k, j * P:(j + 1) * P], ident[:, :])
                        last.then_inc(o_turned.sem, 1)

                def finish(i, h):
                    into = oT if first else xT
                    if not first:
                        pe.wait_ge(n_ready.sem, n_ready.at(i, 1))
                        for j in range(G):
                            for k in range(DC):
                                last = nc.tensor.transpose(ps[:, k, j * P:(j + 1) * P], xn[:, j, k * P:(k + 1) * P], ident[:, :])
                        last.then_inc(n_turned.sem, 1)
                        pe.wait_ge(n_out.sem, n_out.at(i, 1))
                    for j in range(G):
                        out = ps[:, 2 + j // 2, (j % 2) * D:(j % 2 + 1) * D]
                        for k in range(DC):
                            nc.tensor.matmul(out, into[:, k, j * P:(j + 1) * P], wt["Wo"][:, k, :], start=(k == 0), stop=False)
                        last = nc.tensor.matmul(out, ones[:, :], rows[:, 1, :], start=False, stop=True)
                    last.then_inc(wo_done.sem, 1)
                halves(pe, b, attend, finish)

        @block.scalar
        def _(act):
            act.wait_ge(loaded.sem, 16 * NLOAD)
            with act.Fori(0, B) as b:
                def attend(i, h):
                    for step in range(G + 1):
                        j = step
                        if j < G:
                            act.wait_ge(lowered.sem, lowered.at(i, j + 1))
                            nc.scalar.activation(att[:, j % 2].rearrange("p h s -> p (h s)"), att[:, j % 2].rearrange("p h s -> p (h s)"), ACT.Exp,
                                                 scale=1.0 if first else 0.25).then_inc(exped.sem, 1)
                        j = step - 1
                        if 0 <= j < G:
                            act.wait_ge(turned.sem, turned.at(i, j + 1))
                            for n in range(4):
                                last = nc.scalar.activation(pT[:, 4 * n:4 * n + 4, j * P:(j + 1) * P],
                                                            ps[0:S2, n, :].rearrange("s (h q) -> s h q", h=4), ACT.Copy)
                                if n % 2:
                                    last.then_inc(turned_out.sem, 1)
                halves(act, b, attend, lambda i, h: None)

        @block.vector
        def _(dve):
            dve.wait_ge(loaded.sem, 16 * NLOAD)
            dve.wait_ge(masks.sem, 1)
            flat = X[:, :, :].rearrange("p t d -> p (t d)")
            if first:
                nc.vector.tensor_scalar(less[:, :, :], mask[:, :, :], -1.0, 1.0e10, ALU.add, ALU.mult)
                dve.drain()
            with dve.Fori(0, B) as b:
                if not first:
                    dve.wait_ge(ctx_in.sem, ctx_in.at(b, 16))
                    ln_stats(nc.vector, cstats, cmv, cvar.sem, ctx[:, :].unsqueeze(1), 1, 1e-5)
                    dve.wait_ge(crs.sem, crs.at(b, 1))
                    nc.vector.tensor_scalar(ctx[:, :], ctx[:, :], cmv[:, 0, 0:1], crstd[:, 0:1], ALU.subtract, ALU.mult).then_inc(cready.sem, 1)
                dve.wait_ge(kv_mm.sem, kv_mm.at(b, 1))
                for k in range(DC):
                    if first:
                        last = nc.vector.tensor_copy(ctxT[:, k, :], ps[:, k, 0:S2])
                    else:
                        last = nc.vector.tensor_scalar(ctxT[:, k, :], ps[:, k, 0:S2], norms[:, 0, k:k + 1], norms[:, 1, k:k + 1], ALU.mult, ALU.add)
                last.then_inc(kv_out.sem, 1)
                dve.wait_ge(kv_mm.sem, kv_mm.at(b, 2))
                for k in range(DC):
                    nc.vector.tensor_scalar(kT[:, k, :], ps[:, 2 + k, 0:S2], bqk[:, 1, k:k + 1], None, ALU.add)
                dve.drain()
                for n in range(HB):
                    last = nc.vector.tensor_scalar(keys[:, :, n, :], kT[:, :, :], own[:, n:n + 1], None, ALU.mult)
                last.then_inc(kv_out.sem, 1)
                dve.wait_ge(kv_mm.sem, kv_mm.at(b, 3))
                for c in range(DC):
                    for n in range(HB):
                        last = nc.vector.tensor_copy(vals[:, c * HB + n, n * DH:(n + 1) * DH], ps[0:S2, 4, c * P + n * DH:c * P + (n + 1) * DH])
                last.then_inc(kv_out.sem, 1)
                def norm(var, rs, i, n, src, dst):
                    ln_stats(nc.vector, stats, mv, var.sem, src, G, 1e-5)
                    dve.wait_ge(rs.sem, rs.at(i, n + 1))
                    for j in range(G):
                        nc.vector.tensor_scalar(dst(j), src[:, j, :], mv[:, j, 0:1], rstd[:, j:j + 1], ALU.subtract, ALU.mult)
                    dve.drain()

                def attend(i, h):
                    nc.vector.tensor_copy(xg[:, :, :].rearrange("p g d -> p (g d)"), flat[:, bass.ds(i * (G * D), G * D)])
                    dve.drain()
                    if not first:
                        norm(qvar, qrs, i, 0, xg, lambda j: xn[:, j, :])
                    nc.vector.engine_nop().then_inc(x_ready.sem, 1)
                    dve.wait_ge(x_turned.sem, x_turned.at(i, 1))
                    for k in range(DC):
                        if first:
                            last = nc.vector.tensor_copy(xT[:, k, :], ps[:, k, :])
                        else:
                            last = nc.vector.tensor_scalar(xT[:, k, :], ps[:, k, :], norms[:, 0, k:k + 1], norms[:, 1, k:k + 1], ALU.mult, ALU.add)
                    last.then_inc(x_out.sem, 1)
                    dve.wait_ge(q_done.sem, q_done.at(i, 1))
                    for k in range(DC):
                        if first:
                            last = nc.vector.tensor_scalar(qT[:, k, :], ps[:, 2 + k, :], bqk[:, 0, k:k + 1], DH ** -0.5, ALU.add, ALU.mult)
                        else:
                            last = nc.vector.tensor_scalar(qT[:, k, :].rearrange("p (u m) -> p u m", u=DH), ps[:, 2 + k, :].rearrange("p (m u) -> p u m", u=DH),
                                                           bqk[:, 0, k:k + 1], None, ALU.add)
                    last.then_inc(q_out.sem, 1)
                    for step in range(G + 1):
                        j = step
                        if j < G:
                            m = j % 2
                            dve.wait_ge(scored.sem, scored.at(i, j + 1))
                            if j >= 2:
                                dve.wait_ge(turned.sem, turned.at(i, j - 1))
                            att4 = att[:, m].rearrange("p (n h) s -> p n (h s)", n=NB)
                            if first:
                                for n in range(NB):
                                    last = nc.vector.tensor_tensor(att[:, m, n * BH:(n + 1) * BH, :], ps[:, NB + n, 0:BH * S2].rearrange("p (h s) -> p h s", h=BH),
                                                        mask[:, bass.ds(h * G + j, 1), :].broadcast_to((P, BH, S2)), ALU.mult)
                                last.then_inc(scored_out.sem, 1)
                                dve.wait_ge(masked.sem, masked.at(i, j + 1))
                            else:
                                nc.vector.tensor_copy(att4, ps[:, NB:2 * NB, 0:BH * S2]).then_inc(scored_out.sem, 1)
                                dve.drain()
                            nc.vector.tensor_reduce(top[:, m, :], att[:, m], AX.X, ALU.max).then_inc(topped.sem, 1)
                        j = step - 1
                        if 0 <= j < G:
                            m = j % 2
                            dve.wait_ge(exped.sem, exped.at(i, j + 1))
                            nc.vector.tensor_reduce(total[:, m, :], att[:, m], AX.X, ALU.add)
                            dve.drain()
                            nc.vector.reciprocal(total[:, m, :], total[:, m, :]).then_inc(summed.sem, 1)
                    dve.wait_ge(mixed.sem, mixed.at(i, 1))
                    for k in range(DC):
                        if first:
                            last = nc.vector.tensor_copy(oT[:, k, :], ps[:, k, :])
                        else:
                            last = nc.vector.tensor_tensor(oT[:, k, :], ps[:, k, :], qT[:, k, :], ALU.add)
                    last.then_inc(mixed_out.sem, 1)
                    if not first:
                        dve.wait_ge(o_turned.sem, o_turned.at(i, 1))
                        M = P // 4
                        for uu in range(4):
                            for e in range(2):
                                at = (P // 2) * e + M * h
                                last = nc.vector.tensor_copy(o[at:at + M, :, :].rearrange("p c (j u d) -> p u c j d", u=4, d=DH)[:, uu],
                                                             ps[uu * M:(uu + 1) * M, 2:4, :].rearrange("p a (b c e d) -> p e c (a b) d", b=2, e=2, d=DH)[:, e])
                        last.then_inc(o_out.sem, 1)
                        dve.drain()

                def finish(i, h):
                    if first:
                        dve.wait_ge(wo_done.sem, wo_done.at(i, 1))
                        nc.vector.tensor_tensor(y[:, :, :].rearrange("p (a g) d -> p a (g d)", a=2), ps[:, 2:4, :],
                                                xg[:, :, :].rearrange("p (a g) d -> p a (g d)", a=2), ALU.add).then_inc(y_read.sem, 1)
                    else:
                        og = o[:, h * G:(h + 1) * G, :]
                        norm(var, rs, i, 0, og, lambda j: xn[:, j, :])
                        nc.vector.engine_nop().then_inc(n_ready.sem, 1)
                        nc.vector.tensor_tensor(y[:, :, :].rearrange("p g d -> p (g d)"), og.rearrange("p g d -> p (g d)"), flat[:, bass.ds(i * (G * D), G * D)], ALU.add)
                        dve.wait_ge(n_turned.sem, n_turned.at(i, 1))
                        for k in range(DC):
                            last = nc.vector.tensor_scalar(xT[:, k, :], ps[:, k, :], norms[:, 2, k:k + 1], norms[:, 3, k:k + 1], ALU.mult, ALU.add)
                        last.then_inc(n_out.sem, 1)
                        dve.wait_ge(wo_done.sem, wo_done.at(i, 1))
                        nc.vector.tensor_tensor(y[:, :, :].rearrange("p (a g) d -> p a (g d)", a=2), ps[:, 2:4, :],
                                                y[:, :, :].rearrange("p (a g) d -> p a (g d)", a=2), ALU.add).then_inc(y_read.sem, 1)
                    dve.drain()
                    norm(var, rs, i, NLN - 1, y, lambda j: X[:, bass.ds(i * G + j, 1), :].rearrange("p a d -> p (a d)"))
                halves(dve, b, attend, finish)


def slot_projections(nc, X, ident, ps, a, scratch, v_all):
    N = D
    SETS = ("q", "k", "v")
    with ExitStack() as cx:
        sb = tiles(nc, cx)
        kT = sb("d_kT", [P, 3, DC, N])
        vals = sb("d_vals", [P, 3, N // P, D])
        half = sb("d_half", [P, G])
        xg = sb("d_xg", [P, G, D])
        hT = sb("d_hT", [P, DC, GT])
        probs = sb("d_probs", [P, 2, N])
        aT = sb("d_aT", [P, 2, N // P, GT])
        part = {n: sb("d_part_" + n, [P, 3, DC, GT], BF16) for n in ("q", "k")}
        left = sb("d_left", [P, DC, GT])
        nmax = sb("d_nmax", [P, 2])
        total = sb("d_total", [P, 2])
        inv = sb("d_inv", [P, 2])
        stats, mv, rstd = sb("d_stats", [P, G, 6]), sb("d_mv", [P, G, 2]), sb("d_rstd", [P, G])
        NS = 3 * G

        def sig(name, per=1):
            return Signal(cx, nc, "d_" + name, per)
        loaded, consts, var, rs = sig("loaded"), sig("consts"), sig("var"), sig("rs")
        h_ready, h_turned, h_out = sig("h_ready"), sig("h_turned"), sig("h_out")
        scored, maxed, exped, normed = sig("scored", NS), sig("maxed", NS), sig("exped", NS), sig("normed", NS)
        turned, turned_out = sig("turned", NS), sig("turned_out", NS)
        slotted, hi_out, left_out, mid_out, lo_out = sig("slotted", 3), sig("hi_out", 2), sig("left_out", 2), sig("mid_out", 2), sig("lo_out", 2)
        v_out = sig("v_out")
        stored = {n: sig("stored_" + n, 16) for n in ("q", "k")}
        block = cx.enter_context(nc.Block())

        @block.sync
        def _(sp):
            for n, name in enumerate(SETS):
                sp.dma_start(kT[:, n, :, :], a[f"L1_attn_{name}K"].rearrange("(k p) n -> p k n", p=P)).then_inc(loaded.sem, 16)
                sp.dma_start(vals[:, n, :, :], a[f"L1_attn_{name}V"].rearrange("(k p) n -> p k n", p=P)).then_inc(loaded.sem, 16)
            with sp.Fori(0, NG) as i:
                for n, name in enumerate(("q", "k")):
                    sp.wait_ge(lo_out.sem, lo_out.at(i, n + 1))
                    rows = scratch[name].rearrange("s c p t -> p (s c) t")
                    sp.dma_start(rows[:, :, bass.ds(i * GT, GT)], part[name][:, :, :, :].rearrange("p s c t -> p (s c) t")).then_inc(stored[name].sem, 16)
            for name in ("q", "k"):
                sp.wait_ge(stored[name].sem, 16 * NG)

        @block.gpsimd
        def _(pool):
            pool.memset(half[:, :], -0.5)
            pool.drain()
            with pool.Fori(0, NG) as i:
                pool.wait_ge(var.sem, var.at(i, 1))
                pool.tensor_tensor(rstd[:, :], mv[:, :, 1], half[:, :], ALU.pow).then_inc(rs.sem, 1)

        @block.tensor
        def _(pe):
            pe.wait_ge(loaded.sem, 16 * 6)
            with pe.Fori(0, NG) as i:
                pe.wait_ge(h_ready.sem, h_ready.at(i, 1))
                for j in range(G):
                    for k in range(DC):
                        last = nc.tensor.transpose(ps[:, k, j * P:(j + 1) * P], xg[:, j, k * P:(k + 1) * P], ident[:, :])
                last.then_inc(h_turned.sem, 1)
                pe.wait_ge(h_out.sem, h_out.at(i, 1))
                for step in range(NS + 2):
                    n = step
                    if n < NS:
                        s, j = divmod(n, G)
                        if n >= 2:
                            pe.wait_ge(exped.sem, exped.at(i, n - 1))
                        for k in range(DC):
                            last = nc.tensor.matmul(ps[:, 2 + n % 2, 0:N], hT[:, k, j * P:(j + 1) * P], kT[:, s, k, :],
                                                    start=(k == 0), stop=(k == DC - 1))
                        last.then_inc(scored.sem, 1)
                    n = step - 1
                    if 0 <= n < NS:
                        pe.wait_ge(normed.sem, normed.at(i, n + 1))
                        if n >= 2:
                            pe.wait_ge(turned_out.sem, turned_out.at(i, n - 1))
                        for c in range(N // P):
                            last = nc.tensor.transpose(ps[:, 4 + n % 2, c * P:(c + 1) * P], probs[:, n % 2, c * P:(c + 1) * P], ident[:, :])
                        last.then_inc(turned.sem, 1)
                    n = step - 2
                    if n >= 0 and n % G == G - 1:
                        s = n // G
                        pe.wait_ge(turned_out.sem, turned_out.at(i, n + 1))
                        if s:
                            pe.wait_ge(left_out.sem, left_out.at(i, s))
                        else:
                            pe.wait_ge(v_out.sem, v_out.at(i, 0))
                        if s < 2:
                            for n in range(DC):
                                for k in range(N // P):
                                    last = nc.tensor.matmul(ps[:, 6 + n, :], vals[:, s, k, n * P:(n + 1) * P], aT[:, s % 2, k, :],
                                                            start=(k == 0), stop=(k == N // P - 1))
                        else:
                            for j in range(G):
                                for k in range(N // P):
                                    last = nc.tensor.matmul(ps[:, 6 + j // 2, (j % 2) * D:(j % 2 + 1) * D], aT[:, s % 2, k, j * P:(j + 1) * P], vals[:, s, k, :],
                                                            start=(k == 0), stop=(k == N // P - 1))
                        last.then_inc(slotted.sem, 1)

        @block.scalar
        def _(act):
            with act.Fori(0, NG) as i:
                for step in range(NS + 3):
                    n = step
                    if n < NS:
                        act.wait_ge(maxed.sem, maxed.at(i, n + 1))
                        if n >= 2:
                            act.wait_ge(turned.sem, turned.at(i, n - 1))
                        nc.scalar.activation(probs[:, n % 2, :], ps[:, 2 + n % 2, 0:N], ACT.Exp, bias=nmax[:, n % 2:n % 2 + 1],
                                             accum_out=total[:, n % 2:n % 2 + 1]).then_inc(exped.sem, 1)
                    n = step - 3
                    if n >= 0 and n % G == G - 1 and n // G < 2:
                        s = n // G
                        name = SETS[s]
                        act.wait_ge(slotted.sem, slotted.at(i, s + 1))
                        act.wait_ge(stored[name].sem, stored[name].at(i, 0))
                        nc.scalar.activation(part[name][:, 0], ps[:, 6:8, :], ACT.Copy).then_inc(hi_out.sem, 1)
                        act.wait_ge(left_out.sem, left_out.at(i, s + 1))
                        nc.scalar.activation(part[name][:, 1], left[:, :, :], ACT.Copy).then_inc(mid_out.sem, 1)

        @block.vector
        def _(dve):
            flat = X[:, :, :].rearrange("p t d -> p (t d)")
            with dve.Fori(0, NG) as i:
                nc.vector.tensor_copy(xg[:, :, :].rearrange("p g d -> p (g d)"), flat[:, bass.ds(i * (G * D), G * D)])
                dve.drain()
                ln_stats(nc.vector, stats, mv, var.sem, xg, G, 1e-5)
                dve.wait_ge(rs.sem, rs.at(i, 1))
                for j in range(G):
                    last = nc.vector.tensor_scalar(xg[:, j, :], xg[:, j, :], mv[:, j, 0:1], rstd[:, j:j + 1], ALU.subtract, ALU.mult)
                last.then_inc(h_ready.sem, 1)
                dve.wait_ge(h_turned.sem, h_turned.at(i, 1))
                nc.vector.tensor_scalar(hT[:, :, :], ps[:, 0:DC, :], D ** -0.5, None, ALU.mult).then_inc(h_out.sem, 1)
                for step in range(NS + 4):
                    n = step
                    if n < NS:
                        dve.wait_ge(scored.sem, scored.at(i, n + 1))
                        nc.vector.tensor_reduce(nmax[:, n % 2:n % 2 + 1], ps[:, 2 + n % 2, 0:N], AX.X, ALU.max, negate=True).then_inc(maxed.sem, 1)
                    n = step - 2
                    if 0 <= n < NS:
                        s, j = divmod(n, G)
                        dve.wait_ge(turned.sem, turned.at(i, n + 1))
                        if s == 2:
                            dve.wait_ge(slotted.sem, slotted.at(i, 1))
                        nc.vector.tensor_copy(aT[:, s % 2, :, j * P:(j + 1) * P], ps[:, 4 + n % 2, 0:N].rearrange("p (c q) -> p c q", q=P)).then_inc(turned_out.sem, 1)
                    n = step - 1
                    if 0 <= n < NS:
                        dve.wait_ge(exped.sem, exped.at(i, n + 1))
                        nc.vector.reciprocal(inv[:, n % 2:n % 2 + 1], total[:, n % 2:n % 2 + 1])
                        dve.drain()
                        nc.vector.tensor_scalar(probs[:, n % 2, :], probs[:, n % 2, :], inv[:, n % 2:n % 2 + 1], None, ALU.mult).then_inc(normed.sem, 1)
                    n = step - 4
                    if n >= 0 and n % G == G - 1:
                        s = n // G
                        if s < 2:
                            name = SETS[s]
                            dve.wait_ge(hi_out.sem, hi_out.at(i, s + 1))
                            nc.vector.tensor_tensor(left[:, :, :], ps[:, 6:8, :], part[name][:, 0], ALU.subtract).then_inc(left_out.sem, 1)
                            dve.wait_ge(mid_out.sem, mid_out.at(i, s + 1))
                            nc.vector.tensor_tensor(part[name][:, 2], left[:, :, :], part[name][:, 1], ALU.subtract).then_inc(lo_out.sem, 1)
                            dve.drain()
                        else:
                            dve.wait_ge(slotted.sem, slotted.at(i, 3))
                            nc.vector.tensor_copy(v_all[:, :, :].rearrange("p t d -> p (t d)")[:, bass.ds(i * (G * D), G * D)],
                                                  ps[:, 6:8, :].rearrange("p a n -> p (a n)")).then_inc(v_out.sem, 1)


def causal_attention(nc, ident, ps, scratch, v_all, o_all, spare):
    Q4 = 4
    NU = HB // Q4
    NI = B * DC
    QPART = (0, 0, 1, 1, 0, 2)
    KPART = (0, 1, 0, 1, 2, 0)
    NR = len(QPART) * DH
    NR3 = NR + 3
    HALF = 512
    with ExitStack() as cx:
        sb = tiles(nc, cx)
        qs = [sb(f"t_qs{u}", [P, Q4, S], BF16) for u in range(NU)]
        ks = [sb(f"t_ks{u}", [P, Q4, S], BF16) for u in range(NU)]
        vq = [sb(f"t_vq{u}", [P, TB, Q4, 32]) for u in range(NU)]
        identb = sb("t_identb", [P, P], BF16)
        causal = sb("t_causal", [P, P], BF16)
        causalT = sb("t_causalT", [P, P], BF16)
        nm = sb("t_nm", [P, Q4, TB])
        nmp = sb("t_nmp", [P, 3, Q4, TB], BF16)
        nml = sb("t_nml", [P, Q4, TB])
        nmT = sb("t_nmT", [3 * Q4 * TB, P], BF16)
        pT = spare[:, 0:2 * Q4 * S].rearrange("p (m h q) -> p m h q", m=2, h=Q4)
        oT = sb("t_oT", [P, S])
        inv = sb("t_inv", [P, TB, Q4])

        def sig(name, per=1):
            return Signal(cx, nc, "t_" + name, per)
        consts, stacked, v_ready = sig("consts"), [sig(f"stacked{u}", 12 * 16) for u in range(NU)], sig("v_ready", NU)
        scored, maxed = sig("scored", NU * Q4 * TB), sig("maxed", NU * Q4 * TB)
        split, split_turned, split_out, lowered, max_stored = sig("split", NU), sig("split_turned", NU), sig("split_out", NU), [sig(f"lowered{u}", 16) for u in range(NU)], sig("max_stored", 16 * NU)
        tscored, exped, mixed = sig("tscored", NU * TB * Q4), sig("exped", NU * TB * Q4), [sig(f"mixed{u}", TB) for u in range(NU)]
        o_out, o_turned, o_done = sig("o_out", NU), sig("o_turned", NU), sig("o_done", NU)
        block = cx.enter_context(nc.Block())

        @block.sync
        def _(sp):
            with sp.Fori(0, B) as b:
                with sp.Fori(0, DC) as c:
                    i = b * DC + c
                    for u in range(NU):
                        sp.wait_ge(mixed[u].sem, mixed[u].at(i, 0))
                        for name, dst, parts in (("q", qs[u], QPART), ("k", ks[u], KPART)):
                            for r, part in enumerate(parts):
                                src = scratch[name][part].rearrange("c (u h d) (b t) -> d u h c b t", u=NU, h=Q4, b=B)
                                sp.dma_start(dst[r * DH:(r + 1) * DH, :, :].unsqueeze(2).unsqueeze(3), src[:, u, :, bass.ds(c, 1), bass.ds(b, 1), :]).then_inc(stacked[u].sem, 16)

        @block.gpsimd
        def _(pool):
            for t, fill, mul, step in ((identb, 1.0, 1, -1),):
                pool.memset(t[:, :], 0.0)
                pool.drain()
                pool.affine_select(out=t[:, :], in_=t[:, :], compare_op=ALU.not_equal, fill=fill, base=0, pattern=[[step, P]], channel_multiplier=mul)
                pool.drain()
            for t, mul, step in ((causal, 1, -1), (causalT, -1, 1)):
                pool.memset(t[:, :], 0.0)
                pool.drain()
                pool.affine_select(out=t[:, :], in_=t[:, :], compare_op=ALU.is_ge, fill=-1.0e30, base=0, pattern=[[step, P]], channel_multiplier=mul)
                pool.drain()
            for u in range(NU):
                pool.memset(ks[u][NR:NR3 + 29, :, :], 1.0)
                pool.drain()
                pool.memset(vq[u][:, :, :, :], 0.0)
                pool.drain()
                pool.memset(vq[u][:, :, :, DH:DH + 1], 1.0)
                pool.drain()
            pool.engine_nop().then_inc(consts.sem, 1)
            with pool.Fori(0, B) as b:
                with pool.Fori(0, DC) as c:
                    i = b * DC + c
                    for u in range(NU):
                        pool.wait_ge(mixed[u].sem, mixed[u].at(i, 0))
                        src = v_all[:, :, :].rearrange("p (b t) (c u h d) -> p b t c u h d", b=B, c=DC, u=NU, h=Q4)
                        for h in range(Q4):
                            last = pool.tensor_copy(vq[u][:, :, h, 0:DH].unsqueeze(1).unsqueeze(3), src[:, bass.ds(b, 1), :, bass.ds(c, 1), u, h, :])
                            pool.drain()
                        pool.engine_nop().then_inc(v_ready.sem, 1)
        @block.tensor
        def _(pe):
            pe.wait_ge(consts.sem, 1)
            with pe.Fori(0, NI) as i:
                for u in range(NU):
                    pe.wait_ge(stacked[u].sem, stacked[u].at(i, 12 * 16))
                    for h in range(Q4):
                        for t in range(TB):
                            n = (u * Q4 + h) * TB + t
                            pair = 2 * (t % 2)
                            w = (t + 1) * P
                            pe.wait_ge(maxed.sem, maxed.at(i, max(n - 1, 0)))
                            for lo in range(0, w, HALF):
                                hi = min(w, lo + HALF)
                                nc.tensor.matmul(ps[:, pair + lo // HALF, 0:hi - lo], qs[u][0:NR, h, t * P:w], ks[u][0:NR, h, lo:hi], start=True, stop=hi < w)
                            at = t * P % HALF
                            nc.tensor.matmul(ps[:, pair + t * P // HALF, at:at + P], identb[:, :], causal[:, :], start=False, stop=True).then_inc(scored.sem, 1)
                    pe.wait_ge(split.sem, split.at(i, u + 1))
                    nc.tensor.transpose(ps[0:96, 6, :].bitcast(BF16)[:, 0:P], nmp[:, :, :, :].rearrange("p s h t -> p (s h t)"), identb[:, :]).then_inc(split_turned.sem, 1)
                    pe.wait_ge(lowered[u].sem, lowered[u].at(i, 16))
                    pe.wait_ge(v_ready.sem, v_ready.at(i, u + 1))
                    pe.wait_ge(o_out.sem, o_out.at(i, u))
                    for step in range(TB + 1):
                        t = step
                        if t < TB:
                            for h in range(Q4):
                                n = (u * TB + t) * Q4 + h
                                pair = 2 * (h % 2)
                                pe.wait_ge(exped.sem, exped.at(i, max(n - 1, 0)))
                                at = t * P
                                for m, lo in enumerate(range(at // HALF * HALF, S, HALF)):
                                    lo = max(lo, at)
                                    hi = (lo // HALF + 1) * HALF
                                    bank = pair + lo // HALF
                                    nc.tensor.matmul(ps[:, bank, lo % HALF:lo % HALF + hi - lo], ks[u][0:NR3, h, at:at + P], qs[u][0:NR3, h, lo:hi], start=True, stop=m > 0)
                                nc.tensor.matmul(ps[:, pair + at // HALF, at % HALF:at % HALF + P], identb[:, :], causalT[:, :], start=False, stop=True).then_inc(tscored.sem, 1)
                        t = step - 1
                        if t >= 0:
                            pe.wait_ge(exped.sem, exped.at(i, (u * TB + t + 1) * Q4))
                            at = t * P
                            for lo in range(at // HALF * HALF, S, HALF):
                                half = lo // HALF
                                lo = max(lo, at)
                                hi = (half + 1) * HALF
                                for h in range(Q4):
                                    last = nc.tensor.matmul(ps[32 * h:32 * h + 32, 4 + half, lo % HALF:lo % HALF + hi - lo], vq[u][:, t, h, :], pT[:, t % 2, h, lo:hi],
                                                            start=(t == 0), stop=(t == (half + 1) * HALF // P - 1))
                            last.then_inc(mixed[u].sem, 1)
                    pe.wait_ge(o_out.sem, o_out.at(i, u + 1))
                    for t in range(TB):
                        last = nc.tensor.transpose(ps[:, 6 + t // 4, (t % 4) * P:(t % 4 + 1) * P], oT[:, t * P:(t + 1) * P], ident[:, :])
                    last.then_inc(o_turned.sem, 1)
                    pe.wait_ge(o_done.sem, o_done.at(i, u + 1))

        @block.scalar
        def _(act):
            with act.Fori(0, NI) as i:
                for u in range(NU):
                    act.wait_ge(split_out.sem, split_out.at(i, u + 1))
                    act.dma_start(scratch["max"].rearrange("s (n q) -> (s n) q", q=P), nmT[:, :]).then_inc(max_stored.sem, 16)
                    act.wait_ge(max_stored.sem, max_stored.at(i, 16 * (u + 1)))
                    act.dma_start(qs[u][NR:NR3, :, :].rearrange("s h t -> s (h t)"), scratch["max"]).then_inc(lowered[u].sem, 16)
                    for t in range(TB):
                        for h in range(Q4):
                            n = (u * TB + t) * Q4 + h
                            act.wait_ge(tscored.sem, tscored.at(i, n + 1))
                            if t >= 2:
                                act.wait_ge(mixed[u].sem, mixed[u].at(i, t - 1))
                            pair = 2 * (h % 2)
                            nc.scalar.activation(pT[:, t % 2, h, t * P:S], ps[:, pair:pair + 2, :].rearrange("p a n -> p (a n)")[:, t * P:S], ACT.Exp,
                                                 scale=DH ** -0.5).then_inc(exped.sem, 1)

        @block.vector
        def _(dve):
            with dve.Fori(0, B) as b:
                with dve.Fori(0, DC) as c:
                    i = b * DC + c
                    for u in range(NU):
                        for h in range(Q4):
                            for t in range(TB):
                                n = (u * Q4 + h) * TB + t
                                pair = 2 * (t % 2)
                                dve.wait_ge(scored.sem, scored.at(i, n + 1))
                                nc.vector.tensor_reduce(nm[:, h, t:t + 1], ps[:, pair:pair + 2, :].rearrange("p a n -> p (a n)")[:, 0:(t + 1) * P], AX.X, ALU.max,
                                                        negate=True).then_inc(maxed.sem, 1)
                        dve.drain()
                        nc.vector.tensor_copy(nmp[:, 0], nm[:, :, :])
                        dve.drain()
                        nc.vector.tensor_tensor(nml[:, :, :], nm[:, :, :], nmp[:, 0], ALU.subtract)
                        dve.drain()
                        nc.vector.tensor_copy(nmp[:, 1], nml[:, :, :])
                        dve.drain()
                        nc.vector.tensor_tensor(nmp[:, 2], nml[:, :, :], nmp[:, 1], ALU.subtract).then_inc(split.sem, 1)
                        dve.wait_ge(split_turned.sem, split_turned.at(i, u + 1))
                        if u:
                            dve.wait_ge(lowered[0].sem, lowered[0].at(i, 16))
                        else:
                            dve.wait_ge(lowered[1].sem, lowered[1].at(i, 0))
                        nc.vector.tensor_copy(nmT[:, :], ps[0:96, 6, :].bitcast(BF16)[:, 0:P]).then_inc(split_out.sem, 1)
                        dve.wait_ge(mixed[u].sem, mixed[u].at(i, TB))
                        nc.vector.tensor_copy(oT[:, :], ps[:, 4:6, :].rearrange("p a n -> p (a n)")).then_inc(o_out.sem, 1)
                        dve.wait_ge(o_turned.sem, o_turned.at(i, u + 1))
                        turned = ps[:, 6:8, :].rearrange("p a (t h d) -> p (a t) h d", h=Q4, d=32)
                        nc.vector.reciprocal(inv[:, :, :].unsqueeze(3), turned[:, :, :, DH:DH + 1])
                        dve.drain()
                        dst = o_all[:, :, :].rearrange("p (b t) (c u h d) -> p b t c u h d", b=B, c=DC, u=NU, h=Q4)
                        for h in range(Q4):
                            last = nc.vector.tensor_tensor(dst[:, bass.ds(b, 1), :, bass.ds(c, 1), u, h, :], turned[:, :, h, 0:DH].unsqueeze(1).unsqueeze(3),
                                                           inv[:, :, h:h + 1].unsqueeze(1).unsqueeze(3).broadcast_to((P, 1, TB, 1, DH)), ALU.mult)
                        last.then_inc(o_done.sem, 1)


def slot_layers(nc, X, ident, ps, a, o_all, spare):
    NP, NF = 256, 1024
    CP, CF = NP // P, NF // P
    with ExitStack() as cx:
        sb = tiles(nc, cx)
        pK, pV = sb("e_pK", [P, DC, NP]), sb("e_pV", [P, CP, D])
        fK = spare[:, 0:DC * NF].rearrange("p (k n) -> p k n", k=DC)
        fV = spare[:, DC * NF:DC * NF + CF * D].rearrange("p (k n) -> p k n", k=CF)
        half = sb("e_half", [P, G])
        og = sb("e_og", [P, G, D])
        xg = sb("e_xg", [P, G, D])
        oT = sb("e_oT", [P, DC, GT])
        hT = sb("e_hT", [P, DC, GT])
        z = sb("e_z", [P, G, D])
        hz = sb("e_hz", [P, G, D])
        y = sb("e_y", [P, G, D])
        probs = sb("e_probs", [P, 2, NF])
        taken = DC * NF + CF * D
        pT = spare[:, taken:taken + 2 * NF].rearrange("p (m n) -> p m n", m=2)
        nmax, total, inv = sb("e_nmax", [P, 2, G]), sb("e_total", [P, 2, G]), sb("e_inv", [P, 2, G])
        stats, mv, rstd = sb("e_stats", [P, G, 6]), sb("e_mv", [P, G, 2]), sb("e_rstd", [P, G])

        def sig(name, per=1):
            return Signal(cx, nc, "e_" + name, per)
        loaded, var, rs = sig("loaded"), sig("var", 2), sig("rs", 2)
        og_ready, o_turned, oT_out = sig("og_ready"), sig("o_turned"), sig("oT_out")
        h_ready, h_turned, hT_out = sig("h_ready"), sig("h_turned"), sig("hT_out")
        scored, maxed, exped = sig("scored", 2 * G), sig("maxed", 2 * G), sig("exped", 2 * G)
        turned, turned_out, slotted, added = sig("turned", 2 * G), sig("turned_out", 2 * G), sig("slotted", 2 * G), sig("added", 2 * G)
        block = cx.enter_context(nc.Block())

        @block.sync
        def _(sp):
            for dst, name in ((pK, "pK"), (pV, "pV"), (fK, "fK"), (fV, "fV")):
                sp.dma_start(dst[:, :, :], a["L1_attn_" + name].rearrange("(k p) n -> p k n", p=P)).then_inc(loaded.sem, 16)

        @block.gpsimd
        def _(pool):
            pool.memset(half[:, :], -0.5)
            pool.drain()
            with pool.Fori(0, NG) as i:
                for n in range(2):
                    pool.wait_ge(var.sem, var.at(i, n + 1))
                    pool.tensor_tensor(rstd[:, :], mv[:, :, 1], half[:, :], ALU.pow).then_inc(rs.sem, 1)

        def pair(l, j):
            return 2 + j % 2 if l == 0 else 2 * (j % 2)

        @block.tensor
        def _(pe):
            pe.wait_ge(loaded.sem, 16 * 4)
            with pe.Fori(0, NG) as i:
                for l, (ready, done, out, src, dst) in enumerate(((og_ready, o_turned, oT_out, og, oT), (h_ready, h_turned, hT_out, hz, hT))):
                    K, V, C = ((pK, pV, CP), (fK, fV, CF))[l]
                    pe.wait_ge(ready.sem, ready.at(i, 1))
                    for j in range(G):
                        for k in range(DC):
                            last = nc.tensor.transpose(ps[:, k, j * P:(j + 1) * P], src[:, j, k * P:(k + 1) * P], ident[:, :])
                    last.then_inc(done.sem, 1)
                    pe.wait_ge(out.sem, out.at(i, 1))
                    for step in range(G + 2):
                        j = step
                        if j < G:
                            if j >= 2:
                                pe.wait_ge(exped.sem, exped.at(i, l * G + j - 1))
                            for lo in range(0, C * P, 512):
                                w = min(512, C * P)
                                for k in range(DC):
                                    last = nc.tensor.matmul(ps[:, pair(l, j) + lo // 512, 0:w], dst[:, k, j * P:(j + 1) * P], K[:, k, lo:lo + w],
                                                            start=(k == 0), stop=(k == DC - 1))
                            last.then_inc(scored.sem, 1)
                        j = step - 1
                        if 0 <= j < G:
                            n = l * G + j
                            pe.wait_ge(exped.sem, exped.at(i, n + 1))
                            if j >= 1:
                                pe.wait_ge(turned_out.sem, turned_out.at(i, n))
                            for c in range(C):
                                last = nc.tensor.transpose(ps[:, 4 + c // 4, (c % 4) * P:(c % 4 + 1) * P], probs[:, j % 2, c * P:(c + 1) * P], ident[:, :])
                            last.then_inc(turned.sem, 1)
                        j = step - 2
                        if 0 <= j < G:
                            n = l * G + j
                            pe.wait_ge(turned_out.sem, turned_out.at(i, n + 1))
                            if j >= 2:
                                pe.wait_ge(added.sem, added.at(i, n - 1))
                            for c in range(C):
                                last = nc.tensor.matmul(ps[:, 6 + j % 2, 0:D], pT[:, j % 2, c * P:(c + 1) * P], V[:, c, :], start=(c == 0), stop=(c == C - 1))
                            last.then_inc(slotted.sem, 1)

        @block.scalar
        def _(act):
            with act.Fori(0, NG) as i:
                for l in range(2):
                    w = (NP, NF)[l]
                    for step in range(G + 1):
                        j = step
                        if j < G:
                            n = l * G + j
                            act.wait_ge(maxed.sem, maxed.at(i, n + 1))
                            if n >= 2:
                                act.wait_ge(turned.sem, turned.at(i, n - 1))
                            nc.scalar.activation(probs[:, j % 2, 0:w], ps[:, pair(l, j):pair(l, j) + 1 + l, :].rearrange("p a n -> p (a n)")[:, 0:w], ACT.Exp,
                                                 bias=nmax[:, l, j:j + 1], accum_out=total[:, l, j:j + 1]).then_inc(exped.sem, 1)
                        j = step - 1
                        if 0 <= j < G:
                            n = l * G + j
                            act.wait_ge(turned.sem, turned.at(i, n + 1))
                            if n >= 2:
                                act.wait_ge(slotted.sem, slotted.at(i, n - 1))
                            nc.scalar.activation(pT[:, j % 2, 0:w], ps[:, 4:5 + l, :].rearrange("p a n -> p (a n)")[:, 0:w], ACT.Copy).then_inc(turned_out.sem, 1)

        @block.vector
        def _(dve):
            flat = X[:, :, :].rearrange("p t d -> p (t d)")
            oflat = o_all[:, :, :].rearrange("p t d -> p (t d)")
            with dve.Fori(0, NG) as i:
                def norm(n, src, dst):
                    ln_stats(nc.vector, stats, mv, var.sem, src, G, 1e-5)
                    dve.wait_ge(rs.sem, rs.at(i, n + 1))
                    for j in range(G):
                        last = nc.vector.tensor_scalar(dst(j), src[:, j, :], mv[:, j, 0:1], rstd[:, j:j + 1], ALU.subtract, ALU.mult)
                    return last
                nc.vector.tensor_copy(og[:, :, :].rearrange("p g d -> p (g d)"), oflat[:, bass.ds(i * (G * D), G * D)]).then_inc(og_ready.sem, 1)
                nc.vector.tensor_copy(xg[:, :, :].rearrange("p g d -> p (g d)"), flat[:, bass.ds(i * (G * D), G * D)])
                for l, (done, out, dst) in enumerate(((o_turned, oT_out, oT), (h_turned, hT_out, hT))):
                    w = (NP, NF)[l]
                    rest, sums = ((xg, z), (y, y))[l]
                    dve.wait_ge(done.sem, done.at(i, 1))
                    nc.vector.tensor_scalar(dst[:, :, :], ps[:, 0:DC, :], D ** -0.5, None, ALU.mult).then_inc(out.sem, 1)
                    for step in range(G + 2):
                        j = step
                        if j < G:
                            n = l * G + j
                            dve.wait_ge(scored.sem, scored.at(i, n + 1))
                            nc.vector.tensor_reduce(nmax[:, l, j:j + 1], ps[:, pair(l, j):pair(l, j) + 1 + l, :].rearrange("p a n -> p (a n)")[:, 0:w], AX.X, ALU.max,
                                                    negate=True).then_inc(maxed.sem, 1)
                        j = step - 2
                        if 0 <= j < G:
                            n = l * G + j
                            dve.wait_ge(slotted.sem, slotted.at(i, n + 1))
                            nc.vector.reciprocal(inv[:, l, j:j + 1], total[:, l, j:j + 1])
                            dve.drain()
                            nc.vector.scalar_tensor_tensor(out=sums[:, j, :], in0=ps[:, 6 + j % 2, 0:D], scalar=inv[:, l, j:j + 1], in1=rest[:, j, :],
                                                           op0=ALU.mult, op1=ALU.add).then_inc(added.sem, 1)
                    dve.drain()
                    if l == 0:
                        norm(0, z, lambda j: hz[:, j, :]).then_inc(h_ready.sem, 1)
                        nc.vector.tensor_tensor(y[:, :, :], z[:, :, :], xg[:, :, :], ALU.add)
                    else:
                        norm(1, y, lambda j: X[:, bass.ds(i * G + j, 1), :].rearrange("p a d -> p (a d)"))
                dve.drain()


K2 = 2
E8 = 8


def route(nc, X, ident, ps, a, scratch, routing, layer):
    first = layer == 0
    tag = f"r{layer}_"
    lead = 0 if first else T
    NT = routing["tiles"]
    with ExitStack() as cx:
        sb = tiles(nc, cx)
        xn_all = sb(tag + "xn_all", [P, T, D]) if first else X
        xg = sb(tag + "xg", [P, G, D])
        rT = sb(tag + "rT", [P, DC, GT])
        norms = sb(tag + "norms", [P, 2, DC])
        rwT = sb(tag + "rwT", [P, DC, E8])
        rb = sb(tag + "rb", [1, E8])
        ones1 = sb(tag + "ones1", [1, P])
        half = sb(tag + "half", [P, G])
        stats, mv, rstd = sb(tag + "stats", [P, G, 6]), sb(tag + "mv", [P, G, 2]), sb(tag + "rstd", [P, G])
        eight = sb(tag + "eight", [P, E8])
        eight_i = sb(tag + "eight_i", [P, E8], I32)
        before = sb(tag + "before", [P, P])
        every = sb(tag + "every", [P, P])
        starts = sb(tag + "starts", [1, NT])
        starts_i = sb(tag + "starts_i", [1, NT], I32)
        zeros = sb(tag + "zeros", [P, D])
        lg = sb(tag + "lg", [P, G, E8])
        lmax, lsum = sb(tag + "lmax", [P, G]), sb(tag + "lsum", [P, G])
        top = sb(tag + "top", [P, G, E8])
        idx = sb(tag + "idx", [P, G, E8], U32)
        idxf = sb(tag + "idxf", [P, G, K2])
        wsum = sb(tag + "wsum", [P, G])
        chosen = sb(tag + "chosen", [P, K2, T, E8])
        both = sb(tag + "both", [P, T, E8])
        rank = sb(tag + "rank", [P, T, E8])
        prior = sb(tag + "prior", [P, T, E8])
        count = sb(tag + "count", [P, T, E8])
        offset = sb(tag + "offset", [P, E8])
        padded = sb(tag + "padded", [P, E8])
        padded_i = sb(tag + "padded_i", [P, E8], I32)
        ended = sb(tag + "ended", [1, E8])
        prod = sb(tag + "prod", [P, T, E8])
        place = sb(tag + "place", [P, T])
        passed = sb(tag + "passed", [1, NT, E8])
        tile_f = sb(tag + "tile_f", [1, NT])
        weights, places, tile_expert = routing["weights"], routing["places"], routing["tile_expert"]

        def sig(name, per=1):
            return Signal(cx, nc, tag + name, per)
        loaded, consts, var, rs = sig("loaded"), sig("consts"), sig("var"), sig("rs")
        x_ready, x_kept, x_turned, r_out, logits, logits_out, lexp_in, lexp_out = (sig(n) for n in
            ("x_ready", "x_kept", "x_turned", "r_out", "logits", "logits_out", "lexp_in", "lexp_out"))
        chosen_all, counted, placed = sig("chosen_all"), sig("counted"), sig("placed")
        cleared, kept = sig("cleared"), sig("kept")
        scattered = Signal(cx, nc, "scattered", sem=routing["by_pool"][0])
        block = cx.enter_context(nc.Block())
        L = "L0_ffn_" if first else "L1_ffn_"

        @block.sync
        def _(sp):
            routing["load_rest"](sp)
            sp.dma_start(rwT[:, :, :], a[L + "router_w"].rearrange("(k p) e -> p k e", p=P)).then_inc(loaded.sem, 16)
            sp.dma_start(rb[:, :], a[L + ("router_b" if first else "routing_bias")].rearrange("(a n) -> a n", a=1)).then_inc(loaded.sem, 16)
            if first:
                sp.dma_start(norms[:, 0, :], a[L + "router_ln_scale"]).then_inc(loaded.sem, 16)
                sp.dma_start(norms[:, 1, :], a[L + "router_ln_bias"]).then_inc(loaded.sem, 16)
                sp.wait_ge(consts.sem, 1)
                for t in range(scratch["tiles"]):
                    sp.dma_start(scratch["rows"][t * P:(t + 1) * P, :], zeros[:, :]).then_inc(cleared.sem, 16)
            else:
                sp.dma_start(scratch["rows"][0:T * P, :].rearrange("(t p) d -> p t d", p=P), X[:, :, :]).then_inc(kept.sem, 16)
                sp.wait_ge(kept.sem, 16)

        @block.gpsimd
        def _(pool):
            pool.memset(half[:, :], -0.5)
            pool.drain()
            pool.memset(ones1[:, :], 1.0)
            pool.drain()
            pool.memset(every[:, :], 1.0)
            pool.drain()
            pool.memset(before[:, :], 1.0)
            pool.drain()
            pool.affine_select(out=before[:, :], in_=before[:, :], compare_op=ALU.is_ge, fill=0.0, base=-1, pattern=[[1, P]], channel_multiplier=-1)
            pool.drain()
            pool.iota(eight_i[:, :], pattern=[[1, E8]], base=0, channel_multiplier=0)
            pool.drain()
            pool.iota(starts_i[:, :], pattern=[[P, NT]], base=0, channel_multiplier=0)
            pool.drain()
            pool.memset(zeros[:, :], 0.0).then_inc(consts.sem, 1)
            if first:
                with pool.Fori(0, NG) as i:
                    pool.wait_ge(var.sem, var.at(i, 1))
                    pool.tensor_tensor(rstd[:, :], mv[:, :, 1], half[:, :], ALU.pow).then_inc(rs.sem, 1)
                pool.wait_ge(cleared.sem, 16 * scratch["tiles"])
                pool.wait_ge(x_kept.sem, NG)
            pool.wait_ge(placed.sem, 1)
            for t in range(T):
                for k in range(K2):
                    pool.indirect_dma_start(scratch["rows"], bass.IndirectOffsetOnAxis(ap=places[:, t, k:k + 1], axis=0),
                                            xn_all[:, t, :], None).then_inc(scattered.sem, 16)
            pool.wait_ge(scattered.sem, 16 * T * K2)

        @block.tensor
        def _(pe):
            pe.wait_ge(loaded.sem, 16 * (4 if first else 2))
            pe.wait_ge(consts.sem, 1)
            with pe.Fori(0, NG) as i:
                pe.wait_ge(x_ready.sem, x_ready.at(i, 1))
                for j in range(G):
                    for k in range(DC):
                        last = nc.tensor.transpose(ps[:, k, j * P:(j + 1) * P], xg[:, j, k * P:(k + 1) * P], ident[:, :])
                last.then_inc(x_turned.sem, 1)
                pe.wait_ge(r_out.sem, r_out.at(i, 1))
                pe.wait_ge(logits_out.sem, logits_out.at(i, 0))
                for j in range(G):
                    for k in range(DC):
                        nc.tensor.matmul(ps[:, 2, j * E8:(j + 1) * E8], rT[:, k, j * P:(j + 1) * P], rwT[:, k, :], start=(k == 0), stop=False)
                    last = nc.tensor.matmul(ps[:, 2, j * E8:(j + 1) * E8], ones1[:, :], rb[:, :], start=False, stop=True)
                last.then_inc(logits.sem, 1)
            pe.wait_ge(chosen_all.sem, 1)
            flat = both[:, :, :].rearrange("p t e -> p (t e)")
            nc.tensor.matmul(ps[:, 3, 0:T * E8], before[:, :], flat, start=True, stop=True)
            nc.tensor.matmul(ps[:, 4, 0:T * E8], every[:, :], flat, start=True, stop=True).then_inc(counted.sem, 1)

        @block.scalar
        def _(act):
            with act.Fori(0, NG) as i:
                if first:
                    act.wait_ge(x_ready.sem, x_ready.at(i, 1))
                    nc.scalar.activation(xn_all[:, :, :].rearrange("p t d -> p (t d)")[:, bass.ds(i * (G * D), G * D)], xg[:, :, :].rearrange("p g d -> p (g d)"), ACT.Copy).then_inc(x_kept.sem, 1)
                act.wait_ge(lexp_in.sem, lexp_in.at(i, 1))
                nc.scalar.activation(lg[:, :, :], lg[:, :, :], ACT.Exp, scale=1.0 if first else -1.0).then_inc(lexp_out.sem, 1)

        @block.vector
        def _(dve):
            flat = X[:, :, :].rearrange("p t d -> p (t d)")
            dve.wait_ge(consts.sem, 1)
            dve.wait_ge(loaded.sem, 16 * (4 if first else 2))
            nc.vector.tensor_copy(eight[:, :], eight_i[:, :])
            nc.vector.tensor_copy(starts[:, :], starts_i[:, :])
            dve.drain()
            with dve.Fori(0, NG) as i:
                if first:
                    dve.wait_ge(x_kept.sem, x_kept.at(i, 0))
                last = nc.vector.tensor_copy(xg[:, :, :].rearrange("p g d -> p (g d)"), flat[:, bass.ds(i * (G * D), G * D)])
                if first:
                    dve.drain()
                    ln_stats(nc.vector, stats, mv, var.sem, xg, G, 1e-6)
                    dve.wait_ge(rs.sem, rs.at(i, 1))
                    for j in range(G):
                        last = nc.vector.tensor_scalar(xg[:, j, :], xg[:, j, :], mv[:, j, 0:1], rstd[:, j:j + 1], ALU.subtract, ALU.mult)
                last.then_inc(x_ready.sem, 1)
                dve.wait_ge(x_turned.sem, x_turned.at(i, 1))
                for k in range(DC):
                    if first:
                        last = nc.vector.tensor_scalar(rT[:, k, :], ps[:, k, :], norms[:, 0, k:k + 1], norms[:, 1, k:k + 1], ALU.mult, ALU.add)
                    else:
                        last = nc.vector.tensor_copy(rT[:, k, :], ps[:, k, :])
                last.then_inc(r_out.sem, 1)
                dve.wait_ge(logits.sem, logits.at(i, 1))
                nc.vector.tensor_copy(lg[:, :, :].rearrange("p g e -> p (g e)"), ps[:, 2, 0:G * E8]).then_inc(logits_out.sem, 1)
                dve.drain()
                if first:
                    nc.vector.tensor_reduce(lmax[:, :], lg[:, :, :], AX.X, ALU.max)
                    dve.drain()
                    nc.vector.tensor_tensor(lg[:, :, :], lg[:, :, :], lmax[:, :].unsqueeze(2).broadcast_to((P, G, E8)), ALU.subtract)
                    dve.drain()
                nc.vector.engine_nop().then_inc(lexp_in.sem, 1)
                dve.wait_ge(lexp_out.sem, lexp_out.at(i, 1))
                if first:
                    nc.vector.tensor_reduce(lsum[:, :], lg[:, :, :], AX.X, ALU.add)
                    dve.drain()
                    nc.vector.reciprocal(lsum[:, :], lsum[:, :])
                    dve.drain()
                    nc.vector.tensor_tensor(lg[:, :, :], lg[:, :, :], lsum[:, :].unsqueeze(2).broadcast_to((P, G, E8)), ALU.mult)
                else:
                    nc.vector.tensor_scalar(lg[:, :, :], lg[:, :, :], 1.0, None, ALU.add)
                    dve.drain()
                    nc.vector.reciprocal(lg[:, :, :], lg[:, :, :])
                dve.drain()
                for j in range(G):
                    nc.vector.max(top[:, j, :], lg[:, j, :])
                dve.drain()
                for j in range(G):
                    nc.vector.max_index(idx[:, j, :], top[:, j, :], lg[:, j, :])
                nc.vector.tensor_tensor(wsum[:, :], top[:, :, 0], top[:, :, 1], ALU.add)
                dve.drain()
                nc.vector.reciprocal(wsum[:, :], wsum[:, :])
                nc.vector.tensor_copy(idxf[:, :, :], idx[:, :, 0:K2])
                dve.drain()
                nc.vector.tensor_tensor(weights[:, bass.ds(i * G, G), :], top[:, :, 0:K2], wsum[:, :].unsqueeze(2).broadcast_to((P, G, K2)), ALU.mult)
                for j in range(G):
                    for k in range(K2):
                        nc.vector.tensor_scalar(chosen[:, k, bass.ds(i * G + j, 1), :].rearrange("p a e -> p (a e)"), eight[:, :], idxf[:, j, k:k + 1], None, ALU.is_equal)
                dve.drain()
            nc.vector.tensor_tensor(both[:, :, :], chosen[:, 0], chosen[:, 1], ALU.add).then_inc(chosen_all.sem, 1)
            dve.wait_ge(counted.sem, 1)
            nc.vector.tensor_copy(rank[:, :, :].rearrange("p t e -> p (t e)"), ps[:, 3, 0:T * E8])
            nc.vector.tensor_copy(count[:, :, :].rearrange("p t e -> p (t e)"), ps[:, 4, 0:T * E8])
            nc.vector.memset(prior[:, 0, :], 0.0)
            dve.drain()
            for t in range(1, T):
                nc.vector.tensor_tensor(prior[:, t, :], prior[:, t - 1, :], count[:, t - 1, :], ALU.add)
                dve.drain()
            nc.vector.tensor_tensor(padded[:, :], prior[:, T - 1, :], count[:, T - 1, :], ALU.add)
            dve.drain()
            nc.vector.tensor_scalar(padded_i[:, :], padded[:, :], float(P - 1), None, ALU.add)
            dve.drain()
            nc.vector.tensor_scalar(padded_i[:, :], padded_i[:, :], -P, None, ALU.bitwise_and)
            dve.drain()
            nc.vector.tensor_copy(padded[:, :], padded_i[:, :])
            nc.vector.memset(offset[:, 0:1], float(lead * P))
            dve.drain()
            for e in range(1, E8):
                nc.vector.tensor_tensor(offset[:, e:e + 1], offset[:, e - 1:e], padded[:, e - 1:e], ALU.add)
                dve.drain()
            nc.vector.tensor_tensor(ended[:, :], offset[0:1, :], padded[0:1, :], ALU.add)
            nc.vector.tensor_tensor(rank[:, :, :], rank[:, :, :], prior[:, :, :], ALU.add)
            dve.drain()
            nc.vector.tensor_tensor(rank[:, :, :], rank[:, :, :], offset[:, :].unsqueeze(1).broadcast_to((P, T, E8)), ALU.add)
            dve.drain()
            for k in range(K2):
                nc.vector.tensor_tensor(prod[:, :, :], rank[:, :, :], chosen[:, k], ALU.mult)
                dve.drain()
                nc.vector.tensor_reduce(place[:, :], prod[:, :, :], AX.X, ALU.add)
                dve.drain()
                nc.vector.tensor_copy(places[:, :, k], place[:, :])
                dve.drain()
            nc.vector.engine_nop().then_inc(placed.sem, 1)
            nc.vector.tensor_tensor(passed[:, :, :], starts[:, :].unsqueeze(2).broadcast_to((1, NT, E8)), ended[:, :].unsqueeze(1).broadcast_to((1, NT, E8)), ALU.is_ge)
            dve.drain()
            nc.vector.tensor_reduce(tile_f[:, :], passed[:, :, :], AX.X, ALU.add)
            dve.drain()
            nc.vector.tensor_scalar(tile_f[:, :], tile_f[:, :], float(E8 - 1), float(0 if first else 1), ALU.min, ALU.add)
            dve.drain()
            if lead:
                nc.vector.memset(tile_f[:, 0:lead], 0.0)
                dve.drain()
            nc.vector.tensor_copy(tile_expert[:, :], tile_f[:, :])


def experts(nc, W, ident, ps, a, scratch, routing, layer):
    first = layer == 0
    tag = f"m{layer}_"
    NT = routing["tiles"]
    NE = E8 if first else E8 + 1
    F = 1024 if first else 512
    FC = F // P
    IN = DC * 1024
    WE = IN + FC * D
    with ExitStack() as cx:
        sb = tiles(nc, cx)
        scale, shift = sb(tag + "scale", [P, NE, DC]), sb(tag + "shift", [P, NE, DC])
        if first:
            b1, b2 = sb(tag + "b1", [P, NE, F]), sb(tag + "b2", [P, NE, D])
        rows = sb(tag + "rows", [P, 2, D])
        rowsT = sb(tag + "rowsT", [P, 2, DC, P])
        hid = sb(tag + "hid", [P, 2, F])
        gate = None if first else sb(tag + "gate", [P, 2, F])
        hidT = sb(tag + "hidT", [P, 2, F])
        out = sb(tag + "out", [P, 2, D])
        tile_expert = routing["tile_expert"]

        def sig(name, per=1):
            return Signal(cx, nc, tag + name, per)
        loaded = sig("loaded")
        fetched = [sig(f"fetched{m}", 16) for m in range(2)]
        turned, rowsT_out, hidden, activated, acted = sig("turned"), sig("rowsT_out"), sig("hidden"), sig("activated"), sig("acted")
        acted_gate = sig("acted_gate")
        hid_turned, hidT_out, expert_done, out_ready = sig("hid_turned"), sig("hidT_out"), sig("expert_done"), sig("out_ready")
        stored = [sig(f"stored{m}", 16) for m in range(2)]
        if not first:
            acted = activated
        block = cx.enter_context(nc.Block())

        def expert_of(eng, n):
            return eng.value_load(tile_expert[0:1, bass.ds(n, 1)], min_val=0, max_val=NE - 1)

        def steps(eng, begin, step):
            begin()
            with eng.Fori(0, NT // 2 - 1) as i:
                step(2 * i, 0, True)
                step(2 * i + 1, 1, True)
            step(NT - 2, 0, False)
            step(NT - 1, 1, False)

        @block.sync
        def _(sp):
            if first:
                sp.dma_start(scale[:, :, :], a["L0_ffn_expert_ln_scale"]).then_inc(loaded.sem, 16)
                sp.dma_start(shift[:, :, :], a["L0_ffn_expert_ln_bias"]).then_inc(loaded.sem, 16)
                sp.dma_start(b1[:, :, :], a["L0_ffn_b1"].unsqueeze(0).broadcast_to((P, NE, F))).then_inc(loaded.sem, 16)
                sp.dma_start(b2[:, :, :], a["L0_ffn_b2"].unsqueeze(0).broadcast_to((P, NE, D))).then_inc(loaded.sem, 16)
            with sp.Fori(0, NT // 2) as i:
                for m in range(2):
                    n = 2 * i + m
                    if m == 0:
                        sp.wait_ge(turned.sem, 2 * i)
                    else:
                        sp.wait_ge(turned.sem, 2 * i)
                    sp.dma_start(rows[:, m, :], scratch["rows"][bass.ds(n * P, P), :]).then_inc(fetched[m].sem, 16)

        @block.tensor
        def _(pe):
            pe.wait_ge(routing["weights_in"], routing["weights_count"])

            def turn(n, m, fresh):
                pe.wait_ge(fetched[m].sem, n * 8 + 16 - m * 8)
                if not fresh:
                    pe.wait_ge(rowsT_out.sem, n)
                for k in range(DC):
                    last = nc.tensor.transpose(ps[:, 0, k * P:(k + 1) * P], rows[:, m, k * P:(k + 1) * P], ident[:, :])
                last.then_inc(turned.sem, 1)

            def enter(n, m, fresh):
                e = expert_of(pe, n)
                pe.wait_ge(rowsT_out.sem, n + 1)
                if not fresh:
                    pe.wait_ge(activated.sem, n - 1)
                for c in range(2):
                    for k in range(DC):
                        last = nc.tensor.matmul(ps[:, 2 + 2 * m + c, :], rowsT[:, m, k, :], W[:, bass.ds(e * WE + k * 1024 + c * 512, 512)],
                                                start=(k == 0), stop=(k == DC - 1))
                last.then_inc(hidden.sem, 1)

            def begin():
                turn(0, 0, True)
                enter(0, 0, True)
                turn(1, 1, False)

            def step(n, m, more, second=False):
                pe.wait_ge(acted.sem, n + 1)
                pe.wait_ge(hidT_out.sem, n)
                for c in range(FC):
                    last = nc.tensor.transpose(ps[:, 6 + c // 4, (c % 4) * P:(c % 4 + 1) * P], hid[:, m, c * P:(c + 1) * P], ident[:, :])
                last.then_inc(hid_turned.sem, 1)
                if more or m == 0:
                    enter(n + 1, 1 - m, False if not isinstance(n, int) or n + 1 > 1 else True)
                if more:
                    turn(n + 2, m, False)
                e = expert_of(pe, n)
                pe.wait_ge(hidT_out.sem, n + 1)
                pe.wait_ge(out_ready.sem, n)
                for c in range(FC):
                    last = nc.tensor.matmul(ps[:, 1, 0:D], hidT[:, m, c * P:(c + 1) * P], W[:, bass.ds(e * WE + IN + c * D, D)],
                                            start=(c == 0), stop=(c == FC - 1))
                last.then_inc(expert_done.sem, 1)
            steps(pe, begin, step)

        @block.scalar
        def _(act):
            def activate(n, m):
                if first:
                    act.wait_ge(activated.sem, n + 1)
                    nc.scalar.activation(hid[:, m, :], hid[:, m, :], ACT.Gelu).then_inc(acted.sem, 1)
                else:
                    act.wait_ge(hidden.sem, n + 1)
                    nc.scalar.activation(gate[:, m, :], ps[:, 2 + 2 * m, :], ACT.Silu).then_inc(acted_gate.sem, 1)

            def step(n, m, more):
                act.wait_ge(hid_turned.sem, n + 1)
                nc.scalar.activation(hidT[:, m, :], ps[:, 6:6 + FC // 4, :].rearrange("p a n -> p (a n)"), ACT.Copy).then_inc(hidT_out.sem, 1)
                if more or m == 0:
                    activate(n + 1, 1 - m)
                act.wait_ge(out_ready.sem, n + 1)
                act.dma_start(scratch["results"][bass.ds(n * P, P), :], out[:, m, :]).then_inc(stored[m].sem, 16)
            steps(act, lambda: activate(0, 0), step)
            for m in range(2):
                act.wait_ge(stored[m].sem, 16 * (NT // 2))

        @block.vector
        def _(dve):
            if first:
                dve.wait_ge(loaded.sem, 64)

            def take(n, m):
                e = expert_of(dve, n) if first else None
                dve.wait_ge(turned.sem, n + 1)
                dve.wait_ge(hidden.sem, n - 1) if not isinstance(n, int) or n >= 2 else None
                if first:
                    for k in range(DC):
                        last = nc.vector.tensor_scalar(rowsT[:, m, k, :], ps[:, 0, k * P:(k + 1) * P],
                                                       scale[:, :, :].rearrange("p e k -> p (e k)")[:, bass.ds(e * DC + k, 1)],
                                                       shift[:, :, :].rearrange("p e k -> p (e k)")[:, bass.ds(e * DC + k, 1)], ALU.mult, ALU.add)
                else:
                    last = nc.vector.tensor_copy(rowsT[:, m, :, :].rearrange("p k q -> p (k q)"), ps[:, 0, 0:D])
                last.then_inc(rowsT_out.sem, 1)

            def activate(n, m):
                if first:
                    e = expert_of(dve, n)
                    dve.wait_ge(hidden.sem, n + 1)
                    if not isinstance(n, int) or n >= 2:
                        dve.wait_ge(hid_turned.sem, n - 1)
                    nc.vector.tensor_tensor(hid[:, m, :], ps[:, 2 + 2 * m:4 + 2 * m, :].rearrange("p a n -> p (a n)"),
                                            b1[:, :, :].rearrange("p e f -> p (e f)")[:, bass.ds(e * F, F)], ALU.add).then_inc(activated.sem, 1)
                else:
                    dve.wait_ge(acted_gate.sem, n + 1)
                    if not isinstance(n, int) or n >= 2:
                        dve.wait_ge(hid_turned.sem, n - 1)
                    nc.vector.tensor_tensor(hid[:, m, :], ps[:, 3 + 2 * m, :], gate[:, m, :], ALU.mult).then_inc(activated.sem, 1)

            def begin():
                take(0, 0)
                activate(0, 0)
                take(1, 1)

            def step(n, m, more):
                if more or m == 0:
                    activate(n + 1, 1 - m)
                if more:
                    take(n + 2, m)
                e = expert_of(dve, n) if first else None
                dve.wait_ge(expert_done.sem, n + 1)
                dve.wait_ge(stored[m].sem, (n - m) * 8)
                if first:
                    nc.vector.tensor_tensor(out[:, m, :], ps[:, 1, 0:D], b2[:, :, :].rearrange("p e f -> p (e f)")[:, bass.ds(e * D, D)], ALU.add).then_inc(out_ready.sem, 1)
                else:
                    nc.vector.tensor_copy(out[:, m, :], ps[:, 1, 0:D]).then_inc(out_ready.sem, 1)
            steps(dve, begin, step)


def combine(nc, X, scratch, routing, layer, result=None, prefetch=None):
    first = layer == 0
    tag = f"c{layer}_"
    NBUF = 4
    with ExitStack() as cx:
        sb = tiles(nc, cx)
        got = sb(tag + "got", [P, NBUF, K2, D])
        common = None if first else sb(tag + "common", [P, T, D])
        y = sb(tag + "y", [P, T, D])
        half = sb(tag + "half", [P, G])
        stats, mv, rstd = sb(tag + "stats", [P, G, 6]), sb(tag + "mv", [P, G, 2]), sb(tag + "rstd", [P, G])
        weights, places = routing["weights"], routing["places"]

        def sig(name, per=1):
            return Signal(cx, nc, tag + name, per)
        shared, added, var, rs, normed, stored = (sig(n) for n in ("shared", "added", "var", "rs", "normed", "stored"))
        fetched = [Signal(cx, nc, "fetched", sem=routing["by_pool"][1 + m]) for m in range(NBUF)]
        block = cx.enter_context(nc.Block())

        @block.sync
        def _(sp):
            if prefetch is not None:
                prefetch(sp)
            if not first:
                sp.dma_start(common[:, :, :], scratch["results"][0:T * P, :].rearrange("(t p) d -> p t d", p=P)).then_inc(shared.sem, 16)
            if result is not None:
                for g in range(NG):
                    sp.wait_ge(normed.sem, g + 1)
                    sp.dma_start(result.rearrange("b (t p) d -> p (b t) d", p=P)[:, g * G:(g + 1) * G, :], X[:, g * G:(g + 1) * G, :]).then_inc(stored.sem, 16)
                sp.wait_ge(stored.sem, 16 * NG)

        @block.gpsimd
        def _(pool):
            pool.memset(half[:, :], -0.5)
            pool.drain()

            def power(g):
                pool.wait_ge(var.sem, g + 1)
                pool.tensor_tensor(rstd[:, :], mv[:, :, 1], half[:, :], ALU.pow).then_inc(rs.sem, 1)
            for t in range(T):
                if t >= NBUF:
                    pool.wait_ge(added.sem, t - NBUF + 1)
                for k in range(K2):
                    pool.indirect_dma_start(got[:, t % NBUF, k, :], None, scratch["results"][0:routing["tiles"] * P, :],
                                            bass.IndirectOffsetOnAxis(ap=places[:, t, k:k + 1], axis=0)).then_inc(fetched[t % NBUF].sem, 16)
                if t % G == G - 1 and t >= G:
                    power(t // G - 1)
            power(NG - 1)

        @block.vector
        def _(dve):
            if not first:
                dve.wait_ge(shared.sem, 16)
                nc.vector.tensor_tensor(X[:, :, :], X[:, :, :], common[:, :, :], ALU.add)
                dve.drain()
            for g in range(NG):
                for j in range(G):
                    t = g * G + j
                    dve.wait_ge(fetched[t % NBUF].sem, 32 * (t // NBUF + 1))
                    nc.vector.scalar_tensor_tensor(out=y[:, t, :], in0=got[:, t % NBUF, 0, :], scalar=weights[:, t, 0:1], in1=X[:, t, :], op0=ALU.mult, op1=ALU.add)
                    dve.drain()
                    nc.vector.scalar_tensor_tensor(out=y[:, t, :], in0=got[:, t % NBUF, 1, :], scalar=weights[:, t, 1:2], in1=y[:, t, :], op0=ALU.mult, op1=ALU.add).then_inc(added.sem, 1)
                dve.drain()
                ln_stats(nc.vector, stats, mv, var.sem, y[:, g * G:(g + 1) * G, :], G, 1e-5)
                dve.wait_ge(rs.sem, g + 1)
                for j in range(G):
                    t = g * G + j
                    last = nc.vector.tensor_scalar(X[:, t, :], y[:, t, :], mv[:, j, 0:1], rstd[:, j:j + 1], ALU.subtract, ALU.mult)
                last.then_inc(normed.sem, 1)
                dve.drain()


def decoder(nc, a, out):
    with ExitStack() as cx:
        X = cx.enter_context(nc.sbuf_tensor("X", [P, T, D], F32))
        ident = cx.enter_context(nc.sbuf_tensor("ident", [P, P], F32))
        ps = cx.enter_context(nc.psum_tensor("ps", [P, 8, 512], F32))
        EARLY, WORDS = 24 * 1024, 32 * 1024
        W = cx.enter_context(nc.sbuf_tensor("experts_w", [P, WORDS], F32))
        spare = W[:, EARLY:WORDS]
        weights = cx.enter_context(nc.sbuf_tensor("weights", [P, T, K2], F32))
        places = cx.enter_context(nc.sbuf_tensor("places", [P, T, K2], U32))
        tile_expert = cx.enter_context(nc.sbuf_tensor("tile_expert", [1, 64], I32))
        QT = T * K2 + E8
        scratch = {
            "tiles": T + QT,
            "rows": nc.dram_tensor("queue_rows", ((T + QT) * P, D), F32).ap(),
            "results": nc.dram_tensor("queue_results", ((T + QT) * P, D), F32).ap(),
            "q": nc.dram_tensor("q_parts", (3, DC, P, B * S), BF16).ap(),
            "k": nc.dram_tensor("k_parts", (3, DC, P, B * S), BF16).ap(),
            "max": nc.dram_tensor("max_parts", (3, 4 * S), BF16).ap(),
        }
        x_loaded = cx.enter_context(nc.semaphore("x_loaded"))
        weights_in = [cx.enter_context(nc.semaphore(f"weights_in{n}")) for n in range(2)]

        by_pool = [[cx.enter_context(nc.semaphore(f"by_pool{layer}_{n}")) for n in range(5)] for layer in range(2)]

        def routing(layer):
            words = a[f"w_L{layer}"].shape[2]
            experts_in = a[f"w_L{layer}"].shape[1]
            whole = EARLY // words

            def load(sp, which):
                for e in which:
                    sp.dma_start(W[:, e * words:(e + 1) * words], a[f"w_L{layer}"][:, e, :]).then_inc(weights_in[layer], 16)
            return {"by_pool": by_pool[layer], "weights": weights, "places": places, "tiles": QT + (T if layer else 0),
                    "tile_expert": tile_expert[:, 0:QT + (T if layer else 0)],
                    "weights_in": weights_in[layer], "weights_count": 16 * experts_in,
                    "load_early": lambda sp: load(sp, range(whole)), "load_rest": lambda sp: load(sp, range(whole, experts_in))}
        route0, route1 = routing(0), routing(1)

        with nc.Block() as block:
            @block.sync
            def _(sp):
                sp.dma_start(X[:, :, :], a["x"].rearrange("b (t p) d -> p (b t) d", p=P)).then_inc(x_loaded, 16)

            @block.gpsimd
            def _(pool):
                pool.memset(ident[:, :], 0.0)
                pool.drain()
                pool.affine_select(out=ident[:, :], in_=ident[:, :], compare_op=ALU.not_equal, fill=1.0,
                                   base=0, pattern=[[-1, P]], channel_multiplier=1)
        window_attention(nc, X, ident, ps, a, spare, x_loaded, route0["load_early"])
        nc.all_engine_barrier()
        cross_attention(nc, X, ident, ps, a, spare, 0)
        nc.all_engine_barrier()
        route(nc, X, ident, ps, a, scratch, route0, 0)
        nc.all_engine_barrier()
        experts(nc, W, ident, ps, a, scratch, route0, 0)
        nc.all_engine_barrier()
        combine(nc, X, scratch, route0, 0, prefetch=route1["load_early"])
        nc.all_engine_barrier()
        with nc.sbuf_tensor("v_all", [P, T, D], F32) as v_all:
            slot_projections(nc, X, ident, ps, a, scratch, v_all)
            nc.all_engine_barrier()
            causal_attention(nc, ident, ps, scratch, v_all, v_all, spare)
            nc.all_engine_barrier()
            slot_layers(nc, X, ident, ps, a, v_all, spare)
            nc.all_engine_barrier()
        cross_attention(nc, X, ident, ps, a, spare, 1)
        nc.all_engine_barrier()
        route(nc, X, ident, ps, a, scratch, route1, 1)
        nc.all_engine_barrier()
        experts(nc, W, ident, ps, a, scratch, route1, 1)
        nc.all_engine_barrier()
        combine(nc, X, scratch, route1, 1, result=out)
        nc.all_engine_barrier()


def features(v):
    return np.ascontiguousarray(np.moveaxis(v.reshape(v.shape[:-1] + (DC, P)), -1, 0))


def chunks(w):
    e, r, n = w.shape
    return w.reshape(e, r // P, P, n).transpose(2, 0, 1, 3).reshape(P, e, -1)


def kernel(**inputs):
    import concourse.bacc as bacc
    from concourse.bass_utils import run_bass_kernel_spmd

    z = {k: np.asarray(v) for k, v in inputs.items()}
    arrays = {k: v for k, v in z.items() if not k.startswith(("L0_ffn_w", "L1_ffn_shared", "L1_ffn_gate", "L1_ffn_up", "L1_ffn_down"))}
    arrays["xT"] = np.ascontiguousarray(z["x"].reshape(B * S, D).T)
    for n in ("L0_xattn_bq", "L0_xattn_bk", "L1_xattn_bq", "L1_xattn_bk", "L1_xattn_norm_w", "L1_xattn_norm_b",
              "L1_xattn_norm1_w", "L1_xattn_norm1_b", "L0_ffn_router_ln_scale", "L0_ffn_router_ln_bias",
              "L0_ffn_expert_ln_scale", "L0_ffn_expert_ln_bias"):
        arrays[n] = features(z[n])
    for n in ("L0_ffn_router_w", "L1_ffn_router_w", "L1_attn_qK", "L1_attn_kK", "L1_attn_vK", "L1_attn_pK", "L1_attn_fK"):
        arrays[n] = np.ascontiguousarray(z[n].T)
    arrays["w_L0"] = np.ascontiguousarray(np.concatenate(
        [chunks(z["L0_ffn_w1"].transpose(0, 2, 1)), chunks(z["L0_ffn_w2"].transpose(0, 2, 1))], 2))
    gate, up, down = (np.concatenate([z["L1_ffn_shared_" + n].T[None], z[f"L1_ffn_{n}_w"]]) for n in ("gate", "up", "down"))
    arrays["w_L1"] = np.ascontiguousarray(np.concatenate([chunks(np.concatenate([gate, up], 2)), chunks(down)], 2))

    nc = bacc.Bacc("TRN2", target_bir_lowering=False, num_devices=1)
    feeds, a = {}, {}
    for n, v in arrays.items():
        v = np.ascontiguousarray(v)
        feeds[f"in_{n}"] = v
        a[n] = nc.dram_tensor(f"in_{n}", v.shape, mybir.dt.from_np(v.dtype), kind="ExternalInput").ap()
    out = nc.dram_tensor("out", (B, S, D), F32, kind="ExternalOutput").ap()
    decoder(nc, a, out)
    r = run_bass_kernel_spmd(nc, [feeds], core_ids=[0])
    return r.results[0]["out"]
```

```python
import concourse.bass as bass
import numpy as np
from concourse import mybir
from contextlib import ExitStack

F32 = mybir.dt.float32
BF16 = mybir.dt.bfloat16
I32 = mybir.dt.int32
U32 = mybir.dt.uint32
ACT = mybir.ActivationFunctionType
ALU = mybir.AluOpType
AX = mybir.AxisListType

P = 128
B, S, D = 2, 1024, 256
T = B * S // P
TB = S // P
DC = D // P
G = 4
GT = G * P
NG = T // G
GB = TB // G
H, DH = 16, 16
HB = P // DH
S2 = 77
WIN = 64
NEG = -1.0e9


class Signal:

    def __init__(self, cx, nc, name, per=1, sem=None):
        self.sem = sem if sem is not None else cx.enter_context(nc.semaphore(name))
        if sem is None:
            cx.callback(nc.sync.sem_clear, self.sem)
        self.per = per

    def at(self, i, n):
        return i * self.per + n


def tiles(nc, cx):
    def sb(name, shape, dt=F32):
        return cx.enter_context(nc.sbuf_tensor(name, shape, dt))
    return sb


def ln_stats(dve, stats, mv, sem_var, src, n, eps):
    for j in range(n):
        dve.bn_stats(stats[:, j, :], src[:, j, :])
    dve.drain()
    for j in range(n):
        dve.bn_aggr(mv[:, j, :], stats[:, j, :])
    dve.drain()
    dve.tensor_scalar(mv[:, 0:n, 1], mv[:, 0:n, 1], eps, None, ALU.add).then_inc(sem_var, 1)


def pipeline(eng, total, unroll, jobs, back=0):
    lags = [lag for lag, _ in jobs]

    def step(s, at):
        for lag, job in jobs:
            if not isinstance(s, int) or 0 <= s - lag < total:
                job(s - lag, (at - lag) % unroll)
    head = max(lags) + back
    head += (total - head) % unroll
    for s in range(min(head, total)):
        step(s, s)
    if head < total:
        with eng.Fori(0, (total - head) // unroll) as i:
            for r in range(unroll):
                step(i * unroll + (head + r), head + r)
    for s in range(total, total + max(lags)):
        step(s, s)


def done(eng, signal, n, per=1, part=0):
    if not isinstance(n, int) or n >= 0:
        eng.wait_ge(signal.sem, n * per + (per - part))


def window_attention(nc, X, ident, ps, a, spare, x_loaded, prefetch):
    KW = 2 * P
    PADDED = S + 2 * WIN
    with ExitStack() as cx:
        sb = tiles(nc, cx)
        xT = sb("a_xT", [P, DC, B * PADDED])
        xs = spare[:, 0:B * (TB + 1) * D].rearrange("p (b t d) -> p b t d", b=B, t=TB + 1)
        w = sb("a_w", [P, DC, D])
        band = sb("a_band", [P, KW])
        pad = sb("a_pad", [1, B * PADDED])
        ones = sb("a_ones", [1, P])
        xwT = sb("a_xwT", [P, DC, GT])
        probs = sb("a_probs", [P, 2, KW])
        probsT = sb("a_probsT", [P, 2, 2, P])
        nmax = sb("a_nmax", [P, G])
        total = sb("a_total", [P, G])
        inv = sb("a_inv", [P, G])
        ra = sb("a_ra", [P, G, D])
        y = sb("a_y", [P, G, D])
        stats = sb("a_stats", [P, G, 6])
        mv = sb("a_mv", [P, G, 2])
        rstd = sb("a_rstd", [P, G])
        half = sb("a_half", [P, G])

        def sig(name, per=1):
            return Signal(cx, nc, "a_" + name, per)
        loaded, masks, zeroed = sig("loaded"), sig("masks"), sig("zeroed")
        xw_done, xw_out = sig("xw_done"), sig("xw_out")
        scored, maxed, exped = sig("scored", G), sig("maxed", G), sig("exped", G)
        turned, turned_out = sig("turned", G), sig("turned_out", G)
        mixed, relued, inved = sig("mixed", G), sig("relued", G), sig("inved", G)
        var, rs = sig("var"), sig("rs")
        block = cx.enter_context(nc.Block())

        @block.sync
        def _(sp):
            sp.wait_ge(zeroed.sem, 2)
            for b in range(B):
                sp.dma_start(xT[:, :, b * PADDED + WIN:b * PADDED + WIN + S],
                             a["xT"][:, b * S:(b + 1) * S].rearrange("(k p) t -> p k t", p=P)).then_inc(loaded.sem, 16)
            sp.dma_start(w[:, :, :], a["L0_attn_W"].rearrange("(k p) n -> p k n", p=P)).then_inc(loaded.sem, 16)
            for b in range(B):
                sp.dma_start(xs[WIN:P, b, 0:TB, :], a["x"][b, :, :].rearrange("(t p) d -> p t d", p=P)[0:WIN]).then_inc(loaded.sem, 16)
                sp.dma_start(xs[0:WIN, b, 1:TB + 1, :], a["x"][b, :, :].rearrange("(t p) d -> p t d", p=P)[WIN:P]).then_inc(loaded.sem, 16)
            prefetch(sp)

        @block.gpsimd
        def _(pool):
            pool.memset(xT[:, :, :], 0.0).then_inc(zeroed.sem, 1)
            pool.drain()
            for b in range(B):
                pool.memset(xs[0:WIN, b, 0, :], 0.0)
                pool.drain()
                pool.memset(xs[WIN:P, b, TB, :], 0.0)
                pool.drain()
            pool.memset(half[:, :], -0.5).then_inc(zeroed.sem, 1)
            pool.drain()
            pool.memset(pad[:, :], NEG)
            pool.drain()
            pool.memset(band[:, :], 0.0)
            pool.drain()
            pool.memset(ones[:, :], 1.0)
            for b in range(B):
                pool.drain()
                pool.memset(pad[:, b * PADDED + WIN:b * PADDED + WIN + S], 0.0)
            pool.drain()
            pool.affine_select(out=band[:, :], in_=band[:, :], compare_op=ALU.is_ge, fill=NEG,
                               base=0, pattern=[[1, KW]], channel_multiplier=-1)
            pool.drain()
            pool.affine_select(out=band[:, :], in_=band[:, :], compare_op=ALU.is_ge, fill=NEG,
                               base=2 * WIN, pattern=[[-1, KW]], channel_multiplier=1).then_inc(masks.sem, 1)
            with pool.Fori(0, NG) as i:
                pool.wait_ge(var.sem, var.at(i, 1))
                pool.tensor_tensor(rstd[:, :], mv[:, :, 1], half[:, :], ALU.pow).then_inc(rs.sem, 1)

        @block.tensor
        def _(pe):
            pe.wait_ge(loaded.sem, 16 * (3 + 2 * B))
            pe.wait_ge(masks.sem, 1)

            def project(i, at):
                for n in range(DC):
                    for k in range(DC):
                        last = nc.tensor.matmul(ps[:, n, :], w[:, k, n * P:(n + 1) * P], xT[:, k, bass.ds(at + WIN, GT)],
                                                start=(k == 0), stop=(k == DC - 1))
                last.then_inc(xw_done.sem, 1)

            def score(i, at, j):
                if j >= 2:
                    pe.wait_ge(exped.sem, exped.at(i, j - 1))
                out = ps[:, 2 + j % 2, 0:KW]
                for k in range(DC):
                    nc.tensor.matmul(out, xwT[:, k, j * P:(j + 1) * P], xT[:, k, bass.ds(at + j * P, KW)],
                                     start=(k == 0), stop=False)
                nc.tensor.matmul(out, ident[:, :], band[:, :], start=False, stop=False)
                nc.tensor.matmul(out, ones[:, :], pad[:, bass.ds(at + j * P, KW)],
                                 start=False, stop=True).then_inc(scored.sem, 1)

            def turn(i, j):
                pe.wait_ge(exped.sem, exped.at(i, j + 1))
                if j >= 2:
                    pe.wait_ge(turned_out.sem, turned_out.at(i, j - 1))
                for c in range(2):
                    last = nc.tensor.transpose(ps[:, 4 + j % 2, c * P:(c + 1) * P], probs[:, j % 2, c * P:(c + 1) * P], ident[:, :])
                last.then_inc(turned.sem, 1)

            def mix(i, b, h, j):
                pe.wait_ge(turned_out.sem, turned_out.at(i, j + 1))
                if j >= 2:
                    pe.wait_ge(relued.sem, relued.at(i, j - 1))
                for c in range(2):
                    row = (b * (TB + 1) + h * G + (j + c)) * D
                    last = nc.tensor.matmul(ps[:, 6 + j % 2, 0:D], probsT[:, j % 2, c, :],
                                            spare[:, bass.ds(row, D)],
                                            start=(c == 0), stop=(c == 1))
                last.then_inc(mixed.sem, 1)

            with pe.Fori(0, B) as b:
                with pe.Fori(0, GB) as h:
                    i = b * GB + h
                    at = b * PADDED + h * GT
                    pe.wait_ge(relued.sem, relued.at(i, 0))
                    project(i, at)
                    pe.wait_ge(xw_out.sem, xw_out.at(i, 1))
                    for step in range(G + 2):
                        if step < G:
                            score(i, at, step)
                        if 0 <= step - 1 < G:
                            turn(i, step - 1)
                        if 0 <= step - 2 < G:
                            mix(i, b, h, step - 2)

        @block.scalar
        def _(act):
            with act.Fori(0, NG) as i:
                act.wait_ge(xw_done.sem, xw_done.at(i, 1))
                nc.scalar.activation(xwT[:, :, :], ps[:, 0:DC, :], ACT.Copy).then_inc(xw_out.sem, 1)
                for step in range(G + 2):
                    j = step
                    if j < G:
                        act.wait_ge(maxed.sem, maxed.at(i, j + 1))
                        if j >= 2:
                            act.wait_ge(turned.sem, turned.at(i, j - 1))
                        nc.scalar.activation(probs[:, j % 2, :], ps[:, 2 + j % 2, 0:KW], ACT.Exp, bias=nmax[:, j:j + 1],
                                             accum_out=total[:, j:j + 1]).then_inc(exped.sem, 1)
                    j = step - 2
                    if 0 <= j < G:
                        act.wait_ge(mixed.sem, mixed.at(i, j + 1))
                        act.wait_ge(inved.sem, inved.at(i, j + 1))
                        if j == 0:
                            act.wait_ge(rs.sem, rs.at(i, 0))
                        nc.scalar.activation(ra[:, j, :], ps[:, 6 + j % 2, 0:D], ACT.Relu,
                                             scale=inv[:, j:j + 1]).then_inc(relued.sem, 1)

        @block.vector
        def _(dve):
            dve.wait_ge(x_loaded, 16)
            with dve.Fori(0, NG) as i:
                for step in range(G + 1):
                    j = step
                    if j < G:
                        dve.wait_ge(scored.sem, scored.at(i, j + 1))
                        nc.vector.tensor_reduce(nmax[:, j:j + 1], ps[:, 2 + j % 2, 0:KW], AX.X, ALU.max,
                                                negate=True).then_inc(maxed.sem, 1)
                    j = step - 1
                    if 0 <= j < G:
                        dve.wait_ge(turned.sem, turned.at(i, j + 1))
                        if j >= 2:
                            dve.wait_ge(mixed.sem, mixed.at(i, j - 1))
                        nc.vector.tensor_copy(probsT[:, j % 2, :, :].rearrange("p c q -> p (c q)"),
                                              ps[:, 4 + j % 2, 0:KW]).then_inc(turned_out.sem, 1)
                        nc.vector.reciprocal(inv[:, j:j + 1], total[:, j:j + 1]).then_inc(inved.sem, 1)
                dve.wait_ge(relued.sem, relued.at(i, G))
                nc.vector.scalar_tensor_tensor(out=y[:, :, :].rearrange("p g d -> p (g d)"),
                                               in0=X[:, :, :].rearrange("p t d -> p (t d)")[:, bass.ds(i * (G * D), G * D)], scalar=2.0,
                                               in1=ra[:, :, :].rearrange("p g d -> p (g d)"), op0=ALU.mult, op1=ALU.add)
                dve.drain()
                ln_stats(nc.vector, stats, mv, var.sem, y, G, 1e-5)
                dve.wait_ge(rs.sem, rs.at(i, 1))
                for j in range(G):
                    nc.vector.tensor_scalar(X[:, bass.ds(i * G + j, 1), :].rearrange("p a d -> p (a d)"), y[:, j, :],
                                            mv[:, j, 0:1], rstd[:, j:j + 1], ALU.subtract, ALU.mult)
                dve.drain()


def cross_attention(nc, X, ident, ps, a, spare, layer):
    first = layer == 0
    HH = H // 2
    BH = 4
    NM = 4
    with ExitStack() as cx:
        tag = f"x{layer}_"
        sb = tiles(nc, cx)
        names = ["Wq", "Wk", "Wv", "Wo"]
        wt = {n: sb(tag + n, [P, DC, D]) for n in names}
        bqk = sb(tag + "bqk", [P, 2, DC])
        rows = sb(tag + "rows", [1, 2, D])
        norms = sb(tag + "norms", [P, 4, DC])
        ones = sb(tag + "ones", [1, P])
        own = sb(tag + "own", [P, HB])
        half = sb(tag + "half", [P, T])
        if first:
            mask = sb(tag + "mask", [P, TB, S2])
            less = sb(tag + "less", [P, TB, S2])
        ctx = sb(tag + "ctx", [S2, B, D])
        ctxT = sb(tag + "ctxT", [P, DC, S2])
        kT = sb(tag + "kT", [P, DC, S2])
        keys = sb(tag + "keys", [P, B, DC, HB, S2])
        vals = sb(tag + "vals", [S2, B, D])
        work = sb(tag + "work", [P, 2 * HH * P])
        xn = work[:, 0:2 * D].rearrange("p (m d) -> p m d", m=2)
        xT = work[:, 2 * D:4 * D].rearrange("p (m k q) -> p m k q", m=2, k=DC)
        pT = work[0:S2, :].rearrange("s (v h q) -> s v h q", v=2, h=HH)
        qT_all = spare[:, 0:T * D].rearrange("p (t k q) -> p t k q", t=T, k=DC)
        o_all = spare[:, T * D:2 * T * D].rearrange("p (t d) -> p t d", t=T)
        qT = sb(tag + "qT", [P, NM, DC, P])
        att = sb(tag + "att", [P, NM, H, S2])
        top = sb(tag + "top", [P, NM, H])
        total = sb(tag + "total", [P, NM, H])
        o = spare[:, 0:T * D].rearrange("p (t d) -> p t d", t=T)
        stats = sb(tag + "stats", [P, T, 6])
        mv = sb(tag + "mv", [P, T, 2])
        rstd = sb(tag + "rstd", [P, T])

        def sig(name, per=1):
            return Signal(cx, nc, tag + name, per)
        loaded, consts = sig("loaded"), sig("consts")
        kv_mm, kv_out = sig("kv_mm"), sig("kv_out")
        var, rs = sig("var"), sig("rs")
        x_ready, x_turned, x_out, q_done, q_out = (sig(n) for n in ("x_ready", "x_turned", "x_out", "q_done", "q_out"))
        qT_ready, scored, scored_out, masked, topped, lowered, exped, summed = (
            sig(n) for n in ("qT_ready", "scored", "scored_out", "masked", "topped", "lowered", "exped", "summed"))
        turned, turned_out, mixed_lo, mixed, o_out = (sig(n) for n in ("turned", "turned_out", "mixed_lo", "mixed", "o_out"))
        grouped = sig("grouped")
        n_ready, n_turned, n_out, wo_done, y_out = (sig(n) for n in ("n_ready", "n_turned", "n_out", "wo_done", "y_out"))
        block = cx.enter_context(nc.Block())
        L = "L0_xattn_" if first else "L1_xattn_"
        NLOAD = 4 + 2 + 2 + 1 + (1 if first else 4)
        NCTX = 0 if first else 1

        def regroup(eng, b):
            M = P // 4
            eng.wait_ge(o_out.sem, T)
            for h in range(GB):
                for uu in range(4):
                    for e in range(2):
                        at = (P // 2) * e + M * h
                        tiles_o = o_all[uu * M:(uu + 1) * M, (b * GB + h) * G:(b * GB + h + 1) * G, :]
                        eng.tensor_copy(o[at:at + M, b * TB:(b + 1) * TB, :].rearrange("p c (j u d) -> p u c j d", u=4, d=DH)[:, uu],
                                        tiles_o.rearrange("p j (c e d) -> p e c j d", e=2, d=DH)[:, e])
            eng.drain()
            eng.engine_nop().then_inc(grouped.sem, 1)

        def fetch_q(eng, n, m):
            if first:
                done(eng, scored, n - NM, 2)
                nc.scalar.activation(qT[:, m, :, :].rearrange("p k q -> p (k q)"), spare[:, bass.ds(n * D, D)], ACT.Copy).then_inc(qT_ready.sem, 1)
            else:
                done(eng, mixed, n - NM)
                eng.tensor_copy(qT[:, m, :, :].rearrange("p k q -> p (k q)"), spare[:, bass.ds(n * D, D)]).then_inc(qT_ready.sem, 1)

        @block.sync
        def _(sp):
            for n in names:
                sp.dma_start(wt[n][:, :, :], a[L + n].rearrange("(k p) n -> p k n", p=P)).then_inc(loaded.sem, 16)
            for n, name in enumerate(("bq", "bk")):
                sp.dma_start(bqk[:, n, :], a[L + name]).then_inc(loaded.sem, 16)
            for n, name in enumerate(("bv", "bo")):
                sp.dma_start(rows[:, n, :], a[L + name].rearrange("(a n) -> a n", a=1)).then_inc(loaded.sem, 16)
            sp.dma_start(ctx[:, :, :], a["ctx_1024"].rearrange("b s d -> s b d")).then_inc(loaded.sem, 16)
            if first:
                sp.dma_start(mask[:, :, :], a["mask_1x1xSxS2_fk0"].rearrange("a c (t p) s -> p (a c t) s", p=P)).then_inc(loaded.sem, 16)
            else:
                for n, name in enumerate(("norm_w", "norm_b", "norm1_w", "norm1_b")):
                    sp.dma_start(norms[:, n, :], a[L + name]).then_inc(loaded.sem, 16)

        @block.gpsimd
        def _(pool):
            pool.memset(half[:, :], -0.5)
            pool.drain()
            pool.memset(ones[:, :], 1.0)
            pool.drain()
            pool.memset(mv[:, :, :], 1.0)
            pool.drain()
            pool.memset(own[:, :], 1.0)
            pool.drain()
            pool.affine_select(out=own[:, :], in_=own[:, :], compare_op=ALU.is_ge, fill=0.0,
                               base=0, pattern=[[-DH, HB]], channel_multiplier=1)
            pool.drain()
            pool.affine_select(out=own[:, :], in_=own[:, :], compare_op=ALU.is_ge, fill=0.0,
                               base=DH - 1, pattern=[[DH, HB]], channel_multiplier=-1).then_inc(consts.sem, 1)

            def power(n, rows, w):
                pool.wait_ge(var.sem, n + 1)
                pool.tensor_tensor(rstd[0:rows, 0:w], mv[0:rows, 0:w, 1], half[0:rows, 0:w], ALU.pow).then_inc(rs.sem, 1)
            if not first:
                power(0, S2, B)
                power(1, P, T)

            def add_mask(n, m):
                done(pool, scored_out, n, 2)
                pool.tensor_tensor(att[:, m], att[:, m], less[:, bass.ds(n % TB, 1), :].broadcast_to((P, H, S2)), ALU.add).then_inc(masked.sem, 1)

            def lower(n, m):
                done(pool, topped, n)
                pool.tensor_tensor(att[:, m], att[:, m], top[:, m, :].unsqueeze(2).broadcast_to((P, H, S2)), ALU.subtract).then_inc(lowered.sem, 1)
            if first:
                pipeline(pool, T, NM, [(1, lower), (0, add_mask)])
            else:
                pool.wait_ge(q_out.sem, T)
                pipeline(pool, T, NM, [(0, lambda n, m: fetch_q(pool, n, m))], back=4)
                regroup(pool, 0)
                power(2, P, T)
            power(0 if first else 3, P, T)

        @block.tensor
        def _(pe):
            pe.wait_ge(loaded.sem, 16 * NLOAD)
            pe.wait_ge(consts.sem, 1)
            if not first:
                pe.wait_ge(x_ready.sem, 1)
            for b in range(B):
                pe.wait_ge(kv_out.sem, 3 * b) if b else None
                for k in range(DC):
                    last = nc.tensor.transpose(ps[:, k, 0:S2], ctx[:, b, k * P:(k + 1) * P], ident[0:S2, 0:S2])
                last.then_inc(kv_mm.sem, 1)
                pe.wait_ge(kv_out.sem, 3 * b + 1)
                for n in range(DC):
                    for k in range(DC):
                        last = nc.tensor.matmul(ps[:, 2 + n, 0:S2], wt["Wk"][:, k, n * P:(n + 1) * P], ctxT[:, k, :],
                                                start=(k == 0), stop=(k == DC - 1))
                last.then_inc(kv_mm.sem, 1)
                for k in range(DC):
                    nc.tensor.matmul(ps[0:S2, 4, 0:D], ctxT[:, k, :], wt["Wv"][:, k, :], start=(k == 0), stop=False)
                nc.tensor.matmul(ps[0:S2, 4, 0:D], ones[:, 0:S2], rows[:, 0, :], start=False, stop=True).then_inc(kv_mm.sem, 1)
            pe.wait_ge(kv_out.sem, 3 * B)

            def turn_x(n, m):
                done(pe, x_ready, n + NCTX)
                done(pe, x_out, n - 2)
                for k in range(DC):
                    last = nc.tensor.transpose(ps[:, m, k * P:(k + 1) * P], xn[:, m, k * P:(k + 1) * P], ident[:, :])
                last.then_inc(x_turned.sem, 1)

            def query(n, m):
                done(pe, x_out, n)
                done(pe, q_out, n - 2)
                for c in range(DC):
                    for k in range(DC):
                        last = nc.tensor.matmul(ps[:, 2 + m, c * P:(c + 1) * P], wt["Wq"][:, k, c * P:(c + 1) * P], xT[:, m, k, :],
                                                start=(k == 0), stop=(k == DC - 1))
                last.then_inc(q_done.sem, 1)
            pipeline(pe, T, 2, [(0, turn_x), (1, query)], back=2)

            def score(n, m, hi):
                done(pe, qT_ready, n)
                done(pe, scored_out, n - 1, 2, 1 - hi)
                for bank in range(2 * hi, 2 * hi + 2):
                    c, r = bank * BH // HB, bank * BH % HB
                    last = nc.tensor.matmul(ps[:, bank, 0:BH * S2], qT[:, m, c, :],
                                            keys[:, :, :, :, :].rearrange("p b c h s -> p (b c h s)")[:, bass.ds((n // TB) * (H * S2) + (c * HB + r) * S2, BH * S2)],
                                            start=True, stop=True)
                last.then_inc(scored.sem, 1)

            def turn(n, m, hi):
                done(pe, summed, n)
                done(pe, turned_out, n - 1 + hi, 2, hi)
                for h in range(HH):
                    last = nc.tensor.transpose(ps[0:S2, 4 + h // 4, (h % 4) * P:(h % 4 + 1) * P], att[:, m, hi * HH + h, :], ident[:, :])
                last.then_inc(turned.sem, 1)

            def mix(n, m, hi):
                if not hi:
                    done(pe, o_out, n - 2)
                done(pe, turned_out, n, 2, 1 - hi)
                for h in range(hi * HH, (hi + 1) * HH):
                    last = nc.tensor.matmul(ps[:, 6 + m % 2, h * DH:(h + 1) * DH], pT[:, hi, h % HH, :],
                                            vals[:, :, :].rearrange("s b d -> s (b d)")[:, bass.ds((n // TB) * D + h * DH, DH)], start=True, stop=True)
                if not hi:
                    last.then_inc(mixed_lo.sem, 1)
                    return
                if not first:
                    for k in range(DC):
                        last = nc.tensor.transpose(ps[:, 6 + m % 2, D + k * P:D + (k + 1) * P], qT[:, m, k, :], ident[:, :])
                last.then_inc(mixed.sem, 1)
            pe.wait_ge(q_out.sem, T)
            pipeline(pe, T, NM, [(4, lambda n, m: mix(n, m, 1)), (3, lambda n, m: turn(n, m, 0)), (0, lambda n, m: score(n, m, 0)),
                                 (3, lambda n, m: turn(n, m, 1)), (3, lambda n, m: mix(n, m, 0)), (0, lambda n, m: score(n, m, 1))], back=2)

            def turn_o(n, m):
                done(pe, n_ready, n)
                done(pe, n_out, n - 2)
                for k in range(DC):
                    last = nc.tensor.transpose(ps[:, m, k * P:(k + 1) * P], xn[:, m, k * P:(k + 1) * P], ident[:, :])
                last.then_inc(n_turned.sem, 1)

            def leave(n, m):
                done(pe, n_out, n)
                done(pe, y_out, n - 2)
                for k in range(DC):
                    nc.tensor.matmul(ps[:, 2 + m, 0:D], xT[:, m, k, :], wt["Wo"][:, k, :], start=(k == 0), stop=False)
                nc.tensor.matmul(ps[:, 2 + m, 0:D], ones[:, :], rows[:, 1, :], start=False, stop=True).then_inc(wo_done.sem, 1)
            pipeline(pe, T, 2, [(0, turn_o), (1, leave)], back=2)

        @block.scalar
        def _(act):
            act.wait_ge(loaded.sem, 16 * NLOAD)
            act.wait_ge(consts.sem, 1)

            def fill(n, m):
                done(act, x_turned, n - 2)
                nc.scalar.activation(xn[:, m, :], X[:, bass.ds(n, 1), :].rearrange("p a d -> p (a d)"), ACT.Copy).then_inc(x_ready.sem, 1)

            def query_out(n, m):
                done(act, q_done, n)
                for k in range(DC):
                    src = ps[:, 2 + m, k * P:(k + 1) * P]
                    if first:
                        last = nc.scalar.activation(qT_all[:, bass.ds(n, 1), k, :].rearrange("p a q -> p (a q)"), src, ACT.Identity,
                                                    bias=bqk[:, 0, k:k + 1], scale=DH ** -0.5)
                    else:
                        dst = spare[:, 0:T * D].rearrange("p (g v k w m) -> p g k v w m", g=NG, v=4, k=DC, w=4)
                        last = nc.scalar.activation(dst[:, bass.ds(n // G, 1), k, :, :, bass.ds((n % G) * (P // DH), P // DH)],
                                                    src.rearrange("p (a m v w) -> p a v w m", a=1, v=4, w=4), ACT.Identity, bias=bqk[:, 0, k:k + 1])
                last.then_inc(q_out.sem, 1)
            act.wait_ge(kv_out.sem, 3 * B)
            pipeline(act, T, 2, ([(0, fill)] if first else []) + [(1, query_out)], back=2)
            act.drain()

            def exps(n, m):
                if first:
                    done(act, lowered, n)
                else:
                    done(act, scored_out, n, 2)
                nc.scalar.activation(att[:, m].rearrange("p h s -> p (h s)"), att[:, m].rearrange("p h s -> p (h s)"), ACT.Exp,
                                     scale=1.0 if first else DH ** -0.5).then_inc(exped.sem, 1)

            def turn_out(n, m, hi):
                done(act, turned, n, 2, 1 - hi)
                done(act, mixed if hi else mixed_lo, n - 1)
                nc.scalar.activation(pT[:, hi, :, :].rearrange("s h q -> s (h q)"), ps[0:S2, 4:6, :].rearrange("s a n -> s (a n)"), ACT.Copy).then_inc(turned_out.sem, 1)
            pipeline(act, T, NM, ([(0, lambda n, m: fetch_q(act, n, m))] if first else []) + [(4, lambda n, m: turn_out(n, m, 0)), (2, exps), (4, lambda n, m: turn_out(n, m, 1))], back=4)

            def fill_o(n, m):
                done(act, n_turned, n - 2)
                nc.scalar.activation(xn[:, m, :], o_all[:, bass.ds(n, 1), :].rearrange("p a d -> p (a d)"), ACT.Copy).then_inc(n_ready.sem, 1)

            def norm_out(n, m):
                done(act, n_turned, n)
                done(act, wo_done, n - 2)
                if first:
                    last = nc.scalar.activation(xT[:, m, :, :].rearrange("p k q -> p (k q)"), ps[:, m, 0:D], ACT.Copy)
                else:
                    for k in range(DC):
                        last = nc.scalar.activation(xT[:, m, k, :], ps[:, m, k * P:(k + 1) * P], ACT.Identity,
                                                    scale=norms[:, 2, k:k + 1], bias=norms[:, 3, k:k + 1])
                last.then_inc(n_out.sem, 1)
            act.wait_ge(o_out.sem, T)
            pipeline(act, T, 2, ([(0, fill_o)] if first else []) + [(1, norm_out)], back=2)

        @block.vector
        def _(dve):
            dve.wait_ge(loaded.sem, 16 * NLOAD)
            dve.wait_ge(consts.sem, 1)

            def statistics(src, rows, n):
                for t in range(n):
                    nc.vector.bn_stats(stats[0:rows, t, :], src[:, t, :])
                dve.drain()
                for t in range(n):
                    nc.vector.bn_aggr(mv[0:rows, t, :], stats[0:rows, t, :])
                dve.drain()
                nc.vector.tensor_scalar(mv[0:rows, 0:n, 1], mv[0:rows, 0:n, 1], 1e-5, None, ALU.add).then_inc(var.sem, 1)
            if first:
                nc.vector.tensor_scalar(less[:, :, :], mask[:, :, :], -1.0, 1.0e10, ALU.add, ALU.mult)
                nc.vector.tensor_scalar(bqk[:, 0, :], bqk[:, 0, :], DH ** -0.5, None, ALU.mult)
            else:
                statistics(ctx, S2, B)
                dve.wait_ge(rs.sem, 1)
                for b in range(B):
                    last = nc.vector.tensor_scalar(ctx[:, b, :], ctx[:, b, :], mv[0:S2, b, 0:1], rstd[0:S2, b:b + 1], ALU.subtract, ALU.mult)
                last.then_inc(x_ready.sem, 1)
                dve.drain()
                statistics(X, P, T)
            dve.drain()
            for b in range(B):
                dve.wait_ge(kv_mm.sem, 3 * b + 1)
                for k in range(DC):
                    if first:
                        last = nc.vector.tensor_copy(ctxT[:, k, :], ps[:, k, 0:S2])
                    else:
                        last = nc.vector.tensor_scalar(ctxT[:, k, :], ps[:, k, 0:S2], norms[:, 0, k:k + 1], norms[:, 1, k:k + 1], ALU.mult, ALU.add)
                last.then_inc(kv_out.sem, 1)
                dve.wait_ge(kv_mm.sem, 3 * b + 2)
                for k in range(DC):
                    nc.vector.tensor_scalar(kT[:, k, :], ps[:, 2 + k, 0:S2], bqk[:, 1, k:k + 1], None, ALU.add)
                dve.drain()
                for n in range(HB):
                    last = nc.vector.tensor_scalar(keys[:, b, :, n, :], kT[:, :, :], own[:, n:n + 1], None, ALU.mult)
                last.then_inc(kv_out.sem, 1)
                dve.wait_ge(kv_mm.sem, 3 * b + 3)
                nc.vector.tensor_copy(vals[:, b, :], ps[0:S2, 4, 0:D]).then_inc(kv_out.sem, 1)

            def norm_x(n, m):
                done(dve, x_turned, n - 2)
                nc.vector.tensor_scalar(xn[:, m, :], X[:, bass.ds(n, 1), :].rearrange("p a d -> p (a d)"), mv[:, bass.ds(n, 1), 0], rstd[:, bass.ds(n, 1)],
                                        ALU.subtract, ALU.mult).then_inc(x_ready.sem, 1)

            def x_outs(n, m):
                done(dve, x_turned, n)
                done(dve, q_done, n - 2)
                for k in range(DC):
                    if first:
                        last = nc.vector.tensor_copy(xT[:, m, k, :], ps[:, m, k * P:(k + 1) * P])
                    else:
                        last = nc.vector.tensor_scalar(xT[:, m, k, :], ps[:, m, k * P:(k + 1) * P], norms[:, 0, k:k + 1], norms[:, 1, k:k + 1], ALU.mult, ALU.add)
                last.then_inc(x_out.sem, 1)
            if not first:
                dve.wait_ge(rs.sem, 2)
            pipeline(dve, T, 2, ([] if first else [(0, norm_x)]) + [(1, x_outs)], back=2)

            def score_out(n, m):
                for hi in range(2):
                    heads = slice(hi * HH, (hi + 1) * HH)
                    done(dve, scored, n, 2, 1 - hi)
                    if not hi:
                        done(dve, turned, n - NM, 2)
                    src = ps[:, 2 * hi:2 * hi + 2, 0:BH * S2].rearrange("p a (h s) -> p a h s", h=BH)
                    dst = att[:, m, heads, :].rearrange("p (a h) s -> p a h s", a=2)
                    if first:
                        last = nc.vector.tensor_tensor(dst, src, mask[:, bass.ds(n % TB, 1), :].unsqueeze(1).broadcast_to((P, 2, BH, S2)), ALU.mult)
                    else:
                        if not hi:
                            done(dve, exped, n - NM)
                        peak = top[:, m, heads].rearrange("p (a h) -> p a h", a=2)
                        nc.vector.tensor_reduce(peak, src, AX.X, ALU.max)
                        dve.drain()
                        last = nc.vector.tensor_tensor(dst, src, peak.unsqueeze(3).broadcast_to((P, 2, BH, S2)), ALU.subtract)
                    last.then_inc(scored_out.sem, 1)

            def maximum(n, m):
                done(dve, masked, n)
                nc.vector.tensor_reduce(top[:, m, :], att[:, m], AX.X, ALU.max).then_inc(topped.sem, 1)

            def summing(n, m):
                done(dve, exped, n)
                nc.vector.tensor_reduce(total[:, m, :], att[:, m], AX.X, ALU.add)
                dve.drain()
                nc.vector.reciprocal(total[:, m, :], total[:, m, :]).then_inc(summed.sem, 1)

            def out(n, m):
                done(dve, mixed, n)
                dst = o_all[:, bass.ds(n, 1), :].rearrange("p a (h d) -> p (a h) d", d=DH)
                last = nc.vector.tensor_tensor(dst, ps[:, 6 + m % 2, 0:D].rearrange("p (h d) -> p h d", d=DH),
                                               total[:, m, :].unsqueeze(2).broadcast_to((P, H, DH)), ALU.mult)
                if not first:
                    dve.drain()
                    flat = o_all[:, bass.ds(n, 1), :].rearrange("p a d -> p (a d)")
                    last = nc.vector.tensor_tensor(flat, ps[:, 6 + m % 2, D:2 * D], flat, ALU.add)
                last.then_inc(o_out.sem, 1)
            pipeline(dve, T, NM, ([(1, maximum)] if first else []) + [(0, score_out), (2, summing), (4, out)], back=4)
            if not first:
                dve.drain()
                regroup(nc.vector, 1)
                dve.wait_ge(grouped.sem, 2)
                statistics(o, P, T)
                nc.vector.tensor_tensor(X[:, :, :], X[:, :, :], o[:, :, :], ALU.add)
                dve.wait_ge(rs.sem, 3)

            def norm_o(n, m):
                done(dve, n_turned, n - 2)
                nc.vector.tensor_scalar(xn[:, m, :], o[:, bass.ds(n, 1), :].rearrange("p a d -> p (a d)"), mv[:, bass.ds(n, 1), 0], rstd[:, bass.ds(n, 1)],
                                        ALU.subtract, ALU.mult).then_inc(n_ready.sem, 1)

            def add(n, m):
                done(dve, wo_done, n)
                x = X[:, bass.ds(n, 1), :].rearrange("p a d -> p (a d)")
                nc.vector.tensor_tensor(x, ps[:, 2 + m, 0:D], x, ALU.add).then_inc(y_out.sem, 1)
            pipeline(dve, T, 2, ([] if first else [(0, norm_o)]) + [(2, add)], back=2)
            dve.drain()
            statistics(X, P, T)
            dve.wait_ge(rs.sem, 1 if first else 4)
            for t in range(T):
                nc.vector.tensor_scalar(X[:, t, :], X[:, t, :], mv[:, t, 0:1], rstd[:, t:t + 1], ALU.subtract, ALU.mult)


def slot_projections(nc, X, ident, ps, a, scratch, v_all, spare, prefetch):
    N = D
    NC = N // P
    SETS = ("q", "k", "v")
    R = 2
    with ExitStack() as cx:
        sb = tiles(nc, cx)
        words = [0, 3 * NC * GT, 3 * NC * GT + 3 * DC * N, 3 * NC * GT + 3 * DC * N + 3 * NC * D]
        aT = spare[:, words[0]:words[1]].rearrange("p (s c q) -> p s c q", s=3, c=NC)
        kT = spare[:, words[1]:words[2]].rearrange("p (s k n) -> p s k n", s=3, k=DC)
        vals = spare[:, words[2]:words[3]].rearrange("p (s k n) -> p s k n", s=3, k=NC)
        half = sb("d_half", [P, 1])
        xn = sb("d_xn", [P, R, D])
        hT = sb("d_hT", [P, R, DC, P])
        probs = sb("d_probs", [P, R, 3, N])
        part = {n: sb("d_part_" + n, [P, 3, DC, GT], BF16) for n in ("q", "k")}
        left = sb("d_left", [P, DC, GT])
        nmax = sb("d_nmax", [P, R, 3])
        total = sb("d_total", [P, R, 3])
        stats, mv, rstd = sb("d_stats", [P, G, 6]), sb("d_mv", [P, G, 2]), sb("d_rstd", [P, G])

        def sig(name):
            return Signal(cx, nc, "d_" + name)
        loaded, loaded_v, consts, var, rs = sig("loaded"), sig("loaded_v"), sig("consts"), sig("var"), sig("rs")
        h_ready, h_turned, h_out = sig("h_ready"), sig("h_turned"), sig("h_out")
        scored, maxed, exped, normed, turned, turned_out = (sig(n) for n in ("scored", "maxed", "exped", "normed", "turned", "turned_out"))
        slotted, v_out = [sig("slotted_" + n) for n in SETS], sig("v_out")
        hi_out, left_out, mid_out, lo_out, stored = ([sig(f"{w}_{n}") for n in ("q", "k")] for w in ("hi_out", "left_out", "mid_out", "lo_out", "stored"))
        block = cx.enter_context(nc.Block())

        def last_of_group(job):
            return lambda n, m: job(n // G) if m == G - 1 else None

        @block.sync
        def _(sp):
            for n, name in enumerate(SETS):
                sp.dma_start(kT[:, n, :, :], a[f"L1_attn_{name}K"].rearrange("(k p) n -> p k n", p=P)).then_inc(loaded.sem, 16)
            for n, name in enumerate(SETS):
                sp.dma_start(vals[:, n, :, :], a[f"L1_attn_{name}V"].rearrange("(k p) n -> p k n", p=P)).then_inc(loaded_v.sem, 16)
            prefetch(sp)
            with sp.Fori(0, NG) as i:
                for n, name in enumerate(("q", "k")):
                    sp.wait_ge(lo_out[n].sem, i + 1)
                    rows = scratch[name].rearrange("s c p t -> p (s c) t")
                    sp.dma_start(rows[:, :, bass.ds(i * GT, GT)], part[name][:, :, :, :].rearrange("p s c t -> p (s c) t")).then_inc(stored[n].sem, 16)
            for n in range(2):
                sp.wait_ge(stored[n].sem, 16 * NG)

        @block.gpsimd
        def _(pool):
            pool.memset(half[:, :], -0.5)
            pool.drain()

            def power(n, m):
                done(pool, var, n)
                pool.tensor_tensor(rstd[:, m:m + 1], mv[:, m, 1:2], half[:, :], ALU.pow).then_inc(rs.sem, 1)
            pipeline(pool, T, G, [(0, power)])

        def banks(m):
            return ps[:, 2 * (m % R):2 * (m % R) + 2, :].rearrange("p a n -> p (a n)")

        @block.tensor
        def _(pe):
            pe.wait_ge(loaded.sem, 16 * 3)

            def turn_h(n, m):
                done(pe, h_ready, n)
                done(pe, exped, n - R, 3)
                for k in range(DC):
                    last = nc.tensor.transpose(banks(m)[:, 3 * N + k * P:3 * N + (k + 1) * P], xn[:, m % R, k * P:(k + 1) * P], ident[:, :])
                last.then_inc(h_turned.sem, 1)

            def score(n, m):
                done(pe, h_out, n)
                for s in range(3):
                    for k in range(DC):
                        last = nc.tensor.matmul(banks(m)[:, s * N:(s + 1) * N], hT[:, m % R, k, :], kT[:, s, k, :], start=(k == 0), stop=(k == DC - 1))
                last.then_inc(scored.sem, 1)

            def turn(n, m):
                done(pe, normed, n)
                done(pe, turned_out, n - 1)
                for s in range(3):
                    for c in range(NC):
                        at = (s * NC + c) * P
                        last = nc.tensor.transpose(ps[:, 4 + at // 512, at % 512:at % 512 + P], probs[:, m % R, s, c * P:(c + 1) * P], ident[:, :])
                last.then_inc(turned.sem, 1)

            def slots(s):
                def of_group(g):
                    if s == 0:
                        done(pe, turned_out, (g + 1) * G - 1)
                        if isinstance(g, int) and g == 0:
                            pe.wait_ge(loaded_v.sem, 16 * 3)
                        done(pe, v_out, g - 1)
                    else:
                        done(pe, left_out[s - 1], g)
                    if s < 2:
                        for n in range(DC):
                            for k in range(NC):
                                last = nc.tensor.matmul(ps[:, 6 + n, :], vals[:, s, k, n * P:(n + 1) * P], aT[:, s, k, :], start=(k == 0), stop=(k == NC - 1))
                    else:
                        for j in range(G):
                            for k in range(NC):
                                last = nc.tensor.matmul(ps[:, 6 + j // 2, (j % 2) * D:(j % 2 + 1) * D], aT[:, s, k, j * P:(j + 1) * P], vals[:, s, k, :],
                                                        start=(k == 0), stop=(k == NC - 1))
                    last.then_inc(slotted[s].sem, 1)
                return last_of_group(of_group)
            pipeline(pe, T, G, [(3, slots(0)), (1, score), (3, slots(1)), (0, turn_h), (2, turn), (3, slots(2))], back=4)

        @block.scalar
        def _(act):
            def h_copy(n, m):
                done(act, h_turned, n)
                done(act, scored, n - R)
                nc.scalar.activation(hT[:, m % R, :, :].rearrange("p k q -> p (k q)"), banks(m)[:, 3 * N:4 * N], ACT.Copy, scale=D ** -0.5).then_inc(h_out.sem, 1)

            def exps(n, m):
                done(act, maxed, n)
                done(act, turned, n - R)
                for s in range(3):
                    nc.scalar.activation(probs[:, m % R, s, :], banks(m)[:, s * N:(s + 1) * N], ACT.Exp, bias=nmax[:, m % R, s:s + 1],
                                         accum_out=total[:, m % R, s:s + 1]).then_inc(exped.sem, 1)

            def a_copy(n, m):
                done(act, turned, n)
                if m == 0:
                    done(act, slotted[2], n // G - 1)
                nc.scalar.activation(aT[:, :, :, m * P:(m + 1) * P].rearrange("p s c q -> p (s c) q"),
                                     ps[:, 4:6, :].rearrange("p a n -> p (a n)")[:, 0:3 * N].rearrange("p (c q) -> p c q", q=P), ACT.Copy).then_inc(turned_out.sem, 1)

            def hi(s):
                def of_group(g):
                    done(act, slotted[s], g)
                    done(act, stored[s], g - 1, 16)
                    nc.scalar.activation(part[SETS[s]][:, 0], ps[:, 6:8, :], ACT.Copy).then_inc(hi_out[s].sem, 1)
                return last_of_group(of_group)

            def mid(s):
                def of_group(g):
                    done(act, left_out[s], g)
                    nc.scalar.activation(part[SETS[s]][:, 1], left[:, :, :], ACT.Copy).then_inc(mid_out[s].sem, 1)
                return last_of_group(of_group)
            pipeline(act, T, G, [(3, hi(0)), (1, exps), (3, mid(0)), (3, hi(1)), (0, h_copy), (3, mid(1)), (2, a_copy)], back=4)

        @block.vector
        def _(dve):
            flat = X[:, :, :].rearrange("p t d -> p (t d)")

            def statistics(n, m):
                nc.vector.bn_stats(stats[:, m, :], flat[:, bass.ds(n * D, D)])
                dve.drain()
                nc.vector.bn_aggr(mv[:, m, :], stats[:, m, :])
                dve.drain()
                nc.vector.tensor_scalar(mv[:, m, 1:2], mv[:, m, 1:2], 1e-5, None, ALU.add).then_inc(var.sem, 1)

            def norm_x(n, m):
                done(dve, rs, n)
                done(dve, h_turned, n - R)
                nc.vector.tensor_scalar(xn[:, m % R, :], flat[:, bass.ds(n * D, D)], mv[:, m, 0:1], rstd[:, m:m + 1], ALU.subtract, ALU.mult).then_inc(h_ready.sem, 1)

            def maximum(n, m):
                done(dve, scored, n)
                nc.vector.tensor_reduce(nmax[:, m % R, :], banks(m)[:, 0:3 * N].rearrange("p (s n) -> p s n", s=3), AX.X, ALU.max, negate=True).then_inc(maxed.sem, 1)

            def normalise(n, m):
                done(dve, exped, n, 3)
                nc.vector.reciprocal(total[:, m % R, :], total[:, m % R, :])
                dve.drain()
                nc.vector.tensor_tensor(probs[:, m % R], probs[:, m % R], total[:, m % R, :].unsqueeze(2).broadcast_to((P, 3, N)), ALU.mult).then_inc(normed.sem, 1)

            def rest(s):
                def of_group(g):
                    done(dve, hi_out[s], g)
                    nc.vector.tensor_tensor(left[:, :, :], ps[:, 6:8, :], part[SETS[s]][:, 0], ALU.subtract).then_inc(left_out[s].sem, 1)
                return last_of_group(of_group)

            def low(s):
                def of_group(g):
                    done(dve, mid_out[s], g)
                    nc.vector.tensor_tensor(part[SETS[s]][:, 2], left[:, :, :], part[SETS[s]][:, 1], ALU.subtract).then_inc(lo_out[s].sem, 1)
                    dve.drain()
                return last_of_group(of_group)

            def values(g):
                done(dve, slotted[2], g)
                nc.vector.tensor_copy(v_all[:, :, :].rearrange("p t d -> p (t d)")[:, bass.ds(g * (G * D), G * D)],
                                      ps[:, 6:8, :].rearrange("p a n -> p (a n)")).then_inc(v_out.sem, 1)
            pipeline(dve, T, G, [(5, last_of_group(values)), (3, normalise), (0, statistics), (1, norm_x), (4, rest(0)), (2, maximum),
                                 (4, low(0)), (4, rest(1)), (4, low(1))], back=3)


def causal_attention(nc, ident, ps, scratch, v_all, o_all, spare):
    Q4 = 4
    NU = HB // Q4
    NQ = B * DC * NU
    QPART = (0, 0, 1, 1, 0, 2)
    KPART = (0, 1, 0, 1, 2, 0)
    NR = len(QPART) * DH
    NR3 = NR + 3
    HALF = 512
    PIECES = [(h, t, lo) for h in range(Q4) for t in range(TB) for lo in range(0, (t + 1) * P, HALF)]
    NP = len(PIECES)
    WORKS = []
    for t in range(TB + 1):
        scores = [("score", t, h, S - t * P + HALF // 2) for h in range(Q4)] if t < TB else []
        mixes = [("mix", t - 1, half, 4 * ((half + 1) * HALF - max(half * HALF, (t - 1) * P))) for half in range((t - 1) * P // HALF, 2)] if t else []
        WORKS += scores[0:2] + mixes[0:1] + scores[2:3] + mixes[1:] + scores[3:]
    FROM, TO = 0.05, 0.85

    def reached(sizes):
        return np.cumsum(sizes) / sum(sizes)
    behind = [int(np.sum(reached([min((t + 1) * P - lo, HALF) + P for _, t, lo in PIECES]) <= (at - FROM) / (TO - FROM) + 1e-9))
              for at in reached([work[3] for work in WORKS])]
    with ExitStack() as cx:
        sb = tiles(nc, cx)
        qs = [sb(f"t_qs{u}", [P, Q4, S], BF16) for u in range(NU)]
        ks = [sb(f"t_ks{u}", [P, Q4, S], BF16) for u in range(NU)]
        vq = [sb(f"t_vq{u}", [P, TB, Q4, 32]) for u in range(NU)]
        identb = sb("t_identb", [P, P], BF16)
        causal = sb("t_causal", [P, P], BF16)
        causalT = sb("t_causalT", [P, P], BF16)
        nm = sb("t_nm", [P, Q4, TB])
        nm1 = sb("t_nm1", [P, Q4, TB])
        nmp = sb("t_nmp", [P, 3, Q4, TB], BF16)
        nml = sb("t_nml", [P, Q4, TB])
        nmT = sb("t_nmT", [3 * Q4 * TB, P], BF16)
        pT = spare[:, 0:2 * Q4 * S].rearrange("p (m h q) -> p m h q", m=2, h=Q4)
        oT = sb("t_oT", [P, S])
        inv = sb("t_inv", [P, TB, Q4])

        def sig(name):
            return Signal(cx, nc, "t_" + name)
        consts, stacked, v_ready = sig("consts"), [sig(f"stacked{u}") for u in range(NU)], sig("v_ready")
        scored, maxed = sig("scored"), sig("maxed")
        split, split_turned, split_out, max_stored, lowered = (sig(n) for n in ("split", "split_turned", "split_out", "max_stored", "lowered"))
        tscored, exped, mixed = (sig(n) for n in ("tscored", "exped", "mixed"))
        o_out, o_turned, o_done = sig("o_out"), sig("o_turned"), sig("o_done")
        block = cx.enter_context(nc.Block())

        def past(eng, signal, q, k, per):
            if not isinstance(q, int) or q * per + k > 0:
                eng.wait_ge(signal.sem, q * per + k)

        def quads(eng, quad):
            quad(0, 0, False)
            with eng.Fori(0, (NQ - 2) // 2) as j:
                quad(j * 2 + 1, 1, False)
                quad(j * 2 + 2, 0, False)
            quad(NQ - 1, 1, True)

        def place(q):
            return q // (NU * DC), q // NU % DC

        @block.sync
        def _(sp):
            def load(q, u):
                past(sp, mixed, q - 2, TB, TB)
                b, c = place(q)
                for name, dst, parts in (("q", qs[u], QPART), ("k", ks[u], KPART)):
                    for r, part in enumerate(parts):
                        src = scratch[name][part].rearrange("c (u h d) (b t) -> d u h c b t", u=NU, h=Q4, b=B)
                        sp.dma_start(dst[r * DH:(r + 1) * DH, :, :].unsqueeze(2).unsqueeze(3), src[:, u, :, bass.ds(c, 1), bass.ds(b, 1), :]).then_inc(stacked[u].sem, 16)

            def lower(q, u):
                past(sp, split_out, q, 1, 1)
                past(sp, lowered, q - 1, 16, 16)
                sp.dma_start(scratch["max"].rearrange("s (n q) -> (s n) q", q=P), nmT[:, :]).then_inc(max_stored.sem, 16)
                past(sp, max_stored, q, 16, 16)
                sp.dma_start(qs[u][NR:NR3, :, :].rearrange("s h t -> s (h t)"), scratch["max"]).then_inc(lowered.sem, 16)

            load(0, 0)
            load(1, 1)
            lower(0, 0)

            lower(1, 1)
            load(2, 0)
            with sp.Fori(1, NQ // 2 - 1) as j:
                lower(j * 2, 0)
                load(j * 2 + 1, 1)
                lower(j * 2 + 1, 1)
                load(j * 2 + 2, 0)
            lower(NQ - 2, 0)
            load(NQ - 1, 1)
            lower(NQ - 1, 1)

        @block.gpsimd
        def _(pool):
            pool.memset(identb[:, :], 0.0)
            pool.drain()
            pool.affine_select(out=identb[:, :], in_=identb[:, :], compare_op=ALU.not_equal, fill=1.0, base=0, pattern=[[-1, P]], channel_multiplier=1)
            pool.drain()
            for t, mul, step in ((causal, 1, -1), (causalT, -1, 1)):
                pool.memset(t[:, :], 0.0)
                pool.drain()
                pool.affine_select(out=t[:, :], in_=t[:, :], compare_op=ALU.is_ge, fill=-1.0e30, base=0, pattern=[[step, P]], channel_multiplier=mul)
                pool.drain()
            for u in range(NU):
                pool.memset(ks[u][NR:NR3 + 29, :, :], 1.0)
                pool.drain()
                pool.memset(vq[u][:, :, :, :], 0.0)
                pool.drain()
                pool.memset(vq[u][:, :, :, DH:DH + 1], 1.0)
                pool.drain()
            pool.engine_nop().then_inc(consts.sem, 1)

            def values(q, u):
                past(pool, mixed, q - 2, TB, TB)
                b, c = place(q)
                src = v_all[:, :, :].rearrange("p (b t) (c u h d) -> p b t c u h d", b=B, c=DC, u=NU, h=Q4)
                for h in range(Q4):
                    pool.tensor_copy(vq[u][:, :, h, 0:DH].unsqueeze(1).unsqueeze(3), src[:, bass.ds(b, 1), :, bass.ds(c, 1), u, h, :])
                    pool.drain()
                pool.engine_nop().then_inc(v_ready.sem, 1)

            def quad(q, u, last):
                if not last:
                    values(q + 1, 1 - u)
            values(0, 0)
            quads(pool, quad)

        @block.tensor
        def _(pe):
            pe.wait_ge(consts.sem, 1)

            def piece(q, u, n):
                h, t, lo = PIECES[n]
                w = (t + 1) * P
                hi = min(w, lo + HALF)
                past(pe, maxed, q, n - 1, NP)
                last = nc.tensor.matmul(ps[:, 6 + n % 2, 0:hi - lo], qs[u][0:NR, h, t * P:w], ks[u][0:NR, h, lo:hi], start=True, stop=hi < w)
                if hi == w:
                    last = nc.tensor.matmul(ps[:, 6 + n % 2, t * P - lo:w - lo], identb[:, :], causal[:, :], start=False, stop=True)
                last.then_inc(scored.sem, 1)

            def turn_maxima(q):
                past(pe, split, q, 1, 1)
                nc.tensor.transpose(ps[0:96, 6, :].bitcast(BF16)[:, 0:P], nmp[:, :, :, :].rearrange("p s h t -> p (s h t)"), identb[:, :]).then_inc(split_turned.sem, 1)

            def turn_o(q):
                past(pe, o_out, q, 1, 1)
                for t in range(TB):
                    last = nc.tensor.transpose(ps[:, 6 + t // 4, (t % 4) * P:(t % 4 + 1) * P], oT[:, t * P:(t + 1) * P], ident[:, :])
                last.then_inc(o_turned.sem, 1)

            def score(q, u, t, h):
                past(pe, exped, q, t * Q4 + h - 1, TB * Q4)
                at = t * P
                pair = 2 * (h % 2)
                for m, lo in enumerate(range(at // HALF * HALF, S, HALF)):
                    bank = pair + lo // HALF
                    lo = max(lo, at)
                    hi = (lo // HALF + 1) * HALF
                    nc.tensor.matmul(ps[:, bank, lo % HALF:lo % HALF + hi - lo], ks[u][0:NR3, h, at:at + P], qs[u][0:NR3, h, lo:hi], start=True, stop=m > 0)
                nc.tensor.matmul(ps[:, pair + at // HALF, at % HALF:at % HALF + P], identb[:, :], causalT[:, :], start=False, stop=True).then_inc(tscored.sem, 1)

            def mix(q, u, t, half):
                past(pe, exped, q, (t + 1) * Q4, TB * Q4)
                if t == 0 and half == 0:
                    past(pe, v_ready, q, 1, 1)
                    past(pe, o_out, q - 1, 1, 1)
                lo, hi = max(half * HALF, t * P), (half + 1) * HALF
                for h in range(Q4):
                    last = nc.tensor.matmul(ps[32 * h:32 * h + 32, 4 + half, lo % HALF:lo % HALF + hi - lo], vq[u][:, t, h, :], pT[:, t % 2, h, lo:hi],
                                            start=(t == 0), stop=(t == hi // P - 1))
                if half == 1:
                    last.then_inc(mixed.sem, 1)

            def quad(q, u, last):
                n = 0
                past(pe, lowered, q, 16, 16)
                for k, (kind, t, part, _) in enumerate(WORKS):
                    if kind == "score":
                        score(q, u, t, part)
                    else:
                        mix(q, u, t, part)
                    if k == 1 and not (isinstance(q, int) and q == 0):
                        turn_o(q - 1)
                    if last:
                        continue
                    if n == 0 and behind[k]:
                        past(pe, stacked[1 - u], (q + 1) // NU, 12 * 16, 12 * 16)
                        past(pe, o_done, q - 1, 1, 1)
                    for n in range(n, behind[k]):
                        piece(q + 1, 1 - u, n)
                    if behind[k - 4] < NP <= behind[k - 3]:
                        turn_maxima(q + 1)
                    n = behind[k]

            past(pe, stacked[0], 0, 12 * 16, 12 * 16)
            for n in range(NP):
                piece(0, 0, n)
            turn_maxima(0)
            quads(pe, quad)
            turn_o(NQ - 1)

        @block.scalar
        def _(act):
            def quad(q, u, last):
                for t in range(TB):
                    past(act, mixed, q, t - 1, TB)
                    for h in range(Q4):
                        past(act, tscored, q, t * Q4 + h + 1, TB * Q4)
                        pair = 2 * (h % 2)
                        nc.scalar.activation(pT[:, t % 2, h, t * P:S], ps[:, pair:pair + 2, :].rearrange("p a n -> p (a n)")[:, t * P:S], ACT.Exp,
                                             scale=DH ** -0.5).then_inc(exped.sem, 1)
            quads(act, quad)

        @block.vector
        def _(dve):
            def maxima(q):
                for n, (h, t, lo) in enumerate(PIECES):
                    w = min((t + 1) * P, lo + HALF) - lo
                    dst = nm if lo + w == (t + 1) * P else nm1
                    past(dve, scored, q, n + 1, NP)
                    nc.vector.tensor_reduce(dst[:, h, t:t + 1], ps[:, 6 + n % 2, 0:w], AX.X, ALU.max, negate=True).then_inc(maxed.sem, 1)
                dve.drain()
                more = slice(HALF // P, TB)
                nc.vector.tensor_tensor(nm[:, :, more], nm[:, :, more], nm1[:, :, more], ALU.min)
                dve.drain()
                nc.vector.tensor_copy(nmp[:, 0], nm[:, :, :])
                dve.drain()
                nc.vector.tensor_tensor(nml[:, :, :], nm[:, :, :], nmp[:, 0], ALU.subtract)
                dve.drain()
                nc.vector.tensor_copy(nmp[:, 1], nml[:, :, :])
                dve.drain()
                nc.vector.tensor_tensor(nmp[:, 2], nml[:, :, :], nmp[:, 1], ALU.subtract).then_inc(split.sem, 1)
                past(dve, split_turned, q, 1, 1)
                past(dve, max_stored, q - 1, 16, 16)
                nc.vector.tensor_copy(nmT[:, :], ps[0:96, 6, :].bitcast(BF16)[:, 0:P]).then_inc(split_out.sem, 1)

            def outputs(q, u):
                b, c = place(q)
                past(dve, mixed, q, TB, TB)
                nc.vector.tensor_copy(oT[:, :], ps[:, 4:6, :].rearrange("p a n -> p (a n)")).then_inc(o_out.sem, 1)
                past(dve, o_turned, q, 1, 1)
                turned = ps[:, 6:8, :].rearrange("p a (t h d) -> p (a t) h d", h=Q4, d=32)
                nc.vector.reciprocal(inv[:, :, :].unsqueeze(3), turned[:, :, :, DH:DH + 1])
                dve.drain()
                dst = o_all[:, :, :].rearrange("p (b t) (c u h d) -> p b t c u h d", b=B, c=DC, u=NU, h=Q4)
                for h in range(Q4):
                    last = nc.vector.tensor_tensor(dst[:, bass.ds(b, 1), :, bass.ds(c, 1), u, h, :], turned[:, :, h, 0:DH].unsqueeze(1).unsqueeze(3),
                                                   inv[:, :, h:h + 1].unsqueeze(1).unsqueeze(3).broadcast_to((P, 1, TB, 1, DH)), ALU.mult)
                last.then_inc(o_done.sem, 1)

            def quad(q, u, last):
                if not last:
                    maxima(q + 1)
                outputs(q, u)
            maxima(0)
            quads(dve, quad)


def slot_layers(nc, X, ident, ps, a, o_all, spare):
    NP, NF = 256, 1024
    CP, CF = NP // P, NF // P
    with ExitStack() as cx:
        sb = tiles(nc, cx)
        pK, pV = sb("e_pK", [P, DC, NP]), sb("e_pV", [P, CP, D])
        fK = spare[:, 0:DC * NF].rearrange("p (k n) -> p k n", k=DC)
        fV = spare[:, DC * NF:DC * NF + CF * D].rearrange("p (k n) -> p k n", k=CF)
        half = sb("e_half", [P, G])
        og = sb("e_og", [P, G, D])
        xg = sb("e_xg", [P, G, D])
        oT = sb("e_oT", [P, DC, GT])
        hT = sb("e_hT", [P, DC, GT])
        z = sb("e_z", [P, G, D])
        hz = sb("e_hz", [P, G, D])
        y = sb("e_y", [P, G, D])
        probs = sb("e_probs", [P, 2, NF])
        taken = DC * NF + CF * D
        pT = spare[:, taken:taken + 2 * NF].rearrange("p (m n) -> p m n", m=2)
        nmax, total, inv = sb("e_nmax", [P, 2, G]), sb("e_total", [P, 2, G]), sb("e_inv", [P, 2, G])
        stats, mv, rstd = sb("e_stats", [P, G, 6]), sb("e_mv", [P, G, 2]), sb("e_rstd", [P, G])

        def sig(name, per=1):
            return Signal(cx, nc, "e_" + name, per)
        loaded, var, rs = sig("loaded"), sig("var", 2), sig("rs", 2)
        og_ready, o_turned, oT_out = sig("og_ready"), sig("o_turned"), sig("oT_out")
        h_ready, h_turned, hT_out = sig("h_ready"), sig("h_turned"), sig("hT_out")
        scored, maxed, exped = sig("scored", 2 * G), sig("maxed", 2 * G), sig("exped", 2 * G)
        turned, turned_out, slotted, added = sig("turned", 2 * G), sig("turned_out", 2 * G), sig("slotted", 2 * G), sig("added", 2 * G)
        block = cx.enter_context(nc.Block())

        @block.sync
        def _(sp):
            for dst, name in ((pK, "pK"), (pV, "pV"), (fK, "fK"), (fV, "fV")):
                sp.dma_start(dst[:, :, :], a["L1_attn_" + name].rearrange("(k p) n -> p k n", p=P)).then_inc(loaded.sem, 16)

        @block.gpsimd
        def _(pool):
            pool.memset(half[:, :], -0.5)
            pool.drain()
            with pool.Fori(0, NG) as i:
                for n in range(2):
                    pool.wait_ge(var.sem, var.at(i, n + 1))
                    pool.tensor_tensor(rstd[:, :], mv[:, :, 1], half[:, :], ALU.pow).then_inc(rs.sem, 1)

        def pair(l, j):
            return 2 + j % 2 if l == 0 else 2 * (j % 2)

        @block.tensor
        def _(pe):
            pe.wait_ge(loaded.sem, 16 * 4)
            with pe.Fori(0, NG) as i:
                for l, (ready, done, out, src, dst) in enumerate(((og_ready, o_turned, oT_out, og, oT), (h_ready, h_turned, hT_out, hz, hT))):
                    K, V, C = ((pK, pV, CP), (fK, fV, CF))[l]
                    pe.wait_ge(ready.sem, ready.at(i, 1))
                    for j in range(G):
                        for k in range(DC):
                            last = nc.tensor.transpose(ps[:, k, j * P:(j + 1) * P], src[:, j, k * P:(k + 1) * P], ident[:, :])
                    last.then_inc(done.sem, 1)
                    pe.wait_ge(out.sem, out.at(i, 1))
                    for step in range(G + 2):
                        j = step
                        if j < G:
                            if j >= 2:
                                pe.wait_ge(exped.sem, exped.at(i, l * G + j - 1))
                            for lo in range(0, C * P, 512):
                                w = min(512, C * P)
                                for k in range(DC):
                                    last = nc.tensor.matmul(ps[:, pair(l, j) + lo // 512, 0:w], dst[:, k, j * P:(j + 1) * P], K[:, k, lo:lo + w],
                                                            start=(k == 0), stop=(k == DC - 1))
                            last.then_inc(scored.sem, 1)
                        j = step - 1
                        if 0 <= j < G:
                            n = l * G + j
                            pe.wait_ge(exped.sem, exped.at(i, n + 1))
                            if j >= 1:
                                pe.wait_ge(turned_out.sem, turned_out.at(i, n))
                            for c in range(C):
                                last = nc.tensor.transpose(ps[:, 4 + c // 4, (c % 4) * P:(c % 4 + 1) * P], probs[:, j % 2, c * P:(c + 1) * P], ident[:, :])
                            last.then_inc(turned.sem, 1)
                        j = step - 2
                        if 0 <= j < G:
                            n = l * G + j
                            pe.wait_ge(turned_out.sem, turned_out.at(i, n + 1))
                            if j >= 2:
                                pe.wait_ge(added.sem, added.at(i, n - 1))
                            for c in range(C):
                                last = nc.tensor.matmul(ps[:, 6 + j % 2, 0:D], pT[:, j % 2, c * P:(c + 1) * P], V[:, c, :], start=(c == 0), stop=(c == C - 1))
                            last.then_inc(slotted.sem, 1)

        @block.scalar
        def _(act):
            with act.Fori(0, NG) as i:
                for l in range(2):
                    w = (NP, NF)[l]
                    for step in range(G + 1):
                        j = step
                        if j < G:
                            n = l * G + j
                            act.wait_ge(maxed.sem, maxed.at(i, n + 1))
                            if n >= 2:
                                act.wait_ge(turned.sem, turned.at(i, n - 1))
                            nc.scalar.activation(probs[:, j % 2, 0:w], ps[:, pair(l, j):pair(l, j) + 1 + l, :].rearrange("p a n -> p (a n)")[:, 0:w], ACT.Exp,
                                                 bias=nmax[:, l, j:j + 1], accum_out=total[:, l, j:j + 1]).then_inc(exped.sem, 1)
                        j = step - 1
                        if 0 <= j < G:
                            n = l * G + j
                            act.wait_ge(turned.sem, turned.at(i, n + 1))
                            if n >= 2:
                                act.wait_ge(slotted.sem, slotted.at(i, n - 1))
                            nc.scalar.activation(pT[:, j % 2, 0:w], ps[:, 4:5 + l, :].rearrange("p a n -> p (a n)")[:, 0:w], ACT.Copy).then_inc(turned_out.sem, 1)

        @block.vector
        def _(dve):
            flat = X[:, :, :].rearrange("p t d -> p (t d)")
            oflat = o_all[:, :, :].rearrange("p t d -> p (t d)")
            with dve.Fori(0, NG) as i:
                def norm(n, src, dst):
                    ln_stats(nc.vector, stats, mv, var.sem, src, G, 1e-5)
                    dve.wait_ge(rs.sem, rs.at(i, n + 1))
                    for j in range(G):
                        last = nc.vector.tensor_scalar(dst(j), src[:, j, :], mv[:, j, 0:1], rstd[:, j:j + 1], ALU.subtract, ALU.mult)
                    return last
                nc.vector.tensor_copy(og[:, :, :].rearrange("p g d -> p (g d)"), oflat[:, bass.ds(i * (G * D), G * D)]).then_inc(og_ready.sem, 1)
                nc.vector.tensor_copy(xg[:, :, :].rearrange("p g d -> p (g d)"), flat[:, bass.ds(i * (G * D), G * D)])
                for l, (done, out, dst) in enumerate(((o_turned, oT_out, oT), (h_turned, hT_out, hT))):
                    w = (NP, NF)[l]
                    rest, sums = ((xg, z), (y, y))[l]
                    dve.wait_ge(done.sem, done.at(i, 1))
                    nc.vector.tensor_scalar(dst[:, :, :], ps[:, 0:DC, :], D ** -0.5, None, ALU.mult).then_inc(out.sem, 1)
                    for step in range(G + 2):
                        j = step
                        if j < G:
                            n = l * G + j
                            dve.wait_ge(scored.sem, scored.at(i, n + 1))
                            nc.vector.tensor_reduce(nmax[:, l, j:j + 1], ps[:, pair(l, j):pair(l, j) + 1 + l, :].rearrange("p a n -> p (a n)")[:, 0:w], AX.X, ALU.max,
                                                    negate=True).then_inc(maxed.sem, 1)
                        j = step - 2
                        if 0 <= j < G:
                            n = l * G + j
                            dve.wait_ge(slotted.sem, slotted.at(i, n + 1))
                            nc.vector.reciprocal(inv[:, l, j:j + 1], total[:, l, j:j + 1])
                            dve.drain()
                            nc.vector.scalar_tensor_tensor(out=sums[:, j, :], in0=ps[:, 6 + j % 2, 0:D], scalar=inv[:, l, j:j + 1], in1=rest[:, j, :],
                                                           op0=ALU.mult, op1=ALU.add).then_inc(added.sem, 1)
                    dve.drain()
                    if l == 0:
                        norm(0, z, lambda j: hz[:, j, :]).then_inc(h_ready.sem, 1)
                        nc.vector.tensor_tensor(y[:, :, :], z[:, :, :], xg[:, :, :], ALU.add)
                    else:
                        norm(1, y, lambda j: X[:, bass.ds(i * G + j, 1), :].rearrange("p a d -> p (a d)"))
                dve.drain()


K2 = 2
E8 = 8


def route(nc, X, ident, ps, a, scratch, routing, layer):
    first = layer == 0
    tag = f"r{layer}_"
    lead = 0 if first else T
    NT = routing["tiles"]
    with ExitStack() as cx:
        sb = tiles(nc, cx)
        xn_all = sb(tag + "xn_all", [P, T, D]) if first else X
        rT = sb(tag + "rT", [P, 2, DC, GT])
        norms = sb(tag + "norms", [P, 2, DC])
        rwT = sb(tag + "rwT", [P, DC, E8])
        rb = sb(tag + "rb", [1, E8])
        ones1 = sb(tag + "ones1", [1, P])
        half = sb(tag + "half", [P, T])
        stats, mv, rstd = sb(tag + "stats", [P, T, 6]), sb(tag + "mv", [P, T, 2]), sb(tag + "rstd", [P, T])
        eight = sb(tag + "eight", [P, E8])
        eight_i = sb(tag + "eight_i", [P, E8], I32)
        before = sb(tag + "before", [P, P])
        every = sb(tag + "every", [P, P])
        starts = sb(tag + "starts", [1, NT])
        starts_i = sb(tag + "starts_i", [1, NT], I32)
        zeros = sb(tag + "zeros", [P, D])
        lg = sb(tag + "lg", [P, T, E8])
        lmax, lsum = sb(tag + "lmax", [P, T]), sb(tag + "lsum", [P, T])
        top = sb(tag + "top", [P, T, E8])
        idx = sb(tag + "idx", [P, T, E8], U32)
        idxf = sb(tag + "idxf", [P, T, K2])
        wsum = sb(tag + "wsum", [P, T])
        chosen = sb(tag + "chosen", [P, K2, T, E8])
        both = sb(tag + "both", [P, T, E8])
        rank = sb(tag + "rank", [P, T, E8])
        prior = sb(tag + "prior", [P, T, E8])
        count = sb(tag + "count", [P, T, E8])
        offset = sb(tag + "offset", [P, E8])
        padded = sb(tag + "padded", [P, E8])
        padded_i = sb(tag + "padded_i", [P, E8], I32)
        ended = sb(tag + "ended", [1, E8])
        prod = sb(tag + "prod", [P, T, E8])
        place = sb(tag + "place", [P, T])
        passed = sb(tag + "passed", [1, NT, E8])
        tile_f = sb(tag + "tile_f", [1, NT])
        weights, places, tile_expert = routing["weights"], routing["places"], routing["tile_expert"]

        def sig(name, per=1):
            return Signal(cx, nc, tag + name, per)
        loaded, consts, var, rs = sig("loaded"), sig("consts"), sig("var"), sig("rs")
        x_ready, x_turned, r_out, logits, lexp_in, lexp_out = (sig(n) for n in ("x_ready", "x_turned", "r_out", "logits", "lexp_in", "lexp_out"))
        chosen_all, counted, placed = sig("chosen_all"), sig("counted"), sig("placed")
        cleared, kept = sig("cleared"), sig("kept")
        scattered = Signal(cx, nc, "scattered", sem=routing["by_pool"][0])
        block = cx.enter_context(nc.Block())
        L = "L0_ffn_" if first else "L1_ffn_"

        @block.sync
        def _(sp):
            routing["load_rest"](sp)
            sp.dma_start(rwT[:, :, :], a[L + "router_w"].rearrange("(k p) e -> p k e", p=P)).then_inc(loaded.sem, 16)
            sp.dma_start(rb[:, :], a[L + ("router_b" if first else "routing_bias")].rearrange("(a n) -> a n", a=1)).then_inc(loaded.sem, 16)
            if first:
                sp.dma_start(norms[:, 0, :], a[L + "router_ln_scale"]).then_inc(loaded.sem, 16)
                sp.dma_start(norms[:, 1, :], a[L + "router_ln_bias"]).then_inc(loaded.sem, 16)
                sp.wait_ge(consts.sem, 1)
                for t in range(scratch["tiles"]):
                    sp.dma_start(scratch["rows"][t * P:(t + 1) * P, :], zeros[:, :]).then_inc(cleared.sem, 16)
            else:
                sp.dma_start(scratch["rows"][0:T * P, :].rearrange("(t p) d -> p t d", p=P), X[:, :, :]).then_inc(kept.sem, 16)
                sp.wait_ge(kept.sem, 16)

        @block.gpsimd
        def _(pool):
            pool.memset(half[:, :], -0.5)
            pool.drain()
            pool.memset(ones1[:, :], 1.0)
            pool.drain()
            pool.memset(every[:, :], 1.0)
            pool.drain()
            pool.memset(before[:, :], 1.0)
            pool.drain()
            pool.affine_select(out=before[:, :], in_=before[:, :], compare_op=ALU.is_ge, fill=0.0, base=-1, pattern=[[1, P]], channel_multiplier=-1)
            pool.drain()
            pool.iota(eight_i[:, :], pattern=[[1, E8]], base=0, channel_multiplier=0)
            pool.drain()
            pool.iota(starts_i[:, :], pattern=[[P, NT]], base=0, channel_multiplier=0)
            pool.drain()
            pool.memset(zeros[:, :], 0.0).then_inc(consts.sem, 1)
            if first:
                for g in range(NG):
                    own = slice(g * G, (g + 1) * G)
                    pool.wait_ge(var.sem, g + 1)
                    pool.tensor_tensor(rstd[:, own], mv[:, own, 1], half[:, own], ALU.pow).then_inc(rs.sem, 1)
                pool.wait_ge(cleared.sem, 16 * scratch["tiles"])
            pool.wait_ge(placed.sem, 1)
            for t in range(T):
                for k in range(K2):
                    pool.indirect_dma_start(scratch["rows"], bass.IndirectOffsetOnAxis(ap=places[:, t, k:k + 1], axis=0),
                                            xn_all[:, t, :], None).then_inc(scattered.sem, 16)
            pool.wait_ge(scattered.sem, 16 * T * K2)

        @block.tensor
        def _(pe):
            pe.wait_ge(loaded.sem, 16 * (4 if first else 2))
            pe.wait_ge(consts.sem, 1)
            for g in range(NG + 1):
                if g < NG:
                    if first:
                        pe.wait_ge(x_ready.sem, g + 1)
                    if g >= 2:
                        pe.wait_ge(r_out.sem, g - 1)
                    for j in range(G):
                        for k in range(DC):
                            last = nc.tensor.transpose(ps[:, 2 * (g % 2) + k, j * P:(j + 1) * P], xn_all[:, g * G + j, k * P:(k + 1) * P], ident[:, :])
                    last.then_inc(x_turned.sem, 1)
                if g >= 1:
                    pe.wait_ge(r_out.sem, g)
                    for j in range(G):
                        t = (g - 1) * G + j
                        for k in range(DC):
                            nc.tensor.matmul(ps[:, 4, t * E8:(t + 1) * E8], rT[:, (g - 1) % 2, k, j * P:(j + 1) * P], rwT[:, k, :], start=(k == 0), stop=False)
                        last = nc.tensor.matmul(ps[:, 4, t * E8:(t + 1) * E8], ones1[:, :], rb[:, :], start=False, stop=True)
            last.then_inc(logits.sem, 1)
            pe.wait_ge(chosen_all.sem, 1)
            flat = both[:, :, :].rearrange("p t e -> p (t e)")
            nc.tensor.matmul(ps[:, 5, 0:T * E8], before[:, :], flat, start=True, stop=True)
            nc.tensor.matmul(ps[:, 6, 0:T * E8], every[:, :], flat, start=True, stop=True).then_inc(counted.sem, 1)

        @block.scalar
        def _(act):
            act.wait_ge(loaded.sem, 16 * (4 if first else 2))
            for g in range(NG):
                act.wait_ge(x_turned.sem, g + 1)
                for k in range(DC):
                    src = ps[:, 2 * (g % 2) + k, :]
                    if first:
                        last = nc.scalar.activation(rT[:, g % 2, k, :], src, ACT.Identity, scale=norms[:, 0, k:k + 1], bias=norms[:, 1, k:k + 1])
                    else:
                        last = nc.scalar.activation(rT[:, g % 2, k, :], src, ACT.Copy)
                last.then_inc(r_out.sem, 1)
            act.wait_ge(lexp_in.sem, 1)
            nc.scalar.activation(lg[:, :, :], lg[:, :, :], ACT.Exp, scale=1.0 if first else -1.0).then_inc(lexp_out.sem, 1)

        @block.vector
        def _(dve):
            dve.wait_ge(consts.sem, 1)
            nc.vector.tensor_copy(eight[:, :], eight_i[:, :])
            nc.vector.tensor_copy(starts[:, :], starts_i[:, :])
            if first:
                for g in range(NG):
                    own = range(g * G, (g + 1) * G)
                    for t in own:
                        nc.vector.bn_stats(stats[:, t, :], X[:, t, :])
                    dve.drain()
                    for t in own:
                        nc.vector.bn_aggr(mv[:, t, :], stats[:, t, :])
                    dve.drain()
                    nc.vector.tensor_scalar(mv[:, g * G:(g + 1) * G, 1], mv[:, g * G:(g + 1) * G, 1], 1e-6, None, ALU.add).then_inc(var.sem, 1)
                for g in range(NG):
                    dve.wait_ge(rs.sem, g + 1)
                    for t in range(g * G, (g + 1) * G):
                        last = nc.vector.tensor_scalar(xn_all[:, t, :], X[:, t, :], mv[:, t, 0:1], rstd[:, t:t + 1], ALU.subtract, ALU.mult)
                    last.then_inc(x_ready.sem, 1)
            dve.wait_ge(logits.sem, 1)
            nc.vector.tensor_copy(lg[:, :, :].rearrange("p t e -> p (t e)"), ps[:, 4, 0:T * E8])
            dve.drain()
            if first:
                nc.vector.tensor_reduce(lmax[:, :], lg[:, :, :], AX.X, ALU.max)
                dve.drain()
                nc.vector.tensor_tensor(lg[:, :, :], lg[:, :, :], lmax[:, :].unsqueeze(2).broadcast_to((P, T, E8)), ALU.subtract)
                dve.drain()
            nc.vector.engine_nop().then_inc(lexp_in.sem, 1)
            dve.wait_ge(lexp_out.sem, 1)
            if first:
                nc.vector.tensor_reduce(lsum[:, :], lg[:, :, :], AX.X, ALU.add)
                dve.drain()
                nc.vector.reciprocal(lsum[:, :], lsum[:, :])
                dve.drain()
                nc.vector.tensor_tensor(lg[:, :, :], lg[:, :, :], lsum[:, :].unsqueeze(2).broadcast_to((P, T, E8)), ALU.mult)
            else:
                nc.vector.tensor_scalar(lg[:, :, :], lg[:, :, :], 1.0, None, ALU.add)
                dve.drain()
                nc.vector.reciprocal(lg[:, :, :], lg[:, :, :])
            dve.drain()
            for t in range(T):
                nc.vector.max(top[:, t, :], lg[:, t, :])
            dve.drain()
            for t in range(T):
                nc.vector.max_index(idx[:, t, :], top[:, t, :], lg[:, t, :])
            nc.vector.tensor_tensor(wsum[:, :], top[:, :, 0], top[:, :, 1], ALU.add)
            dve.drain()
            nc.vector.reciprocal(wsum[:, :], wsum[:, :])
            nc.vector.tensor_copy(idxf[:, :, :], idx[:, :, 0:K2])
            dve.drain()
            nc.vector.tensor_tensor(weights[:, :, :], top[:, :, 0:K2], wsum[:, :].unsqueeze(2).broadcast_to((P, T, K2)), ALU.mult)
            for k in range(K2):
                nc.vector.tensor_tensor(chosen[:, k], eight[:, :].unsqueeze(1).broadcast_to((P, T, E8)), idxf[:, :, k:k + 1].broadcast_to((P, T, E8)), ALU.is_equal)
            dve.drain()
            nc.vector.tensor_tensor(both[:, :, :], chosen[:, 0], chosen[:, 1], ALU.add).then_inc(chosen_all.sem, 1)
            dve.wait_ge(counted.sem, 1)
            nc.vector.tensor_copy(rank[:, :, :].rearrange("p t e -> p (t e)"), ps[:, 5, 0:T * E8])
            nc.vector.tensor_copy(count[:, :, :].rearrange("p t e -> p (t e)"), ps[:, 6, 0:T * E8])
            nc.vector.memset(prior[:, 0, :], 0.0)
            dve.drain()
            for t in range(1, T):
                nc.vector.tensor_tensor(prior[:, t, :], prior[:, t - 1, :], count[:, t - 1, :], ALU.add)
                dve.drain()
            nc.vector.tensor_tensor(padded[:, :], prior[:, T - 1, :], count[:, T - 1, :], ALU.add)
            dve.drain()
            nc.vector.tensor_scalar(padded_i[:, :], padded[:, :], float(P - 1), None, ALU.add)
            dve.drain()
            nc.vector.tensor_scalar(padded_i[:, :], padded_i[:, :], -P, None, ALU.bitwise_and)
            dve.drain()
            nc.vector.tensor_copy(padded[:, :], padded_i[:, :])
            nc.vector.memset(offset[:, 0:1], float(lead * P))
            dve.drain()
            for e in range(1, E8):
                nc.vector.tensor_tensor(offset[:, e:e + 1], offset[:, e - 1:e], padded[:, e - 1:e], ALU.add)
                dve.drain()
            nc.vector.tensor_tensor(ended[:, :], offset[0:1, :], padded[0:1, :], ALU.add)
            nc.vector.tensor_tensor(rank[:, :, :], rank[:, :, :], prior[:, :, :], ALU.add)
            dve.drain()
            nc.vector.tensor_tensor(rank[:, :, :], rank[:, :, :], offset[:, :].unsqueeze(1).broadcast_to((P, T, E8)), ALU.add)
            dve.drain()
            for k in range(K2):
                nc.vector.tensor_tensor(prod[:, :, :], rank[:, :, :], chosen[:, k], ALU.mult)
                dve.drain()
                nc.vector.tensor_reduce(place[:, :], prod[:, :, :], AX.X, ALU.add)
                dve.drain()
                nc.vector.tensor_copy(places[:, :, k], place[:, :])
                dve.drain()
            nc.vector.engine_nop().then_inc(placed.sem, 1)
            nc.vector.tensor_tensor(passed[:, :, :], starts[:, :].unsqueeze(2).broadcast_to((1, NT, E8)), ended[:, :].unsqueeze(1).broadcast_to((1, NT, E8)), ALU.is_ge)
            dve.drain()
            nc.vector.tensor_reduce(tile_f[:, :], passed[:, :, :], AX.X, ALU.add)
            dve.drain()
            nc.vector.tensor_scalar(tile_f[:, :], tile_f[:, :], float(E8 - 1), float(0 if first else 1), ALU.min, ALU.add)
            dve.drain()
            if lead:
                nc.vector.memset(tile_f[:, 0:lead], 0.0)
                dve.drain()
            nc.vector.tensor_copy(tile_expert[:, :], tile_f[:, :])


def experts(nc, W, ident, ps, a, scratch, routing, layer):
    first = layer == 0
    tag = f"m{layer}_"
    NT = routing["tiles"]
    NE = E8 if first else E8 + 1
    F = 1024 if first else 512
    FC = F // P
    IN = DC * 1024
    WE = IN + FC * D
    with ExitStack() as cx:
        sb = tiles(nc, cx)
        scale, shift = sb(tag + "scale", [P, NE, DC]), sb(tag + "shift", [P, NE, DC])
        if first:
            b1, b2 = sb(tag + "b1", [P, NE, F]), sb(tag + "b2", [P, NE, D])
        rows = sb(tag + "rows", [P, 2, D])
        rowsT = sb(tag + "rowsT", [P, 2, DC, P])
        hid = sb(tag + "hid", [P, 2, F])
        gate = None if first else sb(tag + "gate", [P, 2, F])
        hidT = sb(tag + "hidT", [P, 2, F])
        out = sb(tag + "out", [P, 2, D])
        tile_expert = routing["tile_expert"]

        def sig(name, per=1):
            return Signal(cx, nc, tag + name, per)
        loaded = sig("loaded")
        fetched = [sig(f"fetched{m}", 16) for m in range(2)]
        turned, rowsT_out, hidden, activated, acted = sig("turned"), sig("rowsT_out"), sig("hidden"), sig("activated"), sig("acted")
        acted_gate = sig("acted_gate")
        hid_turned, hidT_out, expert_done, out_ready = sig("hid_turned"), sig("hidT_out"), sig("expert_done"), sig("out_ready")
        stored = [sig(f"stored{m}", 16) for m in range(2)]
        if not first:
            acted = activated
        block = cx.enter_context(nc.Block())

        def expert_of(eng, n):
            return eng.value_load(tile_expert[0:1, bass.ds(n, 1)], min_val=0, max_val=NE - 1)

        def steps(eng, begin, step):
            begin()
            with eng.Fori(0, NT // 2 - 1) as i:
                step(2 * i, 0, True)
                step(2 * i + 1, 1, True)
            step(NT - 2, 0, False)
            step(NT - 1, 1, False)

        @block.sync
        def _(sp):
            if first:
                sp.dma_start(scale[:, :, :], a["L0_ffn_expert_ln_scale"]).then_inc(loaded.sem, 16)
                sp.dma_start(shift[:, :, :], a["L0_ffn_expert_ln_bias"]).then_inc(loaded.sem, 16)
                sp.dma_start(b1[:, :, :], a["L0_ffn_b1"].unsqueeze(0).broadcast_to((P, NE, F))).then_inc(loaded.sem, 16)
                sp.dma_start(b2[:, :, :], a["L0_ffn_b2"].unsqueeze(0).broadcast_to((P, NE, D))).then_inc(loaded.sem, 16)
            with sp.Fori(0, NT // 2) as i:
                for m in range(2):
                    n = 2 * i + m
                    if m == 0:
                        sp.wait_ge(turned.sem, 2 * i)
                    else:
                        sp.wait_ge(turned.sem, 2 * i)
                    sp.dma_start(rows[:, m, :], scratch["rows"][bass.ds(n * P, P), :]).then_inc(fetched[m].sem, 16)

        @block.tensor
        def _(pe):
            pe.wait_ge(routing["weights_in"], routing["weights_count"])

            def turn(n, m, fresh):
                pe.wait_ge(fetched[m].sem, n * 8 + 16 - m * 8)
                if not fresh:
                    pe.wait_ge(rowsT_out.sem, n)
                for k in range(DC):
                    last = nc.tensor.transpose(ps[:, 0, k * P:(k + 1) * P], rows[:, m, k * P:(k + 1) * P], ident[:, :])
                last.then_inc(turned.sem, 1)

            def enter(n, m, fresh):
                e = expert_of(pe, n)
                pe.wait_ge(rowsT_out.sem, n + 1)
                if not fresh:
                    pe.wait_ge(activated.sem, n - 1)
                for c in range(2):
                    for k in range(DC):
                        last = nc.tensor.matmul(ps[:, 2 + 2 * m + c, :], rowsT[:, m, k, :], W[:, bass.ds(e * WE + k * 1024 + c * 512, 512)],
                                                start=(k == 0), stop=(k == DC - 1))
                last.then_inc(hidden.sem, 1)

            def begin():
                turn(0, 0, True)
                enter(0, 0, True)
                turn(1, 1, False)

            def step(n, m, more, second=False):
                pe.wait_ge(acted.sem, n + 1)
                pe.wait_ge(hidT_out.sem, n)
                for c in range(FC):
                    last = nc.tensor.transpose(ps[:, 6 + c // 4, (c % 4) * P:(c % 4 + 1) * P], hid[:, m, c * P:(c + 1) * P], ident[:, :])
                last.then_inc(hid_turned.sem, 1)
                if more or m == 0:
                    enter(n + 1, 1 - m, False if not isinstance(n, int) or n + 1 > 1 else True)
                if more:
                    turn(n + 2, m, False)
                e = expert_of(pe, n)
                pe.wait_ge(hidT_out.sem, n + 1)
                pe.wait_ge(out_ready.sem, n)
                for c in range(FC):
                    last = nc.tensor.matmul(ps[:, 1, 0:D], hidT[:, m, c * P:(c + 1) * P], W[:, bass.ds(e * WE + IN + c * D, D)],
                                            start=(c == 0), stop=(c == FC - 1))
                last.then_inc(expert_done.sem, 1)
            steps(pe, begin, step)

        @block.scalar
        def _(act):
            def activate(n, m):
                if first:
                    act.wait_ge(activated.sem, n + 1)
                    nc.scalar.activation(hid[:, m, :], hid[:, m, :], ACT.Gelu).then_inc(acted.sem, 1)
                else:
                    act.wait_ge(hidden.sem, n + 1)
                    nc.scalar.activation(gate[:, m, :], ps[:, 2 + 2 * m, :], ACT.Silu).then_inc(acted_gate.sem, 1)

            def step(n, m, more):
                act.wait_ge(hid_turned.sem, n + 1)
                nc.scalar.activation(hidT[:, m, :], ps[:, 6:6 + FC // 4, :].rearrange("p a n -> p (a n)"), ACT.Copy).then_inc(hidT_out.sem, 1)
                if more or m == 0:
                    activate(n + 1, 1 - m)
                act.wait_ge(out_ready.sem, n + 1)
                act.dma_start(scratch["results"][bass.ds(n * P, P), :], out[:, m, :]).then_inc(stored[m].sem, 16)
            steps(act, lambda: activate(0, 0), step)
            for m in range(2):
                act.wait_ge(stored[m].sem, 16 * (NT // 2))

        @block.vector
        def _(dve):
            if first:
                dve.wait_ge(loaded.sem, 64)

            def take(n, m):
                e = expert_of(dve, n) if first else None
                dve.wait_ge(turned.sem, n + 1)
                dve.wait_ge(hidden.sem, n - 1) if not isinstance(n, int) or n >= 2 else None
                if first:
                    for k in range(DC):
                        last = nc.vector.tensor_scalar(rowsT[:, m, k, :], ps[:, 0, k * P:(k + 1) * P],
                                                       scale[:, :, :].rearrange("p e k -> p (e k)")[:, bass.ds(e * DC + k, 1)],
                                                       shift[:, :, :].rearrange("p e k -> p (e k)")[:, bass.ds(e * DC + k, 1)], ALU.mult, ALU.add)
                else:
                    last = nc.vector.tensor_copy(rowsT[:, m, :, :].rearrange("p k q -> p (k q)"), ps[:, 0, 0:D])
                last.then_inc(rowsT_out.sem, 1)

            def activate(n, m):
                if first:
                    e = expert_of(dve, n)
                    dve.wait_ge(hidden.sem, n + 1)
                    if not isinstance(n, int) or n >= 2:
                        dve.wait_ge(hid_turned.sem, n - 1)
                    nc.vector.tensor_tensor(hid[:, m, :], ps[:, 2 + 2 * m:4 + 2 * m, :].rearrange("p a n -> p (a n)"),
                                            b1[:, :, :].rearrange("p e f -> p (e f)")[:, bass.ds(e * F, F)], ALU.add).then_inc(activated.sem, 1)
                else:
                    dve.wait_ge(acted_gate.sem, n + 1)
                    if not isinstance(n, int) or n >= 2:
                        dve.wait_ge(hid_turned.sem, n - 1)
                    nc.vector.tensor_tensor(hid[:, m, :], ps[:, 3 + 2 * m, :], gate[:, m, :], ALU.mult).then_inc(activated.sem, 1)

            def begin():
                take(0, 0)
                activate(0, 0)
                take(1, 1)

            def step(n, m, more):
                if more or m == 0:
                    activate(n + 1, 1 - m)
                if more:
                    take(n + 2, m)
                e = expert_of(dve, n) if first else None
                dve.wait_ge(expert_done.sem, n + 1)
                dve.wait_ge(stored[m].sem, (n - m) * 8)
                if first:
                    nc.vector.tensor_tensor(out[:, m, :], ps[:, 1, 0:D], b2[:, :, :].rearrange("p e f -> p (e f)")[:, bass.ds(e * D, D)], ALU.add).then_inc(out_ready.sem, 1)
                else:
                    nc.vector.tensor_copy(out[:, m, :], ps[:, 1, 0:D]).then_inc(out_ready.sem, 1)
            steps(dve, begin, step)


def combine(nc, X, scratch, routing, layer, result=None):
    first = layer == 0
    tag = f"c{layer}_"
    NBUF = 8
    with ExitStack() as cx:
        sb = tiles(nc, cx)
        got = sb(tag + "got", [P, NBUF, K2, D])
        common = None if first else sb(tag + "common", [P, T, D])
        y = sb(tag + "y", [P, T, D])
        half = sb(tag + "half", [P, G])
        stats, mv, rstd = sb(tag + "stats", [P, G, 6]), sb(tag + "mv", [P, G, 2]), sb(tag + "rstd", [P, G])
        weights, places = routing["weights"], routing["places"]

        def sig(name, per=1):
            return Signal(cx, nc, tag + name, per)
        shared, added, var, rs, normed, stored = (sig(n) for n in ("shared", "added", "var", "rs", "normed", "stored"))
        fetched = [Signal(cx, nc, "fetched", sem=routing["by_pool"][1 + m]) for m in range(NBUF)]
        block = cx.enter_context(nc.Block())

        @block.sync
        def _(sp):
            if not first:
                sp.dma_start(common[:, :, :], scratch["results"][0:T * P, :].rearrange("(t p) d -> p t d", p=P)).then_inc(shared.sem, 16)
            if result is not None:
                for g in range(NG):
                    sp.wait_ge(normed.sem, g + 1)
                    sp.dma_start(result.rearrange("b (t p) d -> p (b t) d", p=P)[:, g * G:(g + 1) * G, :], X[:, g * G:(g + 1) * G, :]).then_inc(stored.sem, 16)
                sp.wait_ge(stored.sem, 16 * NG)

        @block.gpsimd
        def _(pool):
            pool.memset(half[:, :], -0.5)
            pool.drain()

            def power(g):
                pool.wait_ge(var.sem, g + 1)
                pool.tensor_tensor(rstd[:, :], mv[:, :, 1], half[:, :], ALU.pow).then_inc(rs.sem, 1)
            for t in range(T):
                if t >= NBUF:
                    pool.wait_ge(added.sem, t - NBUF + 1)
                for k in range(K2):
                    pool.indirect_dma_start(got[:, t % NBUF, k, :], None, scratch["results"][0:routing["tiles"] * P, :],
                                            bass.IndirectOffsetOnAxis(ap=places[:, t, k:k + 1], axis=0)).then_inc(fetched[t % NBUF].sem, 16)
                if t % G == G - 1 and t >= G:
                    power(t // G - 1)
            power(NG - 1)

        @block.vector
        def _(dve):
            if not first:
                dve.wait_ge(shared.sem, 16)
                nc.vector.tensor_tensor(X[:, :, :], X[:, :, :], common[:, :, :], ALU.add)
                dve.drain()
            for g in range(NG):
                for j in range(G):
                    t = g * G + j
                    dve.wait_ge(fetched[t % NBUF].sem, 32 * (t // NBUF + 1))
                    nc.vector.scalar_tensor_tensor(out=y[:, t, :], in0=got[:, t % NBUF, 0, :], scalar=weights[:, t, 0:1], in1=X[:, t, :], op0=ALU.mult, op1=ALU.add)
                    dve.drain()
                    nc.vector.scalar_tensor_tensor(out=y[:, t, :], in0=got[:, t % NBUF, 1, :], scalar=weights[:, t, 1:2], in1=y[:, t, :], op0=ALU.mult, op1=ALU.add).then_inc(added.sem, 1)
                dve.drain()
                ln_stats(nc.vector, stats, mv, var.sem, y[:, g * G:(g + 1) * G, :], G, 1e-5)
                dve.wait_ge(rs.sem, g + 1)
                for j in range(G):
                    t = g * G + j
                    last = nc.vector.tensor_scalar(X[:, t, :], y[:, t, :], mv[:, j, 0:1], rstd[:, j:j + 1], ALU.subtract, ALU.mult)
                last.then_inc(normed.sem, 1)
                dve.drain()


def decoder(nc, a, out):
    with ExitStack() as cx:
        X = cx.enter_context(nc.sbuf_tensor("X", [P, T, D], F32))
        ident = cx.enter_context(nc.sbuf_tensor("ident", [P, P], F32))
        ps = cx.enter_context(nc.psum_tensor("ps", [P, 8, 512], F32))
        EARLY, WORDS = 24 * 1024, 32 * 1024
        W = cx.enter_context(nc.sbuf_tensor("experts_w", [P, WORDS], F32))
        spare = W[:, EARLY:WORDS]
        weights = cx.enter_context(nc.sbuf_tensor("weights", [P, T, K2], F32))
        places = cx.enter_context(nc.sbuf_tensor("places", [P, T, K2], U32))
        tile_expert = cx.enter_context(nc.sbuf_tensor("tile_expert", [1, 64], I32))
        QT = T * K2 + E8
        scratch = {
            "tiles": T + QT,
            "rows": nc.dram_tensor("queue_rows", ((T + QT) * P, D), F32).ap(),
            "results": nc.dram_tensor("queue_results", ((T + QT) * P, D), F32).ap(),
            "q": nc.dram_tensor("q_parts", (3, DC, P, B * S), BF16).ap(),
            "k": nc.dram_tensor("k_parts", (3, DC, P, B * S), BF16).ap(),
            "max": nc.dram_tensor("max_parts", (3, 4 * S), BF16).ap(),
        }
        x_loaded = cx.enter_context(nc.semaphore("x_loaded"))
        weights_in = [cx.enter_context(nc.semaphore(f"weights_in{n}")) for n in range(2)]

        by_pool = [[cx.enter_context(nc.semaphore(f"by_pool{layer}_{n}")) for n in range(9)] for layer in range(2)]

        def routing(layer):
            words = a[f"w_L{layer}"].shape[2]
            experts_in = a[f"w_L{layer}"].shape[1]
            whole = EARLY // words

            def load(sp, which):
                for e in which:
                    sp.dma_start(W[:, e * words:(e + 1) * words], a[f"w_L{layer}"][:, e, :]).then_inc(weights_in[layer], 16)
            return {"by_pool": by_pool[layer], "weights": weights, "places": places, "tiles": QT + (T if layer else 0),
                    "tile_expert": tile_expert[:, 0:QT + (T if layer else 0)],
                    "weights_in": weights_in[layer], "weights_count": 16 * experts_in,
                    "load_early": lambda sp: load(sp, range(whole)), "load_rest": lambda sp: load(sp, range(whole, experts_in))}
        route0, route1 = routing(0), routing(1)

        with nc.Block() as block:
            @block.sync
            def _(sp):
                sp.dma_start(X[:, :, :], a["x"].rearrange("b (t p) d -> p (b t) d", p=P)).then_inc(x_loaded, 16)

            @block.gpsimd
            def _(pool):
                pool.memset(ident[:, :], 0.0)
                pool.drain()
                pool.affine_select(out=ident[:, :], in_=ident[:, :], compare_op=ALU.not_equal, fill=1.0,
                                   base=0, pattern=[[-1, P]], channel_multiplier=1)
        window_attention(nc, X, ident, ps, a, spare, x_loaded, route0["load_early"])
        nc.all_engine_barrier()
        cross_attention(nc, X, ident, ps, a, spare, 0)
        nc.all_engine_barrier()
        route(nc, X, ident, ps, a, scratch, route0, 0)
        nc.all_engine_barrier()
        experts(nc, W, ident, ps, a, scratch, route0, 0)
        nc.all_engine_barrier()
        combine(nc, X, scratch, route0, 0)
        nc.all_engine_barrier()
        with nc.sbuf_tensor("v_all", [P, T, D], F32) as v_all:
            slot_projections(nc, X, ident, ps, a, scratch, v_all, spare, route1["load_early"])
            nc.all_engine_barrier()
            causal_attention(nc, ident, ps, scratch, v_all, v_all, spare)
            nc.all_engine_barrier()
            slot_layers(nc, X, ident, ps, a, v_all, spare)
            nc.all_engine_barrier()
        cross_attention(nc, X, ident, ps, a, spare, 1)
        nc.all_engine_barrier()
        route(nc, X, ident, ps, a, scratch, route1, 1)
        nc.all_engine_barrier()
        experts(nc, W, ident, ps, a, scratch, route1, 1)
        nc.all_engine_barrier()
        combine(nc, X, scratch, route1, 1, result=out)
        nc.all_engine_barrier()


def features(v):
    return np.ascontiguousarray(np.moveaxis(v.reshape(v.shape[:-1] + (DC, P)), -1, 0))


def chunks(w):
    e, r, n = w.shape
    return w.reshape(e, r // P, P, n).transpose(2, 0, 1, 3).reshape(P, e, -1)


def kernel(**inputs):
    import concourse.bacc as bacc
    from concourse.bass_utils import run_bass_kernel_spmd

    z = {k: np.asarray(v) for k, v in inputs.items()}
    arrays = {k: v for k, v in z.items() if not k.startswith(("L0_ffn_w", "L1_ffn_shared", "L1_ffn_gate", "L1_ffn_up", "L1_ffn_down"))}
    arrays["xT"] = np.ascontiguousarray(z["x"].reshape(B * S, D).T)
    for n in ("L0_xattn_bq", "L0_xattn_bk", "L1_xattn_bq", "L1_xattn_bk", "L1_xattn_norm_w", "L1_xattn_norm_b",
              "L1_xattn_norm1_w", "L1_xattn_norm1_b", "L0_ffn_router_ln_scale", "L0_ffn_router_ln_bias",
              "L0_ffn_expert_ln_scale", "L0_ffn_expert_ln_bias"):
        arrays[n] = features(z[n])
    for n in ("L0_ffn_router_w", "L1_ffn_router_w", "L1_attn_qK", "L1_attn_kK", "L1_attn_vK", "L1_attn_pK", "L1_attn_fK"):
        arrays[n] = np.ascontiguousarray(z[n].T)
    arrays["w_L0"] = np.ascontiguousarray(np.concatenate(
        [chunks(z["L0_ffn_w1"].transpose(0, 2, 1)), chunks(z["L0_ffn_w2"].transpose(0, 2, 1))], 2))
    gate, up, down = (np.concatenate([z["L1_ffn_shared_" + n].T[None], z[f"L1_ffn_{n}_w"]]) for n in ("gate", "up", "down"))
    arrays["w_L1"] = np.ascontiguousarray(np.concatenate([chunks(np.concatenate([gate, up], 2)), chunks(down)], 2))

    nc = bacc.Bacc("TRN2", target_bir_lowering=False, num_devices=1)
    feeds, a = {}, {}
    for n, v in arrays.items():
        v = np.ascontiguousarray(v)
        feeds[f"in_{n}"] = v
        a[n] = nc.dram_tensor(f"in_{n}", v.shape, mybir.dt.from_np(v.dtype), kind="ExternalInput").ap()
    out = nc.dram_tensor("out", (B, S, D), F32, kind="ExternalOutput").ap()
    decoder(nc, a, out)
    r = run_bass_kernel_spmd(nc, [feeds], core_ids=[0])
    return r.results[0]["out"]
```

```python
import concourse.bass as bass
import numpy as np
from concourse import mybir
from contextlib import ExitStack

F32 = mybir.dt.float32
BF16 = mybir.dt.bfloat16
I32 = mybir.dt.int32
U32 = mybir.dt.uint32
ACT = mybir.ActivationFunctionType
ALU = mybir.AluOpType
AX = mybir.AxisListType

P = 128
B, S, D = 2, 1024, 256
T = B * S // P
TB = S // P
DC = D // P
G = 4
GT = G * P
NG = T // G
GB = TB // G
H, DH = 16, 16
HB = P // DH
S2 = 77
WIN = 64
NEG = -1.0e9


class Signal:

    def __init__(self, cx, nc, name, per=1, sem=None):
        self.sem = sem if sem is not None else cx.enter_context(nc.semaphore(name))
        if sem is None:
            cx.callback(nc.sync.sem_clear, self.sem)
        self.per = per

    def at(self, i, n):
        return i * self.per + n


def tiles(nc, cx):
    def sb(name, shape, dt=F32):
        return cx.enter_context(nc.sbuf_tensor(name, shape, dt))
    return sb


def ln_stats(dve, stats, mv, sem_var, src, n, eps):
    for j in range(n):
        dve.bn_stats(stats[:, j, :], src[:, j, :])
    dve.drain()
    for j in range(n):
        dve.bn_aggr(mv[:, j, :], stats[:, j, :])
    dve.drain()
    dve.tensor_scalar(mv[:, 0:n, 1], mv[:, 0:n, 1], eps, None, ALU.add).then_inc(sem_var, 1)


def pipeline(eng, total, unroll, jobs, back=0):
    lags = [lag for lag, _ in jobs]

    def step(s, at):
        for lag, job in jobs:
            if not isinstance(s, int) or 0 <= s - lag < total:
                job(s - lag, (at - lag) % unroll)
    head = max(lags) + back
    head += (total - head) % unroll
    for s in range(min(head, total)):
        step(s, s)
    if head < total:
        with eng.Fori(0, (total - head) // unroll) as i:
            for r in range(unroll):
                step(i * unroll + (head + r), head + r)
    for s in range(total, total + max(lags)):
        step(s, s)


def done(eng, signal, n, per=1, part=0):
    if not isinstance(n, int) or n >= 0:
        eng.wait_ge(signal.sem, n * per + (per - part))


def window_attention(nc, X, ident, ps, a, spare, x_loaded, prefetch):
    KW = 2 * P
    PADDED = S + 2 * WIN
    with ExitStack() as cx:
        sb = tiles(nc, cx)
        xT = sb("a_xT", [P, DC, B * PADDED])
        xs = spare[:, 0:B * (TB + 1) * D].rearrange("p (b t d) -> p b t d", b=B, t=TB + 1)
        w = sb("a_w", [P, DC, D])
        band = sb("a_band", [P, KW])
        pad = sb("a_pad", [1, B * PADDED])
        ones = sb("a_ones", [1, P])
        xwT = sb("a_xwT", [P, DC, GT])
        probs = sb("a_probs", [P, 2, KW])
        probsT = sb("a_probsT", [P, 2, 2, P])
        nmax = sb("a_nmax", [P, G])
        total = sb("a_total", [P, G])
        inv = sb("a_inv", [P, G])
        ra = sb("a_ra", [P, G, D])
        y = sb("a_y", [P, G, D])
        stats = sb("a_stats", [P, G, 6])
        mv = sb("a_mv", [P, G, 2])
        rstd = sb("a_rstd", [P, G])
        half = sb("a_half", [P, G])

        def sig(name, per=1):
            return Signal(cx, nc, "a_" + name, per)
        rows_loaded = sig("rows_loaded")
        loaded, masks = sig("loaded"), sig("masks")
        xw_done, xw_out = sig("xw_done"), sig("xw_out")
        scored, maxed, exped = sig("scored", G), sig("maxed", G), sig("exped", G)
        turned, turned_out = sig("turned", G), sig("turned_out", G)
        mixed, relued, inved = sig("mixed", G), sig("relued", G), sig("inved", G)
        var, rs = sig("var"), sig("rs")
        group_free = sig("group_free")
        block = cx.enter_context(nc.Block())

        @block.sync
        def _(sp):
            sp.dma_start(w[:, :, :], a["L0_attn_W"].rearrange("(k p) n -> p k n", p=P)).then_inc(loaded.sem, 16)
            for b in range(B):
                sp.dma_start(xT[:, :, b * PADDED + WIN:b * PADDED + WIN + S],
                             a["xT"][:, b * S:(b + 1) * S].rearrange("(k p) t -> p k t", p=P)).then_inc(loaded.sem, 16)
            for b in range(B):
                sp.dma_start(xs[WIN:P, b, 0:TB, :], a["x"][b, :, :].rearrange("(t p) d -> p t d", p=P)[0:WIN]).then_inc(rows_loaded.sem, 16)
                sp.dma_start(xs[0:WIN, b, 1:TB + 1, :], a["x"][b, :, :].rearrange("(t p) d -> p t d", p=P)[WIN:P]).then_inc(rows_loaded.sem, 16)
            sp.dma_start(X[:, :, :], a["x"].rearrange("b (t p) d -> p (b t) d", p=P)).then_inc(x_loaded, 16)
            prefetch(sp)

        @block.gpsimd
        def _(pool):
            for b in range(B):
                for at in (b * PADDED, (b + 1) * PADDED - WIN):
                    pool.memset(xT[:, :, at:at + WIN], 0.0)
                    pool.drain()
                pool.memset(xs[0:WIN, b, 0, :], 0.0)
                pool.drain()
                pool.memset(xs[WIN:P, b, TB, :], 0.0)
                pool.drain()
            pool.memset(half[:, :], -0.5)
            pool.drain()
            pool.memset(pad[:, :], NEG)
            pool.drain()
            pool.memset(band[:, :], 0.0)
            pool.drain()
            pool.memset(ones[:, :], 1.0)
            for b in range(B):
                pool.drain()
                pool.memset(pad[:, b * PADDED + WIN:b * PADDED + WIN + S], 0.0)
            pool.drain()
            pool.affine_select(out=band[:, :], in_=band[:, :], compare_op=ALU.is_ge, fill=NEG,
                               base=0, pattern=[[1, KW]], channel_multiplier=-1)
            pool.drain()
            pool.affine_select(out=band[:, :], in_=band[:, :], compare_op=ALU.is_ge, fill=NEG,
                               base=2 * WIN, pattern=[[-1, KW]], channel_multiplier=1).then_inc(masks.sem, 1)
            pool.drain()
            with pool.Fori(0, NG) as i:
                pool.wait_ge(var.sem, var.at(i, 1))
                pool.tensor_tensor(rstd[:, :], mv[:, :, 1], half[:, :], ALU.pow).then_inc(rs.sem, 1)

        @block.tensor
        def _(pe):
            pe.wait_ge(loaded.sem, 16 * (1 + B))
            pe.wait_ge(masks.sem, 1)

            def project(i, at):
                for n in range(DC):
                    for k in range(DC):
                        last = nc.tensor.matmul(ps[:, n, :], w[:, k, n * P:(n + 1) * P], xT[:, k, bass.ds(at + WIN, GT)],
                                                start=(k == 0), stop=(k == DC - 1))
                last.then_inc(xw_done.sem, 1)

            def score(i, at, j):
                if j >= 2:
                    pe.wait_ge(exped.sem, exped.at(i, j - 1))
                out = ps[:, 2 + j % 2, 0:KW]
                for k in range(DC):
                    nc.tensor.matmul(out, xwT[:, k, j * P:(j + 1) * P], xT[:, k, bass.ds(at + j * P, KW)],
                                     start=(k == 0), stop=False)
                nc.tensor.matmul(out, ident[:, :], band[:, :], start=False, stop=False)
                nc.tensor.matmul(out, ones[:, :], pad[:, bass.ds(at + j * P, KW)],
                                 start=False, stop=True).then_inc(scored.sem, 1)

            def turn(i, j):
                pe.wait_ge(exped.sem, exped.at(i, j + 1))
                if j >= 2:
                    pe.wait_ge(turned_out.sem, turned_out.at(i, j - 1))
                for c in range(2):
                    last = nc.tensor.transpose(ps[:, 4 + j % 2, c * P:(c + 1) * P], probs[:, j % 2, c * P:(c + 1) * P], ident[:, :])
                last.then_inc(turned.sem, 1)

            def mix(i, b, h, j):
                pe.wait_ge(turned_out.sem, turned_out.at(i, j + 1))
                if j >= 2:
                    pe.wait_ge(relued.sem, relued.at(i, j - 1))
                elif j == 0:
                    pe.wait_ge(rows_loaded.sem, 16 * 2 * B)
                for c in range(2):
                    row = (b * (TB + 1) + h * G + (j + c)) * D
                    last = nc.tensor.matmul(ps[:, 6 + j % 2, 0:D], probsT[:, j % 2, c, :],
                                            spare[:, bass.ds(row, D)],
                                            start=(c == 0), stop=(c == 1))
                last.then_inc(mixed.sem, 1)

            with pe.Fori(0, B) as b:
                with pe.Fori(0, GB) as h:
                    i = b * GB + h
                    at = b * PADDED + h * GT
                    pe.wait_ge(group_free.sem, i + 1)
                    project(i, at)
                    pe.wait_ge(xw_out.sem, xw_out.at(i, 1))
                    for step in range(G + 2):
                        if step < G:
                            score(i, at, step)
                        if 0 <= step - 1 < G:
                            turn(i, step - 1)
                        if 0 <= step - 2 < G:
                            mix(i, b, h, step - 2)

        @block.scalar
        def _(act):
            with act.Fori(0, NG) as i:
                act.wait_ge(xw_done.sem, xw_done.at(i, 1))
                nc.scalar.activation(xwT[:, :, :], ps[:, 0:DC, :], ACT.Copy).then_inc(xw_out.sem, 1)
                for step in range(G + 2):
                    j = step
                    if j < G:
                        act.wait_ge(maxed.sem, maxed.at(i, j + 1))
                        if j >= 2:
                            act.wait_ge(turned.sem, turned.at(i, j - 1))
                        nc.scalar.activation(probs[:, j % 2, :], ps[:, 2 + j % 2, 0:KW], ACT.Exp, bias=nmax[:, j:j + 1],
                                             accum_out=total[:, j:j + 1]).then_inc(exped.sem, 1)
                    j = step - 2
                    if 0 <= j < G:
                        act.wait_ge(mixed.sem, mixed.at(i, j + 1))
                        act.wait_ge(inved.sem, inved.at(i, j + 1))
                        if j == 0:
                            act.wait_ge(group_free.sem, i + 1)
                        nc.scalar.activation(ra[:, j, :], ps[:, 6 + j % 2, 0:D], ACT.Relu,
                                             scale=inv[:, j:j + 1]).then_inc(relued.sem, 1)

        @block.vector
        def _(dve):
            nc.vector.engine_nop().then_inc(group_free.sem, 1)
            with dve.Fori(0, NG) as i:
                for step in range(G + 1):
                    j = step
                    if j < G:
                        dve.wait_ge(scored.sem, scored.at(i, j + 1))
                        nc.vector.tensor_reduce(nmax[:, j:j + 1], ps[:, 2 + j % 2, 0:KW], AX.X, ALU.max,
                                                negate=True).then_inc(maxed.sem, 1)
                    j = step - 1
                    if 0 <= j < G:
                        dve.wait_ge(turned.sem, turned.at(i, j + 1))
                        if j >= 2:
                            dve.wait_ge(mixed.sem, mixed.at(i, j - 1))
                        nc.vector.tensor_copy(probsT[:, j % 2, :, :].rearrange("p c q -> p (c q)"),
                                              ps[:, 4 + j % 2, 0:KW]).then_inc(turned_out.sem, 1)
                        nc.vector.reciprocal(inv[:, j:j + 1], total[:, j:j + 1]).then_inc(inved.sem, 1)
                dve.wait_ge(relued.sem, relued.at(i, G))
                dve.wait_ge(x_loaded, 16)
                nc.vector.scalar_tensor_tensor(out=y[:, :, :].rearrange("p g d -> p (g d)"),
                                               in0=X[:, :, :].rearrange("p t d -> p (t d)")[:, bass.ds(i * (G * D), G * D)], scalar=2.0,
                                               in1=ra[:, :, :].rearrange("p g d -> p (g d)"), op0=ALU.mult, op1=ALU.add).then_inc(group_free.sem, 1)
                dve.drain()
                ln_stats(nc.vector, stats, mv, var.sem, y, G, 1e-5)
                dve.wait_ge(rs.sem, rs.at(i, 1))
                for j in range(G):
                    nc.vector.tensor_scalar(X[:, bass.ds(i * G + j, 1), :].rearrange("p a d -> p (a d)"), y[:, j, :],
                                            mv[:, j, 0:1], rstd[:, j:j + 1], ALU.subtract, ALU.mult)
                dve.drain()


def cross_attention(nc, X, ident, ps, a, spare, layer):
    first = layer == 0
    HH = H // 2
    BH = 4
    NM = 4
    SP = 80
    CH = HH * SP // P
    NCH = 2 * CH
    TURNS = [(0, 4), (4, 8), (8, NCH)]
    with ExitStack() as cx:
        tag = f"x{layer}_"
        sb = tiles(nc, cx)
        names = ["Wq", "Wk", "Wv", "Wo"]
        wt = {n: sb(tag + n, [P, DC, D]) for n in names}
        bqk = sb(tag + "bqk", [P, 2, DC])
        bv = sb(tag + "bv", [1, D])
        bo = sb(tag + "bo", [P, D])
        norms = sb(tag + "norms", [P, 4, DC])
        ones = sb(tag + "ones", [1, P])
        own = sb(tag + "own", [P, HB])
        half = sb(tag + "half", [P, T])
        if first:
            mask = sb(tag + "mask", [P, TB, S2])
            less = sb(tag + "less", [P, TB, S2])
        ctx = sb(tag + "ctx", [S2, B, D])
        ctxT = sb(tag + "ctxT", [P, DC, S2])
        kT = sb(tag + "kT", [P, DC, S2])
        keys = sb(tag + "keys", [P, B, DC, HB, S2])
        vals = sb(tag + "vals", [S2, D])
        vblk = spare[:, 2 * T * D:2 * T * D + B * NCH * P].rearrange("p (b v c n) -> p b v c n", b=B, v=2, c=CH)
        place = sb(tag + "place", [S2, 3 * SP])
        owner = sb(tag + "owner", [P, CH, HH])
        qT_all = spare[:, 0:T * D].rearrange("p (t k q) -> p t k q", t=T, k=DC)
        o_all = spare[:, T * D:2 * T * D].rearrange("p (t d) -> p t d", t=T)
        xg = o_all[:, 0:2 * G, :].rearrange("p (m g) d -> p m g d", m=2)
        xTg = o_all[:, 2 * G:4 * G, :].rearrange("p (m k j) (w q) -> p m k (j w q)", m=2, k=DC, w=2)
        work = sb(tag + "work", [P, NCH * P])
        xn = work[:, 0:2 * D].rearrange("p (m d) -> p m d", m=2)
        xT = work[:, 2 * D:4 * D].rearrange("p (m k q) -> p m k q", m=2, k=DC)
        pT = work[:, :].rearrange("p (c q) -> p c q", c=NCH)
        qT = sb(tag + "qT", [P, NM, DC, P])
        att = sb(tag + "att", [P, NM, H, SP])
        top = sb(tag + "top", [P, NM, H])
        total = sb(tag + "total", [P, NM, H])
        o = spare[:, 0:T * D].rearrange("p (t d) -> p t d", t=T)
        if not first:
            stats = sb(tag + "stats", [P, T, 6])
            mv, rstd = sb(tag + "mv", [P, T, 2]), sb(tag + "rstd", [P, T])
            cmv, crstd = sb(tag + "cmv", [P, B, 2]), sb(tag + "crstd", [P, B])
        ystats, ymv, yrstd = sb(tag + "ystats", [P, NM, 6]), sb(tag + "ymv", [P, NM, 2]), sb(tag + "yrstd", [P, NM])
        y = att[:, :, :, :].rearrange("p m h s -> p m (h s)")[:, :, 0:D]

        def sig(name, per=1):
            return Signal(cx, nc, tag + name, per)
        loaded_q, loaded_kv, loaded_o, consts = sig("loaded_q"), sig("loaded_kv"), sig("loaded_o"), sig("consts")
        ctx_ready, bo_in, bq_scaled, y_var, y_rs = sig("ctx_ready"), sig("bo_in"), sig("bq_scaled"), sig("y_var"), sig("y_rs")
        kv_mm, kv_out = sig("kv_mm"), sig("kv_out")
        var, rs = sig("var"), sig("rs")
        x_ready, x_turned, x_out, q_done, q_out = (sig(n) for n in ("x_ready", "x_turned", "x_out", "q_done", "q_out"))
        qT_ready, scored, scored_out, topped, lowered, exped, summed = (
            sig(n) for n in ("qT_ready", "scored", "scored_out", "topped", "lowered", "exped", "summed"))
        turned, turned_out, mixed, o_out = (sig(n) for n in ("turned", "turned_out", "mixed", "o_out"))
        grouped = sig("grouped")
        n_ready, n_turned, n_out, wo_done, y_out = (sig(n) for n in ("n_ready", "n_turned", "n_out", "wo_done", "y_out"))
        block = cx.enter_context(nc.Block())
        L = "L0_xattn_" if first else "L1_xattn_"
        NQ, NKV, NO = 2 if first else 6, 6 if first else 5, 2

        def regroup(eng, copy, b, which):
            M = P // 4
            for r in which:
                h, uu = divmod(r, 4)
                for e in range(2):
                    at = (P // 2) * e + M * h
                    tiles_o = o_all[uu * M:(uu + 1) * M, (b * GB + h) * G:(b * GB + h + 1) * G, :]
                    last = copy(o[at:at + M, b * TB:(b + 1) * TB, :].rearrange("p c (j u d) -> p u c j d", u=4, d=DH)[:, uu],
                         tiles_o.rearrange("p j (c e d) -> p e c j d", e=2, d=DH)[:, e])
            last.then_inc(grouped.sem, 1)

        @block.sync
        def _(sp):
            def load(dst, src, signal):
                sp.dma_start(dst, src).then_inc(signal.sem, 16)

            def weight(n, signal):
                load(wt[n][:, :, :], a[L + n].rearrange("(k p) n -> p k n", p=P), signal)
            if not first:
                for n, name in enumerate(("norm_w", "norm_b", "norm1_w", "norm1_b")):
                    load(norms[:, n, :], a[L + name], loaded_q)
            load(bqk[:, 0, :], a[L + "bq"], loaded_q)
            weight("Wq", loaded_q)
            load(ctx[:, :, :], a["ctx_1024"].rearrange("b s d -> s b d"), loaded_kv)
            weight("Wk", loaded_kv)
            load(bqk[:, 1, :], a[L + "bk"], loaded_kv)
            weight("Wv", loaded_kv)
            load(bv[:, :], a[L + "bv"].rearrange("(a n) -> a n", a=1), loaded_kv)
            if first:
                load(mask[:, :, :], a["mask_1x1xSxS2_fk0"].rearrange("a c (t p) s -> p (a c t) s", p=P), loaded_kv)
            weight("Wo", loaded_o)
            load(bo[:, :], a[L + "bo"].rearrange("(a n) -> a n", a=1).broadcast_to((P, D)), loaded_o)

        @block.gpsimd
        def _(pool):
            pool.memset(half[:, :], -0.5)
            pool.drain()
            pool.memset(ones[:, :], 1.0)
            pool.drain()
            pool.memset(att[:, :, :, S2:SP], 0.0)
            pool.drain()
            pool.memset(place[:, :], 0.0)
            pool.drain()
            for n in range(3):
                pool.affine_select(out=place[:, :], in_=place[:, :], compare_op=ALU.not_equal, fill=1.0, base=n * SP, pattern=[[-1, 3 * SP]], channel_multiplier=1)
                pool.drain()
            pool.memset(owner[:, :, :], 1.0)
            pool.drain()
            pool.affine_select(out=owner[:, :, :], in_=owner[:, :, :], compare_op=ALU.is_ge, fill=0.0,
                               base=0, pattern=[[P, CH], [-SP, HH]], channel_multiplier=1)
            pool.drain()
            pool.affine_select(out=owner[:, :, :], in_=owner[:, :, :], compare_op=ALU.is_ge, fill=0.0,
                               base=SP - 1, pattern=[[-P, CH], [SP, HH]], channel_multiplier=-1)
            pool.drain()
            if not first:
                pool.memset(cmv[:, :, :], 1.0)
                pool.drain()
            pool.memset(own[:, :], 1.0)
            pool.drain()
            pool.affine_select(out=own[:, :], in_=own[:, :], compare_op=ALU.is_ge, fill=0.0,
                               base=0, pattern=[[-DH, HB]], channel_multiplier=1)
            pool.drain()
            pool.affine_select(out=own[:, :], in_=own[:, :], compare_op=ALU.is_ge, fill=0.0,
                               base=DH - 1, pattern=[[DH, HB]], channel_multiplier=-1).then_inc(consts.sem, 1)

            def power(n, mean, out, rows, w, begin=0):
                own = slice(begin, begin + w)
                pool.wait_ge(var.sem, n)
                return pool.tensor_tensor(out[0:rows, own], mean[0:rows, own, 1], half[0:rows, own], ALU.pow)
            if not first:
                for g in range(NG):
                    power(g + 1, mv, rstd, P, G, g * G).then_inc(rs.sem, 1)
                power(NG + 1, cmv, crstd, S2, B).then_inc(rs.sem, 1)

            def lower(n, m):
                done(pool, topped, n)
                pool.tensor_tensor(att[:, m, :, 0:S2], att[:, m, :, 0:S2], top[:, m, :].unsqueeze(2).broadcast_to((P, H, S2)), ALU.subtract).then_inc(lowered.sem, 1)

            def add_bo(n, m):
                x = X[:, bass.ds(n, 1), :].rearrange("p a d -> p (a d)")
                pool.tensor_tensor(x, x, bo[:, :], ALU.add).then_inc(bo_in.sem, 1)
            pool.wait_ge(loaded_o.sem, 16 * NO)
            pool.wait_ge(q_out.sem, NG)
            pipeline(pool, T, NM, [(0, add_bo)] + ([(0, lower)] if first else []))
            if not first:
                pool.drain()
                pool.wait_ge(o_out.sem, TB)
                regroup(pool, pool.tensor_copy, 0, range(8))
                power(NG + 2, mv, rstd, P, T).then_inc(rs.sem, 1)
            def power_y(n, m):
                done(pool, y_var, n)
                pool.tensor_tensor(yrstd[:, m:m + 1], ymv[:, m, 1:2], half[:, 0:1], ALU.pow).then_inc(y_rs.sem, 1)
            pipeline(pool, T, NM, [(0, power_y)])

        @block.tensor
        def _(pe):
            pe.wait_ge(loaded_q.sem, 16 * NQ)
            for g in range(NG + 1):
                if g < NG:
                    if not first:
                        pe.wait_ge(x_ready.sem, g + 1)
                    if g >= 2:
                        pe.wait_ge(x_out.sem, g - 1)
                    for j in range(G):
                        src = X[:, g * G + j, :] if first else xg[:, g % 2, j, :]
                        for k in range(DC):
                            last = nc.tensor.transpose(ps[:, 2 * (g % 2) + k, j * P:(j + 1) * P], src[:, k * P:(k + 1) * P], ident[:, :])
                    last.then_inc(x_turned.sem, 1)
                if g >= 1:
                    at = 4 + 2 * ((g - 1) % 2)
                    pe.wait_ge(x_out.sem, g)
                    if g >= 3:
                        pe.wait_ge(q_out.sem, g - 2)
                    for c in range(DC):
                        for k in range(DC):
                            last = nc.tensor.matmul(ps[:, at + c, :], wt["Wq"][:, k, c * P:(c + 1) * P], xTg[:, (g - 1) % 2, k, :],
                                                    start=(k == 0), stop=(k == DC - 1))
                    last.then_inc(q_done.sem, 1)
            pe.wait_ge(loaded_kv.sem, 16 * NKV)
            pe.wait_ge(consts.sem, 1)
            if not first:
                pe.wait_ge(ctx_ready.sem, 1)
            pe.wait_ge(q_out.sem, NG)
            for b in range(B):
                if b:
                    pe.wait_ge(kv_out.sem, 4 * b)
                for k in range(DC):
                    last = nc.tensor.transpose(ps[:, k, 0:S2], ctx[:, b, k * P:(k + 1) * P], ident[0:S2, 0:S2])
                last.then_inc(kv_mm.sem, 1)
                pe.wait_ge(kv_out.sem, 4 * b + 1)
                for n in range(DC):
                    for k in range(DC):
                        last = nc.tensor.matmul(ps[:, 2 + n, 0:S2], wt["Wk"][:, k, n * P:(n + 1) * P], ctxT[:, k, :],
                                                start=(k == 0), stop=(k == DC - 1))
                last.then_inc(kv_mm.sem, 1)
                for k in range(DC):
                    nc.tensor.matmul(ps[0:S2, 4, 0:D], ctxT[:, k, :], wt["Wv"][:, k, :], start=(k == 0), stop=False)
                nc.tensor.matmul(ps[0:S2, 4, 0:D], ones[:, 0:S2], bv[:, :], start=False, stop=True).then_inc(kv_mm.sem, 1)
                pe.wait_ge(kv_out.sem, 4 * b + 3)
                for c in range(CH):
                    first_row = c * P % SP
                    last = nc.tensor.matmul(ps[:, 5 + c // 2, (c % 2) * D:(c % 2 + 1) * D], place[:, first_row:first_row + P], vals[:, :], start=True, stop=True)
                last.then_inc(kv_mm.sem, 1)
            pe.wait_ge(kv_out.sem, 4 * B)

            def score(bank):
                def job(n, m):
                    done(pe, qT_ready, n)
                    done(pe, scored_out, n - 1, 2, 1 - bank // 2)
                    c, r = bank * BH // HB, bank * BH % HB
                    last = nc.tensor.matmul(ps[:, bank, 0:BH * S2], qT[:, m, c, :],
                                            keys[:, :, :, :, :].rearrange("p b c h s -> p (b c h s)")[:, bass.ds((n // TB) * (H * S2) + (c * HB + r) * S2, BH * S2)],
                                            start=True, stop=True)
                    if bank % 2:
                        last.then_inc(scored.sem, 1)
                return job

            def turn(r):
                def job(n, m):
                    done(pe, summed, n)
                    if r == 2:
                        done(pe, turned_out, n, 3, 2)
                    else:
                        done(pe, turned_out, n - 1, 3)
                    for c in range(*TURNS[r]):
                        last = nc.tensor.transpose(ps[:, 4 + r % 2, (c - TURNS[r][0]) * P:(c - TURNS[r][0] + 1) * P],
                                                   att[:, m, :, :].rearrange("p h s -> p (h s)")[:, c * P:(c + 1) * P], ident[:, :])
                    last.then_inc(turned.sem, 1)
                return job

            def mix(r):
                def job(n, m):
                    if r == 0:
                        done(pe, o_out, n - 2)
                    done(pe, turned_out, n, 3, 2 - r)
                    for c in range(*TURNS[r]):
                        v = c // CH
                        last = nc.tensor.matmul(ps[:, 6 + m % 2, v * P:(v + 1) * P], pT[:, c, :],
                                                spare[:, bass.ds((n // TB) * (NCH * P) + 2 * T * D + c * P, P)], start=(c % CH == 0), stop=(c % CH == CH - 1))
                    if r < 2:
                        return
                    if not first:
                        for k in range(DC):
                            last = nc.tensor.transpose(ps[:, 6 + m % 2, D + k * P:D + (k + 1) * P], qT[:, m, k, :], ident[:, :])
                    last.then_inc(mixed.sem, 1)
                return job
            pipeline(pe, T, NM, [(3, turn(0)), (3, turn(1)), (0, score(0)), (3, mix(0)), (0, score(1)), (3, turn(2)), (3, mix(1)),
                                 (0, score(2)), (0, score(3)), (3, mix(2))], back=2)
            pe.wait_ge(loaded_o.sem, 16 * NO)

            def turn_o(n, m):
                done(pe, n_ready, n)
                done(pe, n_out, n - 2)
                for k in range(DC):
                    last = nc.tensor.transpose(ps[:, m, k * P:(k + 1) * P], xn[:, m, k * P:(k + 1) * P], ident[:, :])
                last.then_inc(n_turned.sem, 1)

            def leave(n, m):
                done(pe, n_out, n)
                done(pe, y_out, n - 2)
                for k in range(DC):
                    last = nc.tensor.matmul(ps[:, 2 + m, 0:D], xT[:, m, k, :], wt["Wo"][:, k, :], start=(k == 0), stop=(k == DC - 1))
                last.then_inc(wo_done.sem, 1)
            pipeline(pe, T, 2, [(0, turn_o), (1, leave)], back=2)

        @block.scalar
        def _(act):
            act.wait_ge(loaded_q.sem, 16 * NQ)
            if first:
                act.wait_ge(bq_scaled.sem, 1)
            for g in range(NG):
                act.wait_ge(q_done.sem, g + 1)
                for k in range(DC):
                    src = ps[:, 4 + 2 * (g % 2) + k, :]
                    if first:
                        last = nc.scalar.activation(qT_all[:, g * G:(g + 1) * G, k, :], src.rearrange("p (t q) -> p t q", t=G), ACT.Identity,
                                                    bias=bqk[:, 0, k:k + 1], scale=DH ** -0.5)
                    else:
                        last = nc.scalar.activation(qT_all[:, g * G:(g + 1) * G, k, :].rearrange("p v (w m) -> p v w m", w=4),
                                                    src.rearrange("p (m v w) -> p v w m", v=4, w=4), ACT.Identity, bias=bqk[:, 0, k:k + 1])
                last.then_inc(q_out.sem, 1)
            act.drain()

            def fetch_q(n, m):
                done(act, scored if first else mixed, n - NM, 2 if first else 1)
                nc.scalar.activation(qT[:, m, :, :].rearrange("p k q -> p (k q)"), spare[:, bass.ds(n * D, D)], ACT.Copy).then_inc(qT_ready.sem, 1)

            def exps(n, m):
                if first:
                    done(act, lowered, n)
                else:
                    done(act, scored_out, n, 2)
                nc.scalar.activation(att[:, m, :, 0:S2], att[:, m, :, 0:S2], ACT.Exp,
                                     scale=1.0 if first else DH ** -0.5).then_inc(exped.sem, 1)

            def turn_out(r):
                def job(n, m):
                    done(act, turned, n, 3, 2 - r)
                    begin, end = TURNS[r]
                    nc.scalar.activation(pT[:, begin:end, :].rearrange("p c q -> p (c q)"), ps[:, 4 + r % 2, 0:(end - begin) * P], ACT.Copy).then_inc(turned_out.sem, 1)
                return job
            pipeline(act, T, NM, [(4, turn_out(0)), (4, turn_out(1)), (3, exps), (4, turn_out(2)), (0, fetch_q)], back=4)

            def fill_o(n, m):
                done(act, n_turned, n - 2)
                nc.scalar.activation(xn[:, m, :], o_all[:, bass.ds(n, 1), :].rearrange("p a d -> p (a d)"), ACT.Copy).then_inc(n_ready.sem, 1)

            def norm_out(n, m):
                done(act, n_turned, n)
                done(act, wo_done, n - 2)
                if first:
                    last = nc.scalar.activation(xT[:, m, :, :].rearrange("p k q -> p (k q)"), ps[:, m, 0:D], ACT.Copy)
                else:
                    for k in range(DC):
                        last = nc.scalar.activation(xT[:, m, k, :], ps[:, m, k * P:(k + 1) * P], ACT.Identity,
                                                    scale=norms[:, 2, k:k + 1], bias=norms[:, 3, k:k + 1])
                last.then_inc(n_out.sem, 1)
            act.wait_ge(o_out.sem, T)
            if not first:
                regroup(act, lambda dst, src: nc.scalar.activation(dst, src, ACT.Copy), 1, range(4))
            pipeline(act, T, 2, ([(0, fill_o)] if first else []) + [(1, norm_out)], back=2)

        @block.vector
        def _(dve):
            def statistics(src, rows, n, mv, begin=0):
                own = range(begin, begin + n)
                for t in own:
                    nc.vector.bn_stats(stats[0:rows, t, :], src[:, t, :])
                dve.drain()
                for t in own:
                    nc.vector.bn_aggr(mv[0:rows, t, :], stats[0:rows, t, :])
                dve.drain()
                nc.vector.tensor_scalar(mv[0:rows, begin:begin + n, 1], mv[0:rows, begin:begin + n, 1], 1e-5, None, ALU.add).then_inc(var.sem, 1)
            if not first:
                for g in range(2):
                    statistics(X, P, G, mv, g * G)
            dve.wait_ge(loaded_q.sem, 16 * NQ)
            dve.wait_ge(consts.sem, 1)
            if first:
                nc.vector.tensor_scalar(bqk[:, 0, :], bqk[:, 0, :], DH ** -0.5, None, ALU.mult).then_inc(bq_scaled.sem, 1)
            for g in range(NG + 1):
                if g < NG and not first:
                    dve.wait_ge(rs.sem, g + 1)
                    if g >= 2:
                        dve.wait_ge(x_turned.sem, g - 1)
                    for j in range(G):
                        t = g * G + j
                        last = nc.vector.tensor_scalar(xg[:, g % 2, j, :], X[:, t, :], mv[:, t, 0:1], rstd[:, t:t + 1], ALU.subtract, ALU.mult)
                    last.then_inc(x_ready.sem, 1)
                    if g + 2 < NG:
                        statistics(X, P, G, mv, (g + 2) * G)
                if g >= 1:
                    dve.wait_ge(x_turned.sem, g)
                    if g >= 3:
                        dve.wait_ge(q_done.sem, g - 2)
                    for k in range(DC):
                        src = ps[:, 2 * ((g - 1) % 2) + k, :]
                        if first:
                            last = nc.vector.tensor_copy(xTg[:, (g - 1) % 2, k, :], src)
                        else:
                            last = nc.vector.tensor_scalar(xTg[:, (g - 1) % 2, k, :], src, norms[:, 0, k:k + 1], norms[:, 1, k:k + 1], ALU.mult, ALU.add)
                    last.then_inc(x_out.sem, 1)
            dve.wait_ge(loaded_kv.sem, 16 * NKV)
            if first:
                nc.vector.tensor_scalar(less[:, :, :], mask[:, :, :], -1.0, 1.0e10, ALU.add, ALU.mult)
            else:
                statistics(ctx, S2, B, cmv)
                dve.wait_ge(rs.sem, NG + 1)
                for b in range(B):
                    last = nc.vector.tensor_scalar(ctx[:, b, :], ctx[:, b, :], cmv[0:S2, b, 0:1], crstd[0:S2, b:b + 1], ALU.subtract, ALU.mult)
                last.then_inc(ctx_ready.sem, 1)
            for b in range(B):
                dve.wait_ge(kv_mm.sem, 4 * b + 1)
                for k in range(DC):
                    if first:
                        last = nc.vector.tensor_copy(ctxT[:, k, :], ps[:, k, 0:S2])
                    else:
                        last = nc.vector.tensor_scalar(ctxT[:, k, :], ps[:, k, 0:S2], norms[:, 0, k:k + 1], norms[:, 1, k:k + 1], ALU.mult, ALU.add)
                last.then_inc(kv_out.sem, 1)
                dve.wait_ge(kv_mm.sem, 4 * b + 2)
                for k in range(DC):
                    nc.vector.tensor_scalar(kT[:, k, :], ps[:, 2 + k, 0:S2], bqk[:, 1, k:k + 1], None, ALU.add)
                dve.drain()
                for n in range(HB):
                    last = nc.vector.tensor_scalar(keys[:, b, :, n, :], kT[:, :, :], own[:, n:n + 1], None, ALU.mult)
                last.then_inc(kv_out.sem, 1)
                dve.wait_ge(kv_mm.sem, 4 * b + 3)
                nc.vector.tensor_copy(vals[:, :], ps[0:S2, 4, 0:D]).then_inc(kv_out.sem, 1)
                dve.wait_ge(kv_mm.sem, 4 * b + 4)
                rows = ps[:, 5:8, :].rearrange("p a n -> p (a n)")[:, 0:CH * D].rearrange("p (c v h d) -> p c v h d", c=CH, v=2, h=HH)
                for v in range(2):
                    last = nc.vector.tensor_tensor(vblk[:, b, v, :, :].rearrange("p c (h d) -> p c h d", h=HH), rows[:, :, v],
                                                   owner[:, :, :].unsqueeze(3).broadcast_to((P, CH, HH, DH)), ALU.mult)
                last.then_inc(kv_out.sem, 1)

            def score_out(n, m):
                for hi in range(2):
                    heads = slice(hi * HH, (hi + 1) * HH)
                    done(dve, scored, n, 2, 1 - hi)
                    if not hi:
                        done(dve, turned, n - NM, 3)
                    src = ps[:, 2 * hi:2 * hi + 2, 0:BH * S2].rearrange("p a (h s) -> p a h s", h=BH)
                    dst = att[:, m, heads, 0:S2].rearrange("p (a h) s -> p a h s", a=2)
                    if first:
                        last = nc.vector.tensor_tensor(dst, src, mask[:, bass.ds(n % TB, 1), :].unsqueeze(1).broadcast_to((P, 2, BH, S2)), ALU.mult)
                    else:
                        if not hi:
                            done(dve, exped, n - NM)
                        peak = top[:, m, heads].rearrange("p (a h) -> p a h", a=2)
                        nc.vector.tensor_reduce(peak, src, AX.X, ALU.max)
                        dve.drain()
                        last = nc.vector.tensor_tensor(dst, src, peak.unsqueeze(3).broadcast_to((P, 2, BH, S2)), ALU.subtract)
                    last.then_inc(scored_out.sem, 1)
                if not first:
                    return
                dve.drain()
                nc.vector.tensor_tensor(att[:, m, :, 0:S2], att[:, m, :, 0:S2], less[:, bass.ds(n % TB, 1), :].broadcast_to((P, H, S2)), ALU.add)
                dve.drain()
                nc.vector.tensor_reduce(top[:, m, :], att[:, m, :, 0:S2], AX.X, ALU.max).then_inc(topped.sem, 1)

            def summing(n, m):
                done(dve, exped, n)
                nc.vector.tensor_reduce(total[:, m, :], att[:, m, :, 0:S2], AX.X, ALU.add)
                dve.drain()
                nc.vector.reciprocal(total[:, m, :], total[:, m, :]).then_inc(summed.sem, 1)

            def out(n, m):
                done(dve, mixed, n)
                dst = o_all[:, bass.ds(n, 1), :].rearrange("p a (h d) -> p (a h) d", d=DH)
                last = nc.vector.tensor_tensor(dst, ps[:, 6 + m % 2, 0:D].rearrange("p (h d) -> p h d", d=DH),
                                               total[:, m, :].unsqueeze(2).broadcast_to((P, H, DH)), ALU.mult)
                if not first:
                    dve.drain()
                    flat = o_all[:, bass.ds(n, 1), :].rearrange("p a d -> p (a d)")
                    last = nc.vector.tensor_tensor(flat, ps[:, 6 + m % 2, D:2 * D], flat, ALU.add)
                last.then_inc(o_out.sem, 1)
            pipeline(dve, T, NM, [(2, summing), (0, score_out), (4, out)], back=4)
            if not first:
                dve.drain()
                regroup(nc.vector, nc.vector.tensor_copy, 1, range(4, 8))
                dve.wait_ge(grouped.sem, 3)
                statistics(o, P, T, mv)
                dve.wait_ge(bo_in.sem, T)
                nc.vector.tensor_tensor(X[:, :, :], X[:, :, :], o[:, :, :], ALU.add)
                dve.wait_ge(rs.sem, NG + 2)
                dve.drain()

            def norm_o(n, m):
                done(dve, n_turned, n - 2)
                nc.vector.tensor_scalar(xn[:, m, :], o[:, bass.ds(n, 1), :].rearrange("p a d -> p (a d)"), mv[:, bass.ds(n, 1), 0], rstd[:, bass.ds(n, 1)],
                                        ALU.subtract, ALU.mult).then_inc(n_ready.sem, 1)

            def add(n, m):
                done(dve, wo_done, n)
                x = X[:, bass.ds(n, 1), :].rearrange("p a d -> p (a d)")
                nc.vector.tensor_tensor(y[:, m, :], ps[:, 2 + m % 2, 0:D], x, ALU.add).then_inc(y_out.sem, 1)
                dve.drain()
                nc.vector.bn_stats(ystats[:, m, :], y[:, m, :])
                dve.drain()
                nc.vector.bn_aggr(ymv[:, m, :], ystats[:, m, :])
                dve.drain()
                nc.vector.tensor_scalar(ymv[:, m, 1:2], ymv[:, m, 1:2], 1e-5, None, ALU.add).then_inc(y_var.sem, 1)

            def norm_y(n, m):
                done(dve, y_rs, n)
                nc.vector.tensor_scalar(X[:, bass.ds(n, 1), :].rearrange("p a d -> p (a d)"), y[:, m, :], ymv[:, m, 0:1], yrstd[:, m:m + 1], ALU.subtract, ALU.mult)
            if first:
                dve.wait_ge(bo_in.sem, T)
            pipeline(dve, T, NM, ([] if first else [(0, lambda n, m: norm_o(n, m % 2))]) + [(2, add), (3, norm_y)], back=2)


def slot_projections(nc, X, ident, ps, a, scratch, v_all, spare, prefetch):
    N = D
    NC = N // P
    SETS = ("q", "k", "v")
    R = 2
    with ExitStack() as cx:
        sb = tiles(nc, cx)
        words = [0, 3 * NC * GT, 3 * NC * GT + 3 * DC * N, 3 * NC * GT + 3 * DC * N + 3 * NC * D]
        aT = spare[:, words[0]:words[1]].rearrange("p (s c q) -> p s c q", s=3, c=NC)
        kT = spare[:, words[1]:words[2]].rearrange("p (s k n) -> p s k n", s=3, k=DC)
        vals = spare[:, words[2]:words[3]].rearrange("p (s k n) -> p s k n", s=3, k=NC)
        half = sb("d_half", [P, 1])
        xn = sb("d_xn", [P, R, D])
        hT = sb("d_hT", [P, R, DC, P])
        probs = sb("d_probs", [P, R, 3, N])
        part = {n: sb("d_part_" + n, [P, 3, DC, GT], BF16) for n in ("q", "k")}
        left = sb("d_left", [P, DC, GT])
        nmax = sb("d_nmax", [P, R, 3])
        total = sb("d_total", [P, R, 3])
        stats, mv, rstd = sb("d_stats", [P, G, 6]), sb("d_mv", [P, G, 2]), sb("d_rstd", [P, G])

        def sig(name):
            return Signal(cx, nc, "d_" + name)
        loaded, loaded_v, var, rs = sig("loaded"), sig("loaded_v"), sig("var"), sig("rs")
        h_ready, h_turned, h_out = sig("h_ready"), sig("h_turned"), sig("h_out")
        scored, maxed, exped, normed, turned, turned_out = (sig(n) for n in ("scored", "maxed", "exped", "normed", "turned", "turned_out"))
        slotted, v_out = [sig("slotted_" + n) for n in SETS], sig("v_out")
        hi_out, left_out, mid_out, lo_out, stored = ([sig(f"{w}_{n}") for n in ("q", "k")] for w in ("hi_out", "left_out", "mid_out", "lo_out", "stored"))
        block = cx.enter_context(nc.Block())

        def last_of_group(job):
            return lambda n, m: job(n // G) if m == G - 1 else None

        @block.sync
        def _(sp):
            for n, name in enumerate(SETS):
                sp.dma_start(kT[:, n, :, :], a[f"L1_attn_{name}K"].rearrange("(k p) n -> p k n", p=P)).then_inc(loaded.sem, 16)
            for n, name in enumerate(SETS):
                sp.dma_start(vals[:, n, :, :], a[f"L1_attn_{name}V"].rearrange("(k p) n -> p k n", p=P)).then_inc(loaded_v.sem, 16)
            prefetch(sp)
            with sp.Fori(0, NG) as i:
                for n, name in enumerate(("q", "k")):
                    sp.wait_ge(lo_out[n].sem, i + 1)
                    rows = scratch[name].rearrange("s c p t -> p (s c) t")
                    sp.dma_start(rows[:, :, bass.ds(i * GT, GT)], part[name][:, :, :, :].rearrange("p s c t -> p (s c) t")).then_inc(stored[n].sem, 16)
            for n in range(2):
                sp.wait_ge(stored[n].sem, 16 * NG)

        @block.gpsimd
        def _(pool):
            pool.memset(half[:, :], -0.5)
            pool.drain()

            def power(n, m):
                done(pool, var, n)
                pool.tensor_tensor(rstd[:, m:m + 1], mv[:, m, 1:2], half[:, :], ALU.pow).then_inc(rs.sem, 1)
            pipeline(pool, T, G, [(0, power)])

        def banks(m):
            return ps[:, 2 * (m % R):2 * (m % R) + 2, :].rearrange("p a n -> p (a n)")

        @block.tensor
        def _(pe):
            pe.wait_ge(loaded.sem, 16 * 3)

            def turn_h(n, m):
                done(pe, h_ready, n)
                done(pe, exped, n - R, 3)
                for k in range(DC):
                    last = nc.tensor.transpose(banks(m)[:, 3 * N + k * P:3 * N + (k + 1) * P], xn[:, m % R, k * P:(k + 1) * P], ident[:, :])
                last.then_inc(h_turned.sem, 1)

            def score(n, m):
                done(pe, h_out, n)
                for s in range(3):
                    for k in range(DC):
                        last = nc.tensor.matmul(banks(m)[:, s * N:(s + 1) * N], hT[:, m % R, k, :], kT[:, s, k, :], start=(k == 0), stop=(k == DC - 1))
                last.then_inc(scored.sem, 1)

            def turn(n, m):
                done(pe, normed, n)
                done(pe, turned_out, n - 1)
                for s in range(3):
                    for c in range(NC):
                        at = (s * NC + c) * P
                        last = nc.tensor.transpose(ps[:, 4 + at // 512, at % 512:at % 512 + P], probs[:, m % R, s, c * P:(c + 1) * P], ident[:, :])
                last.then_inc(turned.sem, 1)

            def slots(s):
                def of_group(g):
                    if s == 0:
                        done(pe, turned_out, (g + 1) * G - 1)
                        if isinstance(g, int) and g == 0:
                            pe.wait_ge(loaded_v.sem, 16 * 3)
                        done(pe, v_out, g - 1)
                    else:
                        done(pe, left_out[s - 1], g)
                    if s < 2:
                        for n in range(DC):
                            for k in range(NC):
                                last = nc.tensor.matmul(ps[:, 6 + n, :], vals[:, s, k, n * P:(n + 1) * P], aT[:, s, k, :], start=(k == 0), stop=(k == NC - 1))
                    else:
                        for j in range(G):
                            for k in range(NC):
                                last = nc.tensor.matmul(ps[:, 6 + j // 2, (j % 2) * D:(j % 2 + 1) * D], aT[:, s, k, j * P:(j + 1) * P], vals[:, s, k, :],
                                                        start=(k == 0), stop=(k == NC - 1))
                    last.then_inc(slotted[s].sem, 1)
                return last_of_group(of_group)
            pipeline(pe, T, G, [(3, slots(0)), (1, score), (3, slots(1)), (0, turn_h), (2, turn), (3, slots(2))], back=4)

        @block.scalar
        def _(act):
            def h_copy(n, m):
                done(act, h_turned, n)
                done(act, scored, n - R)
                nc.scalar.activation(hT[:, m % R, :, :].rearrange("p k q -> p (k q)"), banks(m)[:, 3 * N:4 * N], ACT.Copy, scale=D ** -0.5).then_inc(h_out.sem, 1)

            def exps(n, m):
                done(act, maxed, n)
                done(act, turned, n - R)
                for s in range(3):
                    nc.scalar.activation(probs[:, m % R, s, :], banks(m)[:, s * N:(s + 1) * N], ACT.Exp, bias=nmax[:, m % R, s:s + 1],
                                         accum_out=total[:, m % R, s:s + 1]).then_inc(exped.sem, 1)

            def a_copy(n, m):
                done(act, turned, n)
                if m == 0:
                    done(act, slotted[2], n // G - 1)
                nc.scalar.activation(aT[:, :, :, m * P:(m + 1) * P].rearrange("p s c q -> p (s c) q"),
                                     ps[:, 4:6, :].rearrange("p a n -> p (a n)")[:, 0:3 * N].rearrange("p (c q) -> p c q", q=P), ACT.Copy).then_inc(turned_out.sem, 1)

            def hi(s):
                def of_group(g):
                    done(act, slotted[s], g)
                    done(act, stored[s], g - 1, 16)
                    nc.scalar.activation(part[SETS[s]][:, 0], ps[:, 6:8, :], ACT.Copy).then_inc(hi_out[s].sem, 1)
                return last_of_group(of_group)

            def mid(s):
                def of_group(g):
                    done(act, left_out[s], g)
                    nc.scalar.activation(part[SETS[s]][:, 1], left[:, :, :], ACT.Copy).then_inc(mid_out[s].sem, 1)
                return last_of_group(of_group)
            pipeline(act, T, G, [(3, hi(0)), (1, exps), (3, mid(0)), (3, hi(1)), (0, h_copy), (3, mid(1)), (2, a_copy)], back=4)

        @block.vector
        def _(dve):
            flat = X[:, :, :].rearrange("p t d -> p (t d)")

            def statistics(n, m):
                nc.vector.bn_stats(stats[:, m, :], flat[:, bass.ds(n * D, D)])
                dve.drain()
                nc.vector.bn_aggr(mv[:, m, :], stats[:, m, :])
                dve.drain()
                nc.vector.tensor_scalar(mv[:, m, 1:2], mv[:, m, 1:2], 1e-5, None, ALU.add).then_inc(var.sem, 1)

            def norm_x(n, m):
                done(dve, rs, n)
                done(dve, h_turned, n - R)
                nc.vector.tensor_scalar(xn[:, m % R, :], flat[:, bass.ds(n * D, D)], mv[:, m, 0:1], rstd[:, m:m + 1], ALU.subtract, ALU.mult).then_inc(h_ready.sem, 1)

            def maximum(n, m):
                done(dve, scored, n)
                nc.vector.tensor_reduce(nmax[:, m % R, :], banks(m)[:, 0:3 * N].rearrange("p (s n) -> p s n", s=3), AX.X, ALU.max, negate=True).then_inc(maxed.sem, 1)

            def normalise(n, m):
                done(dve, exped, n, 3)
                nc.vector.reciprocal(total[:, m % R, :], total[:, m % R, :])
                dve.drain()
                nc.vector.tensor_tensor(probs[:, m % R], probs[:, m % R], total[:, m % R, :].unsqueeze(2).broadcast_to((P, 3, N)), ALU.mult).then_inc(normed.sem, 1)

            def rest(s):
                def of_group(g):
                    done(dve, hi_out[s], g)
                    nc.vector.tensor_tensor(left[:, :, :], ps[:, 6:8, :], part[SETS[s]][:, 0], ALU.subtract).then_inc(left_out[s].sem, 1)
                return last_of_group(of_group)

            def low(s):
                def of_group(g):
                    done(dve, mid_out[s], g)
                    nc.vector.tensor_tensor(part[SETS[s]][:, 2], left[:, :, :], part[SETS[s]][:, 1], ALU.subtract).then_inc(lo_out[s].sem, 1)
                    dve.drain()
                return last_of_group(of_group)

            def values(g):
                done(dve, slotted[2], g)
                nc.vector.tensor_copy(v_all[:, :, :].rearrange("p t d -> p (t d)")[:, bass.ds(g * (G * D), G * D)],
                                      ps[:, 6:8, :].rearrange("p a n -> p (a n)")).then_inc(v_out.sem, 1)
            pipeline(dve, T, G, [(5, last_of_group(values)), (3, normalise), (0, statistics), (1, norm_x), (4, rest(0)), (2, maximum),
                                 (4, low(0)), (4, rest(1)), (4, low(1))], back=3)


def causal_attention(nc, ident, ps, scratch, v_all, o_all, spare):
    Q4 = 4
    NU = HB // Q4
    NQ = B * DC * NU
    QPART = (0, 0, 1, 1, 0, 2)
    KPART = (0, 1, 0, 1, 2, 0)
    NR = len(QPART) * DH
    NR3 = NR + 3
    HALF = 512
    PIECES = [(h, t, lo) for h in range(Q4) for t in range(TB) for lo in range(0, (t + 1) * P, HALF)]
    NP = len(PIECES)
    WORKS = []
    for t in range(TB + 1):
        scores = [("score", t, h, S - t * P + HALF // 2) for h in range(Q4)] if t < TB else []
        mixes = [("mix", t - 1, half, 4 * ((half + 1) * HALF - max(half * HALF, (t - 1) * P))) for half in range((t - 1) * P // HALF, 2)] if t else []
        WORKS += scores[0:2] + mixes[0:1] + scores[2:3] + mixes[1:] + scores[3:]
    FROM, TO = 0.08, 0.85

    def reached(sizes):
        return np.cumsum(sizes) / sum(sizes)
    behind = [int(np.sum(reached([min((t + 1) * P - lo, HALF) + P for _, t, lo in PIECES]) <= (at - FROM) / (TO - FROM) + 1e-9))
              for at in reached([work[3] for work in WORKS])]
    with ExitStack() as cx:
        sb = tiles(nc, cx)
        qs = [sb(f"t_qs{u}", [P, Q4, S], BF16) for u in range(NU)]
        ks = [sb(f"t_ks{u}", [P, Q4, S], BF16) for u in range(NU)]
        vq = [sb(f"t_vq{u}", [P, TB, Q4, 32]) for u in range(NU)]
        identb = sb("t_identb", [P, P], BF16)
        causal = sb("t_causal", [P, P], BF16)
        causalT = sb("t_causalT", [P, P], BF16)
        nm = sb("t_nm", [P, Q4, TB])
        nm1 = sb("t_nm1", [P, Q4, TB])
        nmp = sb("t_nmp", [P, 3, Q4, TB], BF16)
        nml = sb("t_nml", [P, Q4, TB])
        nmT = sb("t_nmT", [3 * Q4 * TB, P], BF16)
        pT = spare[:, 0:2 * Q4 * S].rearrange("p (m h q) -> p m h q", m=2, h=Q4)
        oT = sb("t_oT", [P, S])
        inv = sb("t_inv", [P, TB, Q4])

        def sig(name):
            return Signal(cx, nc, "t_" + name)
        consts, stacked, v_ready = sig("consts"), [sig(f"stacked{u}") for u in range(NU)], sig("v_ready")
        scored, maxed = sig("scored"), sig("maxed")
        split, split_turned, split_out, max_stored, lowered = (sig(n) for n in ("split", "split_turned", "split_out", "max_stored", "lowered"))
        tscored, exped, mixed = (sig(n) for n in ("tscored", "exped", "mixed"))
        o_out, o_turned, o_done = sig("o_out"), sig("o_turned"), sig("o_done")
        block = cx.enter_context(nc.Block())

        def past(eng, signal, q, k, per):
            if not isinstance(q, int) or q * per + k > 0:
                eng.wait_ge(signal.sem, q * per + k)

        def quads(eng, quad):
            quad(0, 0, False)
            with eng.Fori(0, (NQ - 2) // 2) as j:
                quad(j * 2 + 1, 1, False)
                quad(j * 2 + 2, 0, False)
            quad(NQ - 1, 1, True)

        def place(q):
            return q // (NU * DC), q // NU % DC

        @block.sync
        def _(sp):
            def load(q, u):
                past(sp, mixed, q - 2, TB, TB)
                b, c = place(q)
                for name, dst, parts in (("q", qs[u], QPART), ("k", ks[u], KPART)):
                    for r, part in enumerate(parts):
                        src = scratch[name][part].rearrange("c (u h d) (b t) -> d u h c b t", u=NU, h=Q4, b=B)
                        sp.dma_start(dst[r * DH:(r + 1) * DH, :, :].unsqueeze(2).unsqueeze(3), src[:, u, :, bass.ds(c, 1), bass.ds(b, 1), :]).then_inc(stacked[u].sem, 16)

            def lower(q, u):
                past(sp, split_out, q, 1, 1)
                past(sp, lowered, q - 1, 16, 16)
                sp.dma_start(scratch["max"].rearrange("s (n q) -> (s n) q", q=P), nmT[:, :]).then_inc(max_stored.sem, 16)
                past(sp, max_stored, q, 16, 16)
                sp.dma_start(qs[u][NR:NR3, :, :].rearrange("s h t -> s (h t)"), scratch["max"]).then_inc(lowered.sem, 16)

            load(0, 0)
            load(1, 1)
            lower(0, 0)

            lower(1, 1)
            load(2, 0)
            with sp.Fori(1, NQ // 2 - 1) as j:
                lower(j * 2, 0)
                load(j * 2 + 1, 1)
                lower(j * 2 + 1, 1)
                load(j * 2 + 2, 0)
            lower(NQ - 2, 0)
            load(NQ - 1, 1)
            lower(NQ - 1, 1)

        @block.gpsimd
        def _(pool):
            pool.memset(identb[:, :], 0.0)
            pool.drain()
            pool.affine_select(out=identb[:, :], in_=identb[:, :], compare_op=ALU.not_equal, fill=1.0, base=0, pattern=[[-1, P]], channel_multiplier=1)
            pool.drain()
            for t, mul, step in ((causal, 1, -1), (causalT, -1, 1)):
                pool.memset(t[:, :], 0.0)
                pool.drain()
                pool.affine_select(out=t[:, :], in_=t[:, :], compare_op=ALU.is_ge, fill=-1.0e30, base=0, pattern=[[step, P]], channel_multiplier=mul)
                pool.drain()
            for u in range(NU):
                pool.memset(ks[u][NR:NR3 + 29, :, :], 1.0)
                pool.drain()
                pool.memset(vq[u][:, :, :, :], 0.0)
                pool.drain()
                pool.memset(vq[u][:, :, :, DH:DH + 1], 1.0)
                pool.drain()
            pool.engine_nop().then_inc(consts.sem, 1)

            def values(q, u):
                past(pool, mixed, q - 2, TB, TB)
                b, c = place(q)
                src = v_all[:, :, :].rearrange("p (b t) (c u h d) -> p b t c u h d", b=B, c=DC, u=NU, h=Q4)
                for h in range(Q4):
                    pool.tensor_copy(vq[u][:, :, h, 0:DH].unsqueeze(1).unsqueeze(3), src[:, bass.ds(b, 1), :, bass.ds(c, 1), u, h, :])
                    pool.drain()
                pool.engine_nop().then_inc(v_ready.sem, 1)

            def quad(q, u, last):
                if not last:
                    values(q + 1, 1 - u)
            values(0, 0)
            quads(pool, quad)

        @block.tensor
        def _(pe):
            pe.wait_ge(consts.sem, 1)

            def piece(q, u, n):
                h, t, lo = PIECES[n]
                w = (t + 1) * P
                hi = min(w, lo + HALF)
                past(pe, maxed, q, n - 1, NP)
                last = nc.tensor.matmul(ps[:, 6 + n % 2, 0:hi - lo], qs[u][0:NR, h, t * P:w], ks[u][0:NR, h, lo:hi], start=True, stop=hi < w)
                if hi == w:
                    last = nc.tensor.matmul(ps[:, 6 + n % 2, t * P - lo:w - lo], identb[:, :], causal[:, :], start=False, stop=True)
                last.then_inc(scored.sem, 1)

            def turn_maxima(q):
                past(pe, split, q, 1, 1)
                nc.tensor.transpose(ps[0:96, 6, :].bitcast(BF16)[:, 0:P], nmp[:, :, :, :].rearrange("p s h t -> p (s h t)"), identb[:, :]).then_inc(split_turned.sem, 1)

            def turn_o(q):
                past(pe, o_out, q, 1, 1)
                for t in range(TB):
                    last = nc.tensor.transpose(ps[:, 6 + t // 4, (t % 4) * P:(t % 4 + 1) * P], oT[:, t * P:(t + 1) * P], ident[:, :])
                last.then_inc(o_turned.sem, 1)

            def score(q, u, t, h):
                past(pe, exped, q, t * Q4 + h - 1, TB * Q4)
                at = t * P
                pair = 2 * (h % 2)
                for m, lo in enumerate(range(at // HALF * HALF, S, HALF)):
                    bank = pair + lo // HALF
                    lo = max(lo, at)
                    hi = (lo // HALF + 1) * HALF
                    nc.tensor.matmul(ps[:, bank, lo % HALF:lo % HALF + hi - lo], ks[u][0:NR3, h, at:at + P], qs[u][0:NR3, h, lo:hi], start=True, stop=m > 0)
                nc.tensor.matmul(ps[:, pair + at // HALF, at % HALF:at % HALF + P], identb[:, :], causalT[:, :], start=False, stop=True).then_inc(tscored.sem, 1)

            def mix(q, u, t, half):
                past(pe, exped, q, (t + 1) * Q4, TB * Q4)
                if t == 0 and half == 0:
                    past(pe, v_ready, q, 1, 1)
                    past(pe, o_out, q - 1, 1, 1)
                lo, hi = max(half * HALF, t * P), (half + 1) * HALF
                for h in range(Q4):
                    last = nc.tensor.matmul(ps[32 * h:32 * h + 32, 4 + half, lo % HALF:lo % HALF + hi - lo], vq[u][:, t, h, :], pT[:, t % 2, h, lo:hi],
                                            start=(t == 0), stop=(t == hi // P - 1))
                if half == 1:
                    last.then_inc(mixed.sem, 1)

            def quad(q, u, last):
                n = 0
                past(pe, lowered, q, 16, 16)
                for k, (kind, t, part, _) in enumerate(WORKS):
                    if kind == "score":
                        score(q, u, t, part)
                    else:
                        mix(q, u, t, part)
                    if k == 1 and not (isinstance(q, int) and q == 0):
                        turn_o(q - 1)
                    if last:
                        continue
                    if n == 0 and behind[k]:
                        past(pe, stacked[1 - u], (q + 1) // NU, 12 * 16, 12 * 16)
                        past(pe, o_done, q - 1, 1, 1)
                    for n in range(n, behind[k]):
                        piece(q + 1, 1 - u, n)
                    if behind[k - 4] < NP <= behind[k - 3]:
                        turn_maxima(q + 1)
                    n = behind[k]

            past(pe, stacked[0], 0, 12 * 16, 12 * 16)
            for n in range(NP):
                piece(0, 0, n)
            turn_maxima(0)
            quads(pe, quad)
            turn_o(NQ - 1)

        @block.scalar
        def _(act):
            def quad(q, u, last):
                for t in range(TB):
                    past(act, mixed, q, t - 1, TB)
                    for h in range(Q4):
                        past(act, tscored, q, t * Q4 + h + 1, TB * Q4)
                        pair = 2 * (h % 2)
                        nc.scalar.activation(pT[:, t % 2, h, t * P:S], ps[:, pair:pair + 2, :].rearrange("p a n -> p (a n)")[:, t * P:S], ACT.Exp,
                                             scale=DH ** -0.5).then_inc(exped.sem, 1)
            quads(act, quad)

        @block.vector
        def _(dve):
            def maxima(q):
                for n, (h, t, lo) in enumerate(PIECES):
                    w = min((t + 1) * P, lo + HALF) - lo
                    dst = nm if lo + w == (t + 1) * P else nm1
                    past(dve, scored, q, n + 1, NP)
                    nc.vector.tensor_reduce(dst[:, h, t:t + 1], ps[:, 6 + n % 2, 0:w], AX.X, ALU.max, negate=True).then_inc(maxed.sem, 1)
                dve.drain()
                more = slice(HALF // P, TB)
                nc.vector.tensor_tensor(nm[:, :, more], nm[:, :, more], nm1[:, :, more], ALU.min)
                dve.drain()
                nc.vector.tensor_copy(nmp[:, 0], nm[:, :, :])
                dve.drain()
                nc.vector.tensor_tensor(nml[:, :, :], nm[:, :, :], nmp[:, 0], ALU.subtract)
                dve.drain()
                nc.vector.tensor_copy(nmp[:, 1], nml[:, :, :])
                dve.drain()
                nc.vector.tensor_tensor(nmp[:, 2], nml[:, :, :], nmp[:, 1], ALU.subtract).then_inc(split.sem, 1)
                past(dve, split_turned, q, 1, 1)
                past(dve, max_stored, q - 1, 16, 16)
                nc.vector.tensor_copy(nmT[:, :], ps[0:96, 6, :].bitcast(BF16)[:, 0:P]).then_inc(split_out.sem, 1)

            def outputs(q, u):
                b, c = place(q)
                past(dve, mixed, q, TB, TB)
                nc.vector.tensor_copy(oT[:, :], ps[:, 4:6, :].rearrange("p a n -> p (a n)")).then_inc(o_out.sem, 1)
                past(dve, o_turned, q, 1, 1)
                turned = ps[:, 6:8, :].rearrange("p a (t h d) -> p (a t) h d", h=Q4, d=32)
                nc.vector.reciprocal(inv[:, :, :].unsqueeze(3), turned[:, :, :, DH:DH + 1])
                dve.drain()
                dst = o_all[:, :, :].rearrange("p (b t) (c u h d) -> p b t c u h d", b=B, c=DC, u=NU, h=Q4)
                for h in range(Q4):
                    last = nc.vector.tensor_tensor(dst[:, bass.ds(b, 1), :, bass.ds(c, 1), u, h, :], turned[:, :, h, 0:DH].unsqueeze(1).unsqueeze(3),
                                                   inv[:, :, h:h + 1].unsqueeze(1).unsqueeze(3).broadcast_to((P, 1, TB, 1, DH)), ALU.mult)
                last.then_inc(o_done.sem, 1)

            def quad(q, u, last):
                if not last:
                    maxima(q + 1)
                outputs(q, u)
            maxima(0)
            quads(dve, quad)


def slot_layers(nc, X, ident, ps, a, o_all, spare):
    NP, NF = 256, 1024
    CP, CF = NP // P, NF // P
    R = 2
    with ExitStack() as cx:
        sb = tiles(nc, cx)
        words = np.cumsum([0, DC * NF, CF * D, R * NF])
        fK = spare[:, words[0]:words[1]].rearrange("p (k n) -> p k n", k=DC)
        fV = spare[:, words[1]:words[2]].rearrange("p (k n) -> p k n", k=CF)
        pT = spare[:, words[2]:words[3]].rearrange("p (m n) -> p m n", m=R)
        pK, pV = sb("e_pK", [P, DC, NP]), sb("e_pV", [P, CP, D])
        half, eps = sb("e_half", [P, T]), sb("e_eps", [P, 2])
        rows = sb("e_rows", [P, R, D])
        rowsT = sb("e_rowsT", [P, R, DC, P])
        probs = sb("e_probs", [P, R, NF])
        y = sb("e_y", [P, G, D])
        nmax, total = sb("e_nmax", [P, G, 1]), sb("e_total", [P, G, 1])
        stats, mv, rstd = sb("e_stats", [P, G, 6]), sb("e_mv", [P, T, 2]), sb("e_rstd", [P, T])
        ymv, yrstd = sb("e_ymv", [P, G, 2]), sb("e_yrstd", [P, G])
        oflat = o_all[:, :, :].rearrange("p t d -> p (t d)")
        flat = X[:, :, :].rearrange("p t d -> p (t d)")

        def sig(name):
            return Signal(cx, nc, "e_" + name)
        consts, loaded_p, loaded_f, z_var, z_rs, summed, y_var, y_rs = (sig(n) for n in ("consts", "loaded_p", "loaded_f", "z_var", "z_rs", "summed", "y_var", "y_rs"))
        rows_ready, rows_turned, rowsT_out, scored, maxed, exped, turned, turned_out, slotted, added = (
            [sig(f"{n}{l}") for l in range(2)] for n in
            ("rows_ready", "rows_turned", "rowsT_out", "scored", "maxed", "exped", "turned", "turned_out", "slotted", "added"))
        WIDTH, CHUNKS, KEYS, VALUES = (NP, NF), (CP, CF), (pK, fK), (pV, fV)
        block = cx.enter_context(nc.Block())

        def scores(l, m):
            at = (m % R) * (l + 1)
            return ps[:, at:at + l + 1, :].rearrange("p a n -> p (a n)")[:, 0:WIDTH[l]]

        def flipped(l):
            return ps[:, 4:5 + l, :].rearrange("p a n -> p (a n)")[:, 0:WIDTH[l]]

        def of_layer(l, job):
            return lambda n, m: job(l, n, m)

        @block.sync
        def _(sp):
            for dst, name in ((pK, "pK"), (pV, "pV")):
                sp.dma_start(dst[:, :, :], a["L1_attn_" + name].rearrange("(k p) n -> p k n", p=P)).then_inc(loaded_p.sem, 16)
            for dst, name in ((fK, "fK"), (fV, "fV")):
                sp.dma_start(dst[:, :, :], a["L1_attn_" + name].rearrange("(k p) n -> p k n", p=P)).then_inc(loaded_f.sem, 16)

        @block.gpsimd
        def _(pool):
            pool.memset(half[:, :], -0.5)
            pool.drain()
            pool.memset(eps[:, 0:1], 0.0)
            pool.drain()
            pool.memset(eps[:, 1:2], 1e-5)
            pool.drain()
            pool.engine_nop().then_inc(consts.sem, 1)

            def fetch_o(n, m):
                done(pool, rows_turned[0], n - R)
                pool.tensor_copy(rows[:, m % R, :], oflat[:, bass.ds(n * D, D)]).then_inc(rows_ready[0].sem, 1)
            pipeline(pool, T, G, [(0, fetch_o)], back=2)
            pool.wait_ge(z_var.sem, T)
            pool.tensor_tensor(rstd[:, :], mv[:, :, 1], half[:, :], ALU.pow).then_inc(z_rs.sem, 1)

            def add_z(n, m):
                done(pool, z_var, n)
                pool.tensor_tensor(flat[:, bass.ds(n * D, D)], flat[:, bass.ds(n * D, D)], oflat[:, bass.ds(n * D, D)], ALU.add).then_inc(summed.sem, 1)

            def power_y(n, m):
                done(pool, y_var, n)
                pool.tensor_tensor(yrstd[:, m:m + 1], ymv[:, m, 1:2], half[:, 0:1], ALU.pow).then_inc(y_rs.sem, 1)
            pipeline(pool, T, G, [(0, add_z), (1, power_y)])

        @block.tensor
        def _(pe):
            def turn_rows(l, n, m):
                done(pe, rows_ready[l], n)
                done(pe, rowsT_out[l], n - 1)
                for k in range(DC):
                    last = nc.tensor.transpose(ps[:, 7, k * P:(k + 1) * P], rows[:, m % R, k * P:(k + 1) * P], ident[:, :])
                last.then_inc(rows_turned[l].sem, 1)

            def score(l, n, m):
                done(pe, rowsT_out[l], n)
                done(pe, exped[l], n - R)
                w = min(512, WIDTH[l])
                for lo in range(0, WIDTH[l], w):
                    for k in range(DC):
                        last = nc.tensor.matmul(scores(l, m)[:, lo:lo + w], rowsT[:, m % R, k, :], KEYS[l][:, k, lo:lo + w], start=(k == 0), stop=(k == DC - 1))
                last.then_inc(scored[l].sem, 1)

            def turn(l, n, m):
                done(pe, exped[l], n)
                done(pe, turned_out[l], n - 1)
                for c in range(CHUNKS[l]):
                    last = nc.tensor.transpose(flipped(l)[:, c * P:(c + 1) * P], probs[:, m % R, c * P:(c + 1) * P], ident[:, :])
                last.then_inc(turned[l].sem, 1)

            def slots(l, n, m):
                done(pe, turned_out[l], n)
                done(pe, added[l], n - 1)
                for c in range(CHUNKS[l]):
                    last = nc.tensor.matmul(ps[:, 6, 0:D], pT[:, m % R, c * P:(c + 1) * P], VALUES[l][:, c, :], start=(c == 0), stop=(c == CHUNKS[l] - 1))
                last.then_inc(slotted[l].sem, 1)
            pe.wait_ge(loaded_p.sem, 16 * 2)
            for l in range(2):
                if l:
                    pe.wait_ge(loaded_f.sem, 16 * 2)
                    pe.wait_ge(added[0].sem, T)
                pipeline(pe, T, G, [(1, of_layer(l, score)), (0, of_layer(l, turn_rows)), (2, of_layer(l, turn)), (3, of_layer(l, slots))], back=2)

        @block.scalar
        def _(act):
            def exps(l, n, m):
                done(act, maxed[l], n)
                done(act, turned[l], n - R)
                nc.scalar.activation(probs[:, m % R, 0:WIDTH[l]], scores(l, m), ACT.Exp, bias=nmax[:, m, :], accum_out=total[:, m, :]).then_inc(exped[l].sem, 1)

            def turn_out(l, n, m):
                done(act, turned[l], n)
                done(act, slotted[l], n - R)
                nc.scalar.activation(pT[:, m % R, 0:WIDTH[l]], flipped(l), ACT.Copy).then_inc(turned_out[l].sem, 1)
            for l in range(2):
                pipeline(act, T, G, [(1, of_layer(l, exps)), (2, of_layer(l, turn_out))], back=2)

        @block.vector
        def _(dve):
            def statistics(src, m, out, var):
                nc.vector.bn_stats(stats[:, m, :], src)
                dve.drain()
                nc.vector.bn_aggr(ymv[:, m, :], stats[:, m, :])
                dve.drain()
                nc.vector.tensor_tensor(out, ymv[:, m, :], eps[:, :], ALU.add).then_inc(var.sem, 1)
            dve.wait_ge(consts.sem, 1)

            def norm_z(n, m):
                done(dve, rows_turned[1], n - R)
                nc.vector.tensor_scalar(rows[:, m % R, :], oflat[:, bass.ds(n * D, D)], mv[:, bass.ds(n, 1), 0], rstd[:, bass.ds(n, 1)],
                                        ALU.subtract, ALU.mult).then_inc(rows_ready[1].sem, 1)

            def rows_out(l, n, m):
                done(dve, rows_turned[l], n)
                done(dve, scored[l], n - R)
                nc.vector.tensor_scalar(rowsT[:, m % R, :, :].rearrange("p k q -> p (k q)"), ps[:, 7, 0:D], D ** -0.5, None, ALU.mult).then_inc(rowsT_out[l].sem, 1)

            def maximum(l, n, m):
                done(dve, scored[l], n)
                nc.vector.tensor_reduce(nmax[:, m, :], scores(l, m), AX.X, ALU.max, negate=True).then_inc(maxed[l].sem, 1)

            def add(l, n, m):
                if l:
                    done(dve, summed, n)
                done(dve, slotted[l], n)
                nc.vector.reciprocal(total[:, m, :], total[:, m, :])
                dve.drain()
                own = bass.ds(n * D, D)
                dst = y[:, m, :] if l else oflat[:, own]
                nc.vector.scalar_tensor_tensor(out=dst, in0=ps[:, 6, 0:D], scalar=total[:, m, :], in1=flat[:, own], op0=ALU.mult, op1=ALU.add).then_inc(added[l].sem, 1)
                dve.drain()
                if l:
                    statistics(dst, m, ymv[:, m, :], y_var)
                else:
                    statistics(dst, m, mv[:, bass.ds(n, 1), :].rearrange("p a s -> p (a s)"), z_var)

            def norm_y(n, m):
                done(dve, y_rs, n)
                nc.vector.tensor_scalar(flat[:, bass.ds(n * D, D)], y[:, m, :], ymv[:, m, 0:1], yrstd[:, m:m + 1], ALU.subtract, ALU.mult)
            pipeline(dve, T, G, [(0, of_layer(0, rows_out)), (1, of_layer(0, maximum)), (3, of_layer(0, add))], back=2)
            dve.wait_ge(z_rs.sem, 1)
            pipeline(dve, T, G, [(0, norm_z), (0, of_layer(1, rows_out)), (1, of_layer(1, maximum)), (3, of_layer(1, add)), (4, norm_y)], back=3)


K2 = 2
E8 = 8


def scatter(pool, rows, scratch, routing, scattered):
    for t in range(T):
        for k in range(K2):
            pool.indirect_dma_start(scratch["rows"], bass.IndirectOffsetOnAxis(ap=routing["places"][:, t, k:k + 1], axis=0),
                                    rows[:, t, :], None).then_inc(scattered.sem, 16)
    pool.wait_ge(scattered.sem, 16 * T * K2)


def route(nc, X, ident, ps, a, scratch, routing, layer):
    first = layer == 0
    tag = f"r{layer}_"
    lead = 0 if first else T // 2
    NT = routing["tiles"]
    with ExitStack() as cx:
        sb = tiles(nc, cx)
        xn_all = sb(tag + "xn_all", [P, T, D]) if first else X
        R = 2
        rT = sb(tag + "rT", [P, R, DC, GT])
        norms = sb(tag + "norms", [P, 2, DC])
        rwT = sb(tag + "rwT", [P, DC, E8])
        rb = sb(tag + "rb", [1, E8])
        ones1 = sb(tag + "ones1", [1, P])
        half = sb(tag + "half", [P, T])
        stats, mv, rstd = sb(tag + "stats", [P, T, 6]), sb(tag + "mv", [P, T, 2]), sb(tag + "rstd", [P, T])
        eight = sb(tag + "eight", [P, E8])
        eight_i = sb(tag + "eight_i", [P, E8], I32)
        before = sb(tag + "before", [P, P])
        every = sb(tag + "every", [P, P])
        starts = sb(tag + "starts", [1, NT])
        starts_i = sb(tag + "starts_i", [1, NT], I32)
        zeros = sb(tag + "zeros", [P, D])
        lg = sb(tag + "lg", [P, T, E8])
        lmax, lsum = sb(tag + "lmax", [P, T]), sb(tag + "lsum", [P, T])
        top = sb(tag + "top", [P, T, E8])
        idx = sb(tag + "idx", [P, T, E8], U32)
        idxf = sb(tag + "idxf", [P, T, K2])
        wsum = sb(tag + "wsum", [P, T])
        chosen = sb(tag + "chosen", [P, K2, T, E8])
        both = sb(tag + "both", [P, T, E8])
        rank = sb(tag + "rank", [P, T, E8])
        prior = sb(tag + "prior", [P, T, E8])
        count = sb(tag + "count", [P, T, E8])
        offset = sb(tag + "offset", [P, E8])
        padded = sb(tag + "padded", [P, E8])
        padded_i = sb(tag + "padded_i", [P, E8], I32)
        ended = sb(tag + "ended", [1, E8])
        prod = sb(tag + "prod", [P, T, E8])
        place = sb(tag + "place", [P, T])
        passed = sb(tag + "passed", [1, NT, E8])
        tile_f = sb(tag + "tile_f", [1, NT])
        weights, places, tile_expert = routing["weights"], routing["places"], routing["tile_expert"]

        def sig(name, per=1):
            return Signal(cx, nc, tag + name, per)
        loaded, consts, var, rs = sig("loaded"), sig("consts"), sig("var"), sig("rs")
        x_ready, x_turned, r_out, logits, lexp_in, lexp_out = (sig(n) for n in ("x_ready", "x_turned", "r_out", "logits", "lexp_in", "lexp_out"))
        chosen_all, counted, placed = sig("chosen_all"), sig("counted"), sig("placed")
        cleared, kept = sig("cleared"), sig("kept")
        scattered = Signal(cx, nc, "scattered", sem=routing["by_pool"][0])
        block = cx.enter_context(nc.Block())
        L = "L0_ffn_" if first else "L1_ffn_"

        @block.sync
        def _(sp):
            sp.dma_start(rwT[:, :, :], a[L + "router_w"].rearrange("(k p) e -> p k e", p=P)).then_inc(loaded.sem, 16)
            sp.dma_start(rb[:, :], a[L + ("router_b" if first else "routing_bias")].rearrange("(a n) -> a n", a=1)).then_inc(loaded.sem, 16)
            if first:
                sp.dma_start(norms[:, 0, :], a[L + "router_ln_scale"]).then_inc(loaded.sem, 16)
                sp.dma_start(norms[:, 1, :], a[L + "router_ln_bias"]).then_inc(loaded.sem, 16)
                routing["load_rest"](sp)
                sp.wait_ge(consts.sem, 1)
                for t in range(scratch["tiles"]):
                    sp.dma_start(scratch["rows"][t * P:(t + 1) * P, :], zeros[:, :]).then_inc(cleared.sem, 16)
            else:
                for n, at in enumerate((0, NT - lead)):
                    sp.dma_start(scratch["rows"][at * P:(at + lead) * P, :].rearrange("(t p) d -> p t d", p=P), X[:, n * lead:(n + 1) * lead, :]).then_inc(kept.sem, 16)
                routing["load_rest"](sp)
                sp.wait_ge(kept.sem, 32)

        @block.gpsimd
        def _(pool):
            pool.memset(half[:, :], -0.5)
            pool.drain()
            pool.memset(ones1[:, :], 1.0)
            pool.drain()
            pool.memset(every[:, :], 1.0)
            pool.drain()
            pool.memset(before[:, :], 1.0)
            pool.drain()
            pool.affine_select(out=before[:, :], in_=before[:, :], compare_op=ALU.is_ge, fill=0.0, base=-1, pattern=[[1, P]], channel_multiplier=-1)
            pool.drain()
            pool.iota(eight_i[:, :], pattern=[[1, E8]], base=0, channel_multiplier=0)
            pool.drain()
            pool.iota(starts_i[:, :], pattern=[[P, NT]], base=0, channel_multiplier=0)
            pool.drain()
            pool.memset(zeros[:, :], 0.0).then_inc(consts.sem, 1)
            if first:
                for g in range(NG):
                    own = slice(g * G, (g + 1) * G)
                    pool.wait_ge(var.sem, g + 1)
                    pool.tensor_tensor(rstd[:, own], mv[:, own, 1], half[:, own], ALU.pow).then_inc(rs.sem, 1)
                pool.wait_ge(cleared.sem, 16 * scratch["tiles"])
                pool.wait_ge(placed.sem, 1)
                scatter(pool, xn_all, scratch, routing, scattered)

        @block.tensor
        def _(pe):
            pe.wait_ge(loaded.sem, 16 * (4 if first else 2))
            pe.wait_ge(consts.sem, 1)
            for g in range(NG + 1):
                if g < NG:
                    if first:
                        pe.wait_ge(x_ready.sem, g + 1)
                    if g >= 2:
                        pe.wait_ge(r_out.sem, g - 1)
                    for j in range(G):
                        for k in range(DC):
                            last = nc.tensor.transpose(ps[:, 2 * (g % 2) + k, j * P:(j + 1) * P], xn_all[:, g * G + j, k * P:(k + 1) * P], ident[:, :])
                    last.then_inc(x_turned.sem, 1)
                if g >= 1:
                    pe.wait_ge(r_out.sem, g)
                    for j in range(G):
                        t = (g - 1) * G + j
                        for k in range(DC):
                            nc.tensor.matmul(ps[:, 4, t * E8:(t + 1) * E8], rT[:, (g - 1) % R, k, j * P:(j + 1) * P], rwT[:, k, :], start=(k == 0), stop=False)
                        last = nc.tensor.matmul(ps[:, 4, t * E8:(t + 1) * E8], ones1[:, :], rb[:, :], start=False, stop=True)
                    last.then_inc(logits.sem, 1)
            pe.wait_ge(chosen_all.sem, 1)
            flat = both[:, :, :].rearrange("p t e -> p (t e)")
            nc.tensor.matmul(ps[:, 5, 0:T * E8], before[:, :], flat, start=True, stop=True)
            nc.tensor.matmul(ps[:, 6, 0:T * E8], every[:, :], flat, start=True, stop=True).then_inc(counted.sem, 1)

        @block.scalar
        def _(act):
            act.wait_ge(loaded.sem, 16 * (4 if first else 2))
            for g in range(NG):
                act.wait_ge(x_turned.sem, g + 1)
                if g >= R:
                    act.wait_ge(logits.sem, g - R + 1)
                for k in range(DC):
                    src = ps[:, 2 * (g % 2) + k, :]
                    if first:
                        last = nc.scalar.activation(rT[:, g % R, k, :], src, ACT.Identity, scale=norms[:, 0, k:k + 1], bias=norms[:, 1, k:k + 1])
                    else:
                        last = nc.scalar.activation(rT[:, g % R, k, :], src, ACT.Copy)
                last.then_inc(r_out.sem, 1)
            act.wait_ge(lexp_in.sem, 1)
            nc.scalar.activation(lg[:, :, :], lg[:, :, :], ACT.Exp, scale=1.0 if first else -1.0).then_inc(lexp_out.sem, 1)

        @block.vector
        def _(dve):
            dve.wait_ge(consts.sem, 1)
            nc.vector.tensor_copy(eight[:, :], eight_i[:, :])
            nc.vector.tensor_copy(starts[:, :], starts_i[:, :])
            if first:
                def statistics(g):
                    own = range(g * G, (g + 1) * G)
                    for t in own:
                        nc.vector.bn_stats(stats[:, t, :], X[:, t, :])
                    dve.drain()
                    for t in own:
                        nc.vector.bn_aggr(mv[:, t, :], stats[:, t, :])
                    dve.drain()
                    nc.vector.tensor_scalar(mv[:, g * G:(g + 1) * G, 1], mv[:, g * G:(g + 1) * G, 1], 1e-6, None, ALU.add).then_inc(var.sem, 1)
                statistics(0)
                for g in range(NG):
                    if g + 1 < NG:
                        statistics(g + 1)
                    dve.wait_ge(rs.sem, g + 1)
                    for t in range(g * G, (g + 1) * G):
                        last = nc.vector.tensor_scalar(xn_all[:, t, :], X[:, t, :], mv[:, t, 0:1], rstd[:, t:t + 1], ALU.subtract, ALU.mult)
                    last.then_inc(x_ready.sem, 1)
            dve.wait_ge(logits.sem, NG)
            nc.vector.tensor_copy(lg[:, :, :].rearrange("p t e -> p (t e)"), ps[:, 4, 0:T * E8])
            dve.drain()
            if first:
                nc.vector.tensor_reduce(lmax[:, :], lg[:, :, :], AX.X, ALU.max)
                dve.drain()
                nc.vector.tensor_tensor(lg[:, :, :], lg[:, :, :], lmax[:, :].unsqueeze(2).broadcast_to((P, T, E8)), ALU.subtract)
                dve.drain()
            nc.vector.engine_nop().then_inc(lexp_in.sem, 1)
            dve.wait_ge(lexp_out.sem, 1)
            if first:
                nc.vector.tensor_reduce(lsum[:, :], lg[:, :, :], AX.X, ALU.add)
                dve.drain()
                nc.vector.reciprocal(lsum[:, :], lsum[:, :])
                dve.drain()
                nc.vector.tensor_tensor(lg[:, :, :], lg[:, :, :], lsum[:, :].unsqueeze(2).broadcast_to((P, T, E8)), ALU.mult)
            else:
                nc.vector.tensor_scalar(lg[:, :, :], lg[:, :, :], 1.0, None, ALU.add)
                dve.drain()
                nc.vector.reciprocal(lg[:, :, :], lg[:, :, :])
            dve.drain()
            for t in range(T):
                nc.vector.max(top[:, t, :], lg[:, t, :])
            dve.drain()
            for t in range(T):
                nc.vector.max_index(idx[:, t, :], top[:, t, :], lg[:, t, :])
            nc.vector.tensor_tensor(wsum[:, :], top[:, :, 0], top[:, :, 1], ALU.add)
            dve.drain()
            nc.vector.reciprocal(wsum[:, :], wsum[:, :])
            nc.vector.tensor_copy(idxf[:, :, :], idx[:, :, 0:K2])
            dve.drain()
            nc.vector.tensor_tensor(weights[:, :, :], top[:, :, 0:K2], wsum[:, :].unsqueeze(2).broadcast_to((P, T, K2)), ALU.mult)
            for k in range(K2):
                nc.vector.tensor_tensor(chosen[:, k], eight[:, :].unsqueeze(1).broadcast_to((P, T, E8)), idxf[:, :, k:k + 1].broadcast_to((P, T, E8)), ALU.is_equal)
            dve.drain()
            nc.vector.tensor_tensor(both[:, :, :], chosen[:, 0], chosen[:, 1], ALU.add).then_inc(chosen_all.sem, 1)
            dve.wait_ge(counted.sem, 1)
            nc.vector.tensor_copy(rank[:, :, :].rearrange("p t e -> p (t e)"), ps[:, 5, 0:T * E8])
            nc.vector.tensor_copy(count[:, :, :].rearrange("p t e -> p (t e)"), ps[:, 6, 0:T * E8])
            nc.vector.memset(prior[:, 0, :], 0.0)
            dve.drain()
            for t in range(1, T):
                nc.vector.tensor_tensor(prior[:, t, :], prior[:, t - 1, :], count[:, t - 1, :], ALU.add)
                dve.drain()
            nc.vector.tensor_tensor(padded[:, :], prior[:, T - 1, :], count[:, T - 1, :], ALU.add)
            dve.drain()
            nc.vector.tensor_scalar(padded_i[:, :], padded[:, :], float(P - 1), None, ALU.add)
            dve.drain()
            nc.vector.tensor_scalar(padded_i[:, :], padded_i[:, :], -P, None, ALU.bitwise_and)
            dve.drain()
            nc.vector.tensor_copy(padded[:, :], padded_i[:, :])
            nc.vector.memset(offset[:, 0:1], float(lead * P))
            dve.drain()
            for e in range(1, E8):
                nc.vector.tensor_tensor(offset[:, e:e + 1], offset[:, e - 1:e], padded[:, e - 1:e], ALU.add)
                dve.drain()
            nc.vector.tensor_tensor(ended[:, :], offset[0:1, :], padded[0:1, :], ALU.add)
            nc.vector.tensor_tensor(rank[:, :, :], rank[:, :, :], prior[:, :, :], ALU.add)
            dve.drain()
            nc.vector.tensor_tensor(rank[:, :, :], rank[:, :, :], offset[:, :].unsqueeze(1).broadcast_to((P, T, E8)), ALU.add)
            dve.drain()
            for k in range(K2):
                nc.vector.tensor_tensor(prod[:, :, :], rank[:, :, :], chosen[:, k], ALU.mult)
                dve.drain()
                nc.vector.tensor_reduce(place[:, :], prod[:, :, :], AX.X, ALU.add)
                dve.drain()
                nc.vector.tensor_copy(places[:, :, k], place[:, :])
                dve.drain()
            nc.vector.engine_nop().then_inc(placed.sem, 1)
            nc.vector.tensor_tensor(passed[:, :, :], starts[:, :].unsqueeze(2).broadcast_to((1, NT, E8)), ended[:, :].unsqueeze(1).broadcast_to((1, NT, E8)), ALU.is_ge)
            dve.drain()
            nc.vector.tensor_reduce(tile_f[:, :], passed[:, :, :], AX.X, ALU.add)
            dve.drain()
            nc.vector.tensor_scalar(tile_f[:, :], tile_f[:, :], float(E8 - 1), float(0 if first else 1), ALU.min, ALU.add)
            dve.drain()
            if lead:
                nc.vector.memset(tile_f[:, 0:lead], 0.0)
                nc.vector.memset(tile_f[:, NT - lead:NT], 0.0)
                dve.drain()
            nc.vector.tensor_copy(tile_expert[:, :], tile_f[:, :])


def experts(nc, X, W, ident, ps, a, scratch, routing, layer, got=None):
    first = layer == 0
    tag = f"m{layer}_"
    NT = routing["tiles"]
    NE = E8 if first else E8 + 1
    F = 1024 if first else 512
    FC = F // P
    IN = DC * 1024
    WE = IN + FC * D
    with ExitStack() as cx:
        sb = tiles(nc, cx)
        scale, shift = sb(tag + "scale", [P, NE, DC]), sb(tag + "shift", [P, NE, DC])
        if first:
            b1, b2 = sb(tag + "b1", [P, NE, FC]), sb(tag + "b2", [P, NE, D])
        rows = sb(tag + "rows", [P, 2, D])
        rowsT = sb(tag + "rowsT", [P, 2, DC, P])
        hid = sb(tag + "hid", [P, 2, F])
        gate = None if first else sb(tag + "gate", [P, 2, F])
        enterw = sb(tag + "enterw", [P, 2, IN])
        out = sb(tag + "out", [P, 2, D])
        tile_expert = routing["tile_expert"]

        def sig(name, per=1):
            return Signal(cx, nc, tag + name, per)
        loaded = sig("loaded")
        fetched = [sig(f"fetched{m}", 16) for m in range(2)]
        turned, rowsT_out, hidden, activated, acted = sig("turned"), sig("rowsT_out"), sig("hidden"), sig("activated"), sig("acted")
        acted_gate = sig("acted_gate")
        weights_ready, expert_done, out_ready = sig("weights_ready"), sig("expert_done"), sig("out_ready")
        stored = [sig(f"stored{m}", 16) for m in range(2)]
        rows_in = sig("rows_in")
        scattered = Signal(cx, nc, "scattered", sem=routing["by_pool"][0])
        gathered = Signal(cx, nc, "gathered", sem=routing["by_pool"][1])
        if not first:
            acted = activated
        block = cx.enter_context(nc.Block())

        def expert_of(eng, n):
            return eng.value_load(tile_expert[0:1, bass.ds(n, 1)], min_val=0, max_val=NE - 1)

        def reach(eng, signal, value):
            if not isinstance(value, int) or value > 0:
                eng.wait_ge(signal.sem, value)

        def steps(eng, begin, step):
            begin()
            step(0, 0, True)
            step(1, 1, True)
            with eng.Fori(1, NT // 2 - 1) as i:
                step(2 * i, 0, True)
                step(2 * i + 1, 1, True)
            step(NT - 2, 0, False)
            step(NT - 1, 1, False)

        @block.sync
        def _(sp):
            if first:
                sp.dma_start(scale[:, :, :], a["L0_ffn_expert_ln_scale"]).then_inc(loaded.sem, 16)
                sp.dma_start(shift[:, :, :], a["L0_ffn_expert_ln_bias"]).then_inc(loaded.sem, 16)
                sp.dma_start(b1[:, :, :], a["L0_ffn_b1"]).then_inc(loaded.sem, 16)
                sp.dma_start(b2[:, :, :], a["L0_ffn_b2"].unsqueeze(0).broadcast_to((P, NE, D))).then_inc(loaded.sem, 16)
            def fetch(i, m):
                reach(sp, turned, 2 * i)
                sp.dma_start(rows[:, m, :], scratch["rows"][bass.ds((2 * i + m) * P, P), :]).then_inc(fetched[m].sem, 16)
            fetch(0, 0)
            fetch(0, 1)
            begin = 1
            if not first:
                for begin in range(1, T // 4):
                    fetch(begin, 0)
                    fetch(begin, 1)
                begin += 1
                sp.wait_ge(rows_in.sem, 1)
            with sp.Fori(begin, NT // 2) as i:
                fetch(i, 0)
                fetch(i, 1)

        if not first:
            @block.gpsimd
            def _(pool):
                scatter(pool, X, scratch, routing, scattered)
                pool.engine_nop().then_inc(rows_in.sem, 1)
                for m in range(2):
                    pool.wait_ge(stored[m].sem, 16 * (NT - T // 2) // 2)
                for t in range(T):
                    for k in range(K2):
                        pool.indirect_dma_start(got[:, t, k, :], None, scratch["results"][0:(NT - T // 2) * P, :],
                                                bass.IndirectOffsetOnAxis(ap=routing["places"][:, t, k:k + 1], axis=0)).then_inc(gathered.sem, 16)
                pool.wait_ge(gathered.sem, 16 * T * K2)

        @block.tensor
        def _(pe):
            pe.wait_ge(routing["weights_in"], routing["weights_count"])

            def turn(n, m):
                pe.wait_ge(fetched[m].sem, n * 8 + 16 - m * 8)
                reach(pe, rowsT_out, n)
                for k in range(DC):
                    last = nc.tensor.transpose(ps[:, 0, k * P:(k + 1) * P], rows[:, m, k * P:(k + 1) * P], ident[:, :])
                last.then_inc(turned.sem, 1)

            def enter(n, m):
                pe.wait_ge(rowsT_out.sem, n + 1)
                pe.wait_ge(weights_ready.sem, n + 1)
                reach(pe, activated, n - 1)
                for c in range(1024 // P):
                    for k in range(DC):
                        last = nc.tensor.matmul(ps[:, 2 + 2 * m + c // 4, (c % 4) * P:(c % 4 + 1) * P], enterw[:, m, k * 1024 + c * P:k * 1024 + (c + 1) * P], rowsT[:, m, k, :],
                                                start=(k == 0), stop=(k == DC - 1))
                last.then_inc(hidden.sem, 1)

            def begin():
                turn(0, 0)
                enter(0, 0)
                turn(1, 1)

            def step(n, m, more):
                if more or m == 0:
                    enter(n + 1, 1 - m)
                if more:
                    turn(n + 2, m)
                e = expert_of(pe, n)
                pe.wait_ge(acted.sem, n + 1)
                reach(pe, out_ready, n)
                for c in range(FC):
                    last = nc.tensor.matmul(ps[:, 1, 0:D], hid[:, m, c * P:(c + 1) * P], W[:, bass.ds(e * WE + IN + c * D, D)],
                                            start=(c == 0), stop=(c == FC - 1))
                last.then_inc(expert_done.sem, 1)
            steps(pe, begin, step)

        @block.scalar
        def _(act):
            def fetch_weights(n, m):
                e = expert_of(act, n)
                reach(act, hidden, n - 1)
                nc.scalar.activation(enterw[:, m, :], W[:, bass.ds(e * WE, IN)], ACT.Copy).then_inc(weights_ready.sem, 1)

            def activate(n, m):
                if first:
                    act.wait_ge(activated.sem, n + 1)
                    nc.scalar.activation(hid[:, m, :], hid[:, m, :], ACT.Gelu).then_inc(acted.sem, 1)
                else:
                    act.wait_ge(hidden.sem, n + 1)
                    nc.scalar.activation(gate[:, m, :], ps[:, 2 + 2 * m, :], ACT.Silu).then_inc(acted_gate.sem, 1)

            def step(n, m, more):
                if more:
                    fetch_weights(n + 2, m)
                if more or m == 0:
                    activate(n + 1, 1 - m)
                act.wait_ge(out_ready.sem, n + 1)
                act.dma_start(scratch["results"][bass.ds(n * P, P), :], out[:, m, :]).then_inc(stored[m].sem, 16)

            def begin():
                act.wait_ge(routing["weights_in"], routing["weights_count"])
                for n in range(2):
                    fetch_weights(n, n)
                activate(0, 0)
            steps(act, begin, step)
            for m in range(2):
                act.wait_ge(stored[m].sem, 16 * (NT // 2))

        @block.vector
        def _(dve):
            if first:
                dve.wait_ge(loaded.sem, 64)

            def take(n, m):
                e = expert_of(dve, n) if first else None
                dve.wait_ge(turned.sem, n + 1)
                reach(dve, hidden, n - 1)
                if first:
                    for k in range(DC):
                        last = nc.vector.tensor_scalar(rowsT[:, m, k, :], ps[:, 0, k * P:(k + 1) * P],
                                                       scale[:, :, :].rearrange("p e k -> p (e k)")[:, bass.ds(e * DC + k, 1)],
                                                       shift[:, :, :].rearrange("p e k -> p (e k)")[:, bass.ds(e * DC + k, 1)], ALU.mult, ALU.add)
                else:
                    last = nc.vector.tensor_copy(rowsT[:, m, :, :].rearrange("p k q -> p (k q)"), ps[:, 0, 0:D])
                last.then_inc(rowsT_out.sem, 1)

            def activate(n, m):
                if first:
                    e = expert_of(dve, n)
                    dve.wait_ge(hidden.sem, n + 1)
                    reach(dve, expert_done, n - 1)
                    nc.vector.tensor_tensor(hid[:, m, :].rearrange("p (c q) -> p c q", c=FC), ps[:, 2 + 2 * m:4 + 2 * m, :].rearrange("p a (c q) -> p (a c) q", q=P),
                                            b1[:, :, :].rearrange("p e c -> p (e c)")[:, bass.ds(e * FC, FC)].unsqueeze(2).broadcast_to((P, FC, P)), ALU.add).then_inc(activated.sem, 1)
                else:
                    dve.wait_ge(acted_gate.sem, n + 1)
                    reach(dve, expert_done, n - 1)
                    nc.vector.tensor_tensor(hid[:, m, :], ps[:, 3 + 2 * m, :], gate[:, m, :], ALU.mult).then_inc(activated.sem, 1)

            def begin():
                take(0, 0)
                activate(0, 0)
                take(1, 1)

            def step(n, m, more):
                if more or m == 0:
                    activate(n + 1, 1 - m)
                if more:
                    take(n + 2, m)
                e = expert_of(dve, n) if first else None
                dve.wait_ge(expert_done.sem, n + 1)
                reach(dve, stored[m], (n - m) * 8)
                if first:
                    nc.vector.tensor_tensor(out[:, m, :], ps[:, 1, 0:D], b2[:, :, :].rearrange("p e f -> p (e f)")[:, bass.ds(e * D, D)], ALU.add).then_inc(out_ready.sem, 1)
                else:
                    nc.vector.tensor_copy(out[:, m, :], ps[:, 1, 0:D]).then_inc(out_ready.sem, 1)
            steps(dve, begin, step)


def combine(nc, X, scratch, routing, layer, result=None, gathered=None):
    first = layer == 0
    tag = f"c{layer}_"
    NBUF = 8
    with ExitStack() as cx:
        sb = tiles(nc, cx)
        got = sb(tag + "got", [P, NBUF, K2, D]) if first else gathered
        common = None if first else sb(tag + "common", [P, T, D])
        y = sb(tag + "y", [P, T, D]) if first else got[:, :, 0, :]
        half = sb(tag + "half", [P, T])
        stats, mv, rstd = sb(tag + "stats", [P, T, 6]), sb(tag + "mv", [P, T, 2]), sb(tag + "rstd", [P, T])
        weights, places = routing["weights"], routing["places"]

        def sig(name, per=1):
            return Signal(cx, nc, tag + name, per)
        shared = [sig(f"shared{g}") for g in range(NG)]
        shared_in, added, var, rs, normed, stored = (sig(n) for n in ("shared_in", "added", "var", "rs", "normed", "stored"))
        fetched = [Signal(cx, nc, "fetched", sem=routing["by_pool"][1 + m]) for m in range(NBUF)]
        block = cx.enter_context(nc.Block())

        @block.sync
        def _(sp):
            if not first:
                for g in range(NG):
                    at = g * G if g < NG // 2 else routing["tiles"] - T + g * G
                    sp.dma_start(common[:, g * G:(g + 1) * G, :], scratch["results"][at * P:(at + G) * P, :].rearrange("(t p) d -> p t d", p=P)).then_inc(shared[g].sem, 16)
            if result is not None:
                for g in range(NG):
                    sp.wait_ge(normed.sem, g + 1)
                    sp.dma_start(result.rearrange("b (t p) d -> p (b t) d", p=P)[:, g * G:(g + 1) * G, :], X[:, g * G:(g + 1) * G, :]).then_inc(stored.sem, 16)
                sp.wait_ge(stored.sem, 16 * NG)

        @block.gpsimd
        def _(pool):
            pool.memset(half[:, :], -0.5)
            pool.drain()

            def power(g):
                own = slice(g * G, (g + 1) * G)
                pool.wait_ge(var.sem, g + 1)
                pool.tensor_tensor(rstd[:, own], mv[:, own, 1], half[:, own], ALU.pow).then_inc(rs.sem, 1)
            for g in range(NG):
                if first:
                    for t in range(g * G, (g + 1) * G):
                        if t >= NBUF:
                            pool.wait_ge(added.sem, t - NBUF + 1)
                        for k in range(K2):
                            pool.indirect_dma_start(got[:, t % NBUF, k, :], None, scratch["results"][0:routing["tiles"] * P, :],
                                                    bass.IndirectOffsetOnAxis(ap=places[:, t, k:k + 1], axis=0)).then_inc(fetched[t % NBUF].sem, 16)
                else:
                    own = slice(g * G, (g + 1) * G)
                    pool.wait_ge(shared[g].sem, 16)
                    pool.tensor_tensor(X[:, own, :], X[:, own, :], common[:, own, :], ALU.add).then_inc(shared_in.sem, 1)
                if g:
                    power(g - 1)
            power(NG - 1)

        @block.vector
        def _(dve):
            def mix(g):
                own = range(g * G, (g + 1) * G)
                if not first:
                    dve.wait_ge(shared_in.sem, g + 1)
                slot = (lambda t: t % NBUF) if first else (lambda t: t)
                for k in range(K2):
                    for t in own:
                        if first and k == 0:
                            dve.wait_ge(fetched[t % NBUF].sem, 32 * (t // NBUF + 1))
                        last = nc.vector.scalar_tensor_tensor(out=y[:, t, :], in0=got[:, slot(t), k, :], scalar=weights[:, t, k:k + 1],
                                                              in1=y[:, t, :] if k else X[:, t, :], op0=ALU.mult, op1=ALU.add)
                        if k:
                            last.then_inc(added.sem, 1)
                    dve.drain()
                for t in own:
                    nc.vector.bn_stats(stats[:, t, :], y[:, t, :])
                dve.drain()
                for t in own:
                    nc.vector.bn_aggr(mv[:, t, :], stats[:, t, :])
                dve.drain()
                nc.vector.tensor_scalar(mv[:, g * G:(g + 1) * G, 1], mv[:, g * G:(g + 1) * G, 1], 1e-5, None, ALU.add).then_inc(var.sem, 1)
            for g in range(NG + 1):
                if g < NG:
                    mix(g)
                if g:
                    dve.wait_ge(rs.sem, g)
                    for t in range((g - 1) * G, g * G):
                        last = nc.vector.tensor_scalar(X[:, t, :], y[:, t, :], mv[:, t, 0:1], rstd[:, t:t + 1], ALU.subtract, ALU.mult)
                    last.then_inc(normed.sem, 1)


def decoder(nc, a, out):
    with ExitStack() as cx:
        X = cx.enter_context(nc.sbuf_tensor("X", [P, T, D], F32))
        ident = cx.enter_context(nc.sbuf_tensor("ident", [P, P], F32))
        ps = cx.enter_context(nc.psum_tensor("ps", [P, 8, 512], F32))
        EARLY, WORDS = 20 * 1024, 32 * 1024
        W = cx.enter_context(nc.sbuf_tensor("experts_w", [P, WORDS], F32))
        spare = W[:, EARLY:WORDS]
        weights = cx.enter_context(nc.sbuf_tensor("weights", [P, T, K2], F32))
        places = cx.enter_context(nc.sbuf_tensor("places", [P, T, K2], U32))
        tile_expert = cx.enter_context(nc.sbuf_tensor("tile_expert", [1, 64], I32))
        QT = T * K2 + E8
        scratch = {
            "tiles": T + QT,
            "rows": nc.dram_tensor("queue_rows", ((T + QT) * P, D), F32).ap(),
            "results": nc.dram_tensor("queue_results", ((T + QT) * P, D), F32).ap(),
            "q": nc.dram_tensor("q_parts", (3, DC, P, B * S), BF16).ap(),
            "k": nc.dram_tensor("k_parts", (3, DC, P, B * S), BF16).ap(),
            "max": nc.dram_tensor("max_parts", (3, 4 * S), BF16).ap(),
        }
        x_loaded = cx.enter_context(nc.semaphore("x_loaded"))
        weights_in = [cx.enter_context(nc.semaphore(f"weights_in{n}")) for n in range(2)]

        by_pool = [[cx.enter_context(nc.semaphore(f"by_pool{layer}_{n}")) for n in range(9)] for layer in range(2)]

        def routing(layer):
            words = a[f"w_L{layer}"].shape[2]
            experts_in = a[f"w_L{layer}"].shape[1]
            whole = EARLY // words

            def load(sp, which):
                for e in which:
                    sp.dma_start(W[:, e * words:(e + 1) * words], a[f"w_L{layer}"][:, e, :]).then_inc(weights_in[layer], 16)
            return {"by_pool": by_pool[layer], "weights": weights, "places": places, "tiles": QT + (T if layer else 0),
                    "tile_expert": tile_expert[:, 0:QT + (T if layer else 0)],
                    "weights_in": weights_in[layer], "weights_count": 16 * experts_in,
                    "load_early": lambda sp: load(sp, range(whole)), "load_rest": lambda sp: load(sp, range(whole, experts_in))}
        route0, route1 = routing(0), routing(1)

        with nc.Block() as block:
            @block.gpsimd
            def _(pool):
                pool.memset(ident[:, :], 0.0)
                pool.drain()
                pool.affine_select(out=ident[:, :], in_=ident[:, :], compare_op=ALU.not_equal, fill=1.0,
                                   base=0, pattern=[[-1, P]], channel_multiplier=1)
        window_attention(nc, X, ident, ps, a, spare, x_loaded, route0["load_early"])
        nc.all_engine_barrier()
        cross_attention(nc, X, ident, ps, a, spare, 0)
        nc.all_engine_barrier()
        route(nc, X, ident, ps, a, scratch, route0, 0)
        nc.all_engine_barrier()
        experts(nc, X, W, ident, ps, a, scratch, route0, 0)
        nc.all_engine_barrier()
        combine(nc, X, scratch, route0, 0)
        nc.all_engine_barrier()
        with nc.sbuf_tensor("v_all", [P, T, D], F32) as v_all:
            slot_projections(nc, X, ident, ps, a, scratch, v_all, spare, route1["load_early"])
            nc.all_engine_barrier()
            causal_attention(nc, ident, ps, scratch, v_all, v_all, spare)
            nc.all_engine_barrier()
            slot_layers(nc, X, ident, ps, a, v_all, spare)
            nc.all_engine_barrier()
        cross_attention(nc, X, ident, ps, a, spare, 1)
        nc.all_engine_barrier()
        route(nc, X, ident, ps, a, scratch, route1, 1)
        nc.all_engine_barrier()
        with nc.sbuf_tensor("gathered", [P, T, K2, D], F32) as gathered:
            experts(nc, X, W, ident, ps, a, scratch, route1, 1, gathered)
            nc.all_engine_barrier()
            combine(nc, X, scratch, route1, 1, result=out, gathered=gathered)
            nc.all_engine_barrier()


def features(v):
    return np.ascontiguousarray(np.moveaxis(v.reshape(v.shape[:-1] + (DC, P)), -1, 0))


def chunks(w):
    e, r, n = w.shape
    return w.reshape(e, r // P, P, n).transpose(2, 0, 1, 3).reshape(P, e, -1)


def kernel(**inputs):
    import concourse.bacc as bacc
    from concourse.bass_utils import run_bass_kernel_spmd

    z = {k: np.asarray(v) for k, v in inputs.items()}
    arrays = {k: v for k, v in z.items() if not k.startswith(("L0_ffn_w", "L1_ffn_shared", "L1_ffn_gate", "L1_ffn_up", "L1_ffn_down"))}
    arrays["xT"] = np.ascontiguousarray(z["x"].reshape(B * S, D).T)
    arrays["L0_ffn_b1"] = np.ascontiguousarray(z["L0_ffn_b1"].reshape(E8, 1024 // P, P).transpose(2, 0, 1))
    for n in ("L0_xattn_bq", "L0_xattn_bk", "L1_xattn_bq", "L1_xattn_bk", "L1_xattn_norm_w", "L1_xattn_norm_b",
              "L1_xattn_norm1_w", "L1_xattn_norm1_b", "L0_ffn_router_ln_scale", "L0_ffn_router_ln_bias",
              "L0_ffn_expert_ln_scale", "L0_ffn_expert_ln_bias"):
        arrays[n] = features(z[n])
    for n in ("L0_ffn_router_w", "L1_ffn_router_w", "L1_attn_qK", "L1_attn_kK", "L1_attn_vK", "L1_attn_pK", "L1_attn_fK"):
        arrays[n] = np.ascontiguousarray(z[n].T)
    arrays["w_L0"] = np.ascontiguousarray(np.concatenate(
        [chunks(z["L0_ffn_w1"].transpose(0, 2, 1)), chunks(z["L0_ffn_w2"].transpose(0, 2, 1))], 2))
    gate, up, down = (np.concatenate([z["L1_ffn_shared_" + n].T[None], z[f"L1_ffn_{n}_w"]]) for n in ("gate", "up", "down"))
    arrays["w_L1"] = np.ascontiguousarray(np.concatenate([chunks(np.concatenate([gate, up], 2)), chunks(down)], 2))

    nc = bacc.Bacc("TRN2", target_bir_lowering=False, num_devices=1)
    feeds, a = {}, {}
    for n, v in arrays.items():
        v = np.ascontiguousarray(v)
        feeds[f"in_{n}"] = v
        a[n] = nc.dram_tensor(f"in_{n}", v.shape, mybir.dt.from_np(v.dtype), kind="ExternalInput").ap()
    out = nc.dram_tensor("out", (B, S, D), F32, kind="ExternalOutput").ap()
    decoder(nc, a, out)
    r = run_bass_kernel_spmd(nc, [feeds], core_ids=[0])
    return r.results[0]["out"]
```
